# Optimizing a Trainium2 kernel written in Bass

```python
import numpy as np
import jax
import jax.numpy as jnp

def _softmax(x, axis=-1):
    return jax.nn.softmax(x, axis=axis)

def _gelu(x):
    return jax.nn.gelu(x, approximate=True)

def _silu(x):
    return jax.nn.silu(x)

def _sigmoid(x):
    return jax.nn.sigmoid(x)

def _layernorm(x, axis=-1, eps=1e-05):
    m = jnp.mean(x, axis=axis, keepdims=True)
    v = jnp.var(x, axis=axis, keepdims=True)
    return (x - m) / jnp.sqrt(v + eps)

def _scatter_add(tgt, idx, src, axis=0):
    return tgt.at[idx].add(src)

def _segment_sum(src, seg, n):
    return jax.ops.segment_sum(src, seg, n)
kernel_name = 'mk_flamingo_gated_d2_seqx_r4_c17fbb'

def setup_inputs(seed: int=0):
    np.random.seed(seed)
    _w = jnp.asarray

    def _rec_inputs():
        import jax
        import jax.numpy as jnp
        _rk = jax.random.key(seed)
        x = 4.136e-05 + 0.9999 * jax.random.normal(jax.random.fold_in(_rk, 1), (4, 512, 512), jnp.float32)
        _lenS = 512 - jax.random.randint(jax.random.fold_in(_rk, 7), (4,), 0, max(1, 512 // 4) + 1, jnp.int32)
        _lenS2 = 512 - jax.random.randint(jax.random.fold_in(_rk, 8), (4,), 0, max(1, 512 // 4) + 1, jnp.int32)
        _ctx_1024P = jax.random.normal(jax.random.fold_in(_rk, 11), (4, 16, 256), jnp.float32)
        _ctx_1024c = jax.random.dirichlet(jax.random.fold_in(_rk, 511), 0.3 * jnp.ones((16,), jnp.float32), (4, 512))
        _ctx_1024t = jnp.einsum('bsk,bkd->bsd', _ctx_1024c, _ctx_1024P)
        _ctx_1024t = _ctx_1024t * jax.lax.rsqrt(jnp.mean(jnp.square(_ctx_1024t)) + 1e-12) * 0.953939
        ctx_1024 = -0.000292821 + 1.00034 * (_ctx_1024t + 0.3 * jax.random.normal(jax.random.fold_in(_rk, 611), (4, 512, 256), jnp.float32))
        _g = jax.random.normal(jax.random.fold_in(_rk, 9001), (2, 2), jnp.float32)
        _g = jnp.sign(_g) * jnp.maximum(jnp.abs(_g), 1.0) + (_g == 0) * 1.0
        g_xattn = _g[0]
        g_ffn = _g[1]
        return (x, ctx_1024, g_xattn, g_ffn)
    x, ctx_1024, g_xattn, g_ffn = _rec_inputs()

    def _L0_xattn_setup():
        import jax, jax.numpy as jnp
        import numpy as np
        import math
        B, L, DM = (2, 512, 256)
        DS, DC, EXP = (16, 4, 2)
        DI = EXP * DM
        DR = math.ceil(DM / 16)
        DT_MIN, DT_MAX, DT_FLOOR = (0.001, 0.1, 0.0001)

        def _ssm_forward(hidden_states, z, in_proj_w, conv_w, conv_b, x_proj_w, dt_proj_w, dt_proj_b, A_log, D):
            b = hidden_states.shape[0]
            x = jnp.einsum('ed,bld->bel', in_proj_w, hidden_states)
            xp = jnp.pad(x, ((0, 0), (0, 0), (DC - 1, 0)))
            xc = jax.lax.conv_general_dilated(xp, conv_w[:, None, :], window_strides=(1,), padding='VALID', dimension_numbers=('NCH', 'OIH', 'NCH'), feature_group_count=DI)
            u = jax.nn.silu(xc + conv_b[None, :, None])
            x_dbl = jnp.einsum('ke,bel->bkl', x_proj_w, u)
            dt_lo = x_dbl[:, :DR]
            Bm = x_dbl[:, DR:DR + DS]
            Cm = x_dbl[:, DR + DS:]
            delta = jax.nn.softplus(jnp.einsum('er,brl->bel', dt_proj_w, dt_lo) + dt_proj_b[None, :, None])
            A = -jnp.exp(A_log)

            def step(state, xs):
                d_t, B_t, C_t, u_t = xs
                dA = jnp.exp(d_t[..., None] * A)
                state = state * dA + (d_t * u_t)[..., None] * B_t[:, None, :]
                y_t = jnp.einsum('ben,bn->be', state, C_t)
                return (state, y_t)
            xs = (jnp.moveaxis(delta, -1, 0), jnp.moveaxis(Bm, -1, 0), jnp.moveaxis(Cm, -1, 0), jnp.moveaxis(u, -1, 0))
            state0 = jnp.zeros((b, DI, DS), delta.dtype)
            _, ys = jax.lax.scan(step, state0, xs)
            y = jnp.moveaxis(ys, 0, -1)
            y = y + D[None, :, None] * u
            y = y * jax.nn.silu(z)
            return jnp.swapaxes(y, 1, 2)
        key = jax.random.key(seed)
        ks = jax.random.split(key, 8)
        hidden_states = jax.random.normal(ks[0], (B, L, DM), jnp.float32)
        z = jax.random.normal(ks[1], (B, DI, L), jnp.float32)
        in_proj_w = jax.random.normal(ks[2], (DI, DM), jnp.float32) * DM ** (-0.5)
        conv_w = jax.random.normal(ks[3], (DI, DC), jnp.float32) * DC ** (-0.5)
        conv_b = jnp.zeros((DI,), jnp.float32)
        x_proj_w = jax.random.normal(ks[4], (DR + 2 * DS, DI), jnp.float32) * DI ** (-0.5)
        dt_std = DR ** (-0.5)
        dt_proj_w = jax.random.uniform(ks[5], (DI, DR), jnp.float32, -dt_std, dt_std)
        dt = jnp.exp(jax.random.uniform(ks[6], (DI,), jnp.float32) * (math.log(DT_MAX) - math.log(DT_MIN)) + math.log(DT_MIN))
        dt = jnp.clip(dt, DT_FLOOR)
        dt_proj_b = dt + jnp.log(-jnp.expm1(-dt))
        A_log = jnp.log(jnp.broadcast_to(jnp.arange(1, DS + 1, dtype=jnp.float32), (DI, DS)))
        D = jnp.ones((DI,), jnp.float32)
        return dict(hidden_states=hidden_states, z=z, in_proj_w=in_proj_w, conv_w=conv_w, conv_b=conv_b, x_proj_w=x_proj_w, dt_proj_w=dt_proj_w, dt_proj_b=dt_proj_b, A_log=A_log, D=D)
    _L0_xattn_all = _L0_xattn_setup()
    _L0_xattn_in = {k: v for k, v in _L0_xattn_all.items() if k in ('in_proj_w', 'conv_w', 'conv_b', 'x_proj_w', 'dt_proj_w', 'dt_proj_b', 'A_log', 'D')}
    del _L0_xattn_all

    def _L0_ffn_setup():
        import jax, jax.numpy as jnp
        import numpy as np
        NUM_EXPERTS = 16
        TOP_K = 4
        N_GROUP = 4
        TOPK_GROUP = 2
        SCALING = 2.5

        def _route(x, gate_weight, expert_bias):
            logits = x @ gate_weight.T
            scores = jax.nn.sigmoid(logits)
            biased = scores + expert_bias[None, :]
            T = x.shape[0]
            gsz = NUM_EXPERTS // N_GROUP
            grp = biased.reshape(T, N_GROUP, gsz)
            top2, _ = jax.lax.top_k(grp, 2)
            group_scores = top2.sum(-1)
            _, gidx = jax.lax.top_k(group_scores, TOPK_GROUP)
            gmask = jax.nn.one_hot(gidx, N_GROUP, dtype=scores.dtype).sum(1)
            emask = jnp.repeat(gmask, gsz, axis=1)
            masked = jnp.where(emask > 0, biased, -jnp.inf)
            _, sel = jax.lax.top_k(masked, TOP_K)
            w = jnp.take_along_axis(scores, sel, axis=1)
            w = w / (w.sum(-1, keepdims=True) + 1e-20)
            return (w * SCALING, sel)

        def _moe(x, w, sel, gate_proj, up_proj, down_proj):
            cw = (jax.nn.one_hot(sel, NUM_EXPERTS, dtype=x.dtype) * w[..., None]).sum(1)

            def body(acc, inp):
                g, u, d, we = inp
                y = jax.nn.silu(x @ g.T) * (x @ u.T) @ d.T
                return (acc + we[:, None] * y, None)
            out, _ = jax.lax.scan(body, jnp.zeros_like(x), (gate_proj, up_proj, down_proj, cw.T))
            return out
        key = jax.random.key(seed)
        ks = jax.random.split(key, 9)
        B, S, H, I = (2, 256, 512, 256)
        w = lambda k, shape: jax.random.normal(k, shape, jnp.float32) * 0.02
        return {'hidden_states': jax.random.normal(ks[0], (B, S, H), jnp.float32), 'gate_weight': w(ks[1], (NUM_EXPERTS, H)), 'expert_bias': jnp.zeros((NUM_EXPERTS,), jnp.float32), 'gate_proj': w(ks[2], (NUM_EXPERTS, I, H)), 'up_proj': w(ks[3], (NUM_EXPERTS, I, H)), 'down_proj': w(ks[4], (NUM_EXPERTS, H, I)), 'shared_gate': w(ks[5], (I, H)), 'shared_up': w(ks[6], (I, H)), 'shared_down': w(ks[7], (H, I))}
    _L0_ffn_all = _L0_ffn_setup()
    _L0_ffn_in = {k: v for k, v in _L0_ffn_all.items() if k in ('gate_weight', 'expert_bias', 'gate_proj', 'up_proj', 'down_proj', 'shared_gate', 'shared_up', 'shared_down')}
    del _L0_ffn_all

    def _L1_xattn_setup():
        import jax, jax.numpy as jnp
        import numpy as np
        B_, L_, D_MODEL = (4, 512, 256)
        D_STATE, D_CONV, EXPAND = (16, 4, 2)
        D_INNER = EXPAND * D_MODEL
        DT_RANK = (D_MODEL + 15) // 16

        def silu(x):
            return x * jax.nn.sigmoid(x)
        key = jax.random.key(seed)
        ks = jax.random.split(key, 10)
        f32 = jnp.float32
        hidden_states = jax.random.normal(ks[0], (B_, L_, D_MODEL), dtype=f32)
        z = jax.random.normal(ks[1], (B_, D_INNER, L_), dtype=f32)
        in_proj_w = jax.random.normal(ks[2], (D_INNER, D_MODEL), dtype=f32) * 0.02
        conv_w = jax.random.normal(ks[3], (D_INNER, 1, D_CONV), dtype=f32) * 0.1
        conv_b = jax.random.normal(ks[4], (D_INNER,), dtype=f32) * 0.02
        x_proj_w = jax.random.normal(ks[5], (DT_RANK + 2 * D_STATE, D_INNER), dtype=f32) * 0.02
        dt_proj_w = jax.random.uniform(ks[6], (D_INNER, DT_RANK), dtype=f32, minval=-DT_RANK ** (-0.5), maxval=DT_RANK ** (-0.5))
        dt = jnp.exp(jax.random.uniform(ks[7], (D_INNER,), dtype=f32, minval=np.log(0.001), maxval=np.log(0.1)))
        dt_proj_b = jnp.log(jnp.expm1(dt))
        A_log = jnp.log(jnp.broadcast_to(jnp.arange(1, D_STATE + 1, dtype=f32), (D_INNER, D_STATE)))
        D = jnp.ones((D_INNER,), f32)
        return {'hidden_states': hidden_states, 'z': z, 'in_proj_w': in_proj_w, 'conv_w': conv_w, 'conv_b': conv_b, 'x_proj_w': x_proj_w, 'dt_proj_w': dt_proj_w, 'dt_proj_b': dt_proj_b, 'A_log': A_log, 'D': D}
    _L1_xattn_all = _L1_xattn_setup()
    _L1_xattn_in = {k: v for k, v in _L1_xattn_all.items() if k in ('in_proj_w', 'conv_w', 'conv_b', 'x_proj_w', 'dt_proj_w', 'dt_proj_b', 'A_log', 'D')}
    del _L1_xattn_all

    def _L1_ffn_setup():
        import jax, jax.numpy as jnp
        import numpy as np
        B, S, D_IN, D_OUT, E, R = (4, 512, 512, 512, 8, 16)
        SCALING = 32.0 / 16.0
        key = jax.random.key(seed)
        ks = jax.random.split(key, 7)
        return {'x': jax.random.normal(ks[0], (B, S, D_IN), jnp.float32), 'base_w': jax.random.normal(ks[1], (D_OUT, D_IN), jnp.float32) * 0.02, 'base_b': jax.random.normal(ks[2], (D_OUT,), jnp.float32) * 0.02, 'router_w': jax.random.normal(ks[3], (E, D_IN), jnp.float32) * 0.02, 'router_b': jax.random.normal(ks[4], (E,), jnp.float32) * 0.02, 'lora_A': jax.random.normal(ks[5], (E, D_IN, R), jnp.float32) * 0.02, 'lora_B': jax.random.normal(ks[6], (E, R, D_OUT), jnp.float32) * 0.02}
    _L1_ffn_all = _L1_ffn_setup()
    _L1_ffn_in = {k: v for k, v in _L1_ffn_all.items() if k in ('base_w', 'base_b', 'router_w', 'router_b', 'lora_A', 'lora_B')}
    del _L1_ffn_all
    return {'x': x, 'ctx_1024': ctx_1024, 'g_xattn': g_xattn, 'g_ffn': g_ffn, 'L0_xattn_in_proj_w': _L0_xattn_in['in_proj_w'], 'L0_xattn_conv_w': _L0_xattn_in['conv_w'], 'L0_xattn_conv_b': _L0_xattn_in['conv_b'], 'L0_xattn_x_proj_w': _L0_xattn_in['x_proj_w'], 'L0_xattn_dt_proj_w': _L0_xattn_in['dt_proj_w'], 'L0_xattn_dt_proj_b': _L0_xattn_in['dt_proj_b'], 'L0_xattn_A_log': _L0_xattn_in['A_log'], 'L0_xattn_D': _L0_xattn_in['D'], 'L0_ffn_gate_weight': _L0_ffn_in['gate_weight'], 'L0_ffn_expert_bias': _L0_ffn_in['expert_bias'], 'L0_ffn_gate_proj': _L0_ffn_in['gate_proj'], 'L0_ffn_up_proj': _L0_ffn_in['up_proj'], 'L0_ffn_down_proj': _L0_ffn_in['down_proj'], 'L0_ffn_shared_gate': _L0_ffn_in['shared_gate'], 'L0_ffn_shared_up': _L0_ffn_in['shared_up'], 'L0_ffn_shared_down': _L0_ffn_in['shared_down'], 'L1_xattn_in_proj_w': _L1_xattn_in['in_proj_w'], 'L1_xattn_conv_w': _L1_xattn_in['conv_w'], 'L1_xattn_conv_b': _L1_xattn_in['conv_b'], 'L1_xattn_x_proj_w': _L1_xattn_in['x_proj_w'], 'L1_xattn_dt_proj_w': _L1_xattn_in['dt_proj_w'], 'L1_xattn_dt_proj_b': _L1_xattn_in['dt_proj_b'], 'L1_xattn_A_log': _L1_xattn_in['A_log'], 'L1_xattn_D': _L1_xattn_in['D'], 'L1_ffn_base_w': _L1_ffn_in['base_w'], 'L1_ffn_base_b': _L1_ffn_in['base_b'], 'L1_ffn_router_w': _L1_ffn_in['router_w'], 'L1_ffn_router_b': _L1_ffn_in['router_b'], 'L1_ffn_lora_A': _L1_ffn_in['lora_A'], 'L1_ffn_lora_B': _L1_ffn_in['lora_B']}

def reference(x, ctx_1024, g_xattn, g_ffn, L0_xattn_in_proj_w, L0_xattn_conv_w, L0_xattn_conv_b, L0_xattn_x_proj_w, L0_xattn_dt_proj_w, L0_xattn_dt_proj_b, L0_xattn_A_log, L0_xattn_D, L0_ffn_gate_weight, L0_ffn_expert_bias, L0_ffn_gate_proj, L0_ffn_up_proj, L0_ffn_down_proj, L0_ffn_shared_gate, L0_ffn_shared_up, L0_ffn_shared_down, L1_xattn_in_proj_w, L1_xattn_conv_w, L1_xattn_conv_b, L1_xattn_x_proj_w, L1_xattn_dt_proj_w, L1_xattn_dt_proj_b, L1_xattn_A_log, L1_xattn_D, L1_ffn_base_w, L1_ffn_base_b, L1_ffn_router_w, L1_ffn_router_b, L1_ffn_lora_A, L1_ffn_lora_B):
    import jax
    import jax.numpy as jnp

    def _L0_xattn_ref(hidden_states, z, in_proj_w, conv_w, conv_b, x_proj_w, dt_proj_w, dt_proj_b, A_log, D):
        import jax, jax.numpy as jnp
        import numpy as np
        import math
        B, L, DM = (2, 512, 256)
        DS, DC, EXP = (16, 4, 2)
        DI = EXP * DM
        DR = math.ceil(DM / 16)
        DT_MIN, DT_MAX, DT_FLOOR = (0.001, 0.1, 0.0001)

        def _ssm_forward(hidden_states, z, in_proj_w, conv_w, conv_b, x_proj_w, dt_proj_w, dt_proj_b, A_log, D):
            b = hidden_states.shape[0]
            x = jnp.einsum('ed,bld->bel', in_proj_w, hidden_states)
            xp = jnp.pad(x, ((0, 0), (0, 0), (DC - 1, 0)))
            xc = jax.lax.conv_general_dilated(xp, conv_w[:, None, :], window_strides=(1,), padding='VALID', dimension_numbers=('NCH', 'OIH', 'NCH'), feature_group_count=DI)
            u = jax.nn.silu(xc + conv_b[None, :, None])
            x_dbl = jnp.einsum('ke,bel->bkl', x_proj_w, u)
            dt_lo = x_dbl[:, :DR]
            Bm = x_dbl[:, DR:DR + DS]
            Cm = x_dbl[:, DR + DS:]
            delta = jax.nn.softplus(jnp.einsum('er,brl->bel', dt_proj_w, dt_lo) + dt_proj_b[None, :, None])
            A = -jnp.exp(A_log)

            def step(state, xs):
                d_t, B_t, C_t, u_t = xs
                dA = jnp.exp(d_t[..., None] * A)
                state = state * dA + (d_t * u_t)[..., None] * B_t[:, None, :]
                y_t = jnp.einsum('ben,bn->be', state, C_t)
                return (state, y_t)
            xs = (jnp.moveaxis(delta, -1, 0), jnp.moveaxis(Bm, -1, 0), jnp.moveaxis(Cm, -1, 0), jnp.moveaxis(u, -1, 0))
            state0 = jnp.zeros((b, DI, DS), delta.dtype)
            _, ys = jax.lax.scan(step, state0, xs)
            y = jnp.moveaxis(ys, 0, -1)
            y = y + D[None, :, None] * u
            y = y * jax.nn.silu(z)
            return jnp.swapaxes(y, 1, 2)
        return _ssm_forward(hidden_states, z, in_proj_w, conv_w, conv_b, x_proj_w, dt_proj_w, dt_proj_b, A_log, D)

    def _L0_ffn_ref(hidden_states, gate_weight, expert_bias, gate_proj, up_proj, down_proj, shared_gate, shared_up, shared_down):
        import jax, jax.numpy as jnp
        import numpy as np
        NUM_EXPERTS = 16
        TOP_K = 4
        N_GROUP = 4
        TOPK_GROUP = 2
        SCALING = 2.5

        def _route(x, gate_weight, expert_bias):
            logits = x @ gate_weight.T
            scores = jax.nn.sigmoid(logits)
            biased = scores + expert_bias[None, :]
            T = x.shape[0]
            gsz = NUM_EXPERTS // N_GROUP
            grp = biased.reshape(T, N_GROUP, gsz)
            top2, _ = jax.lax.top_k(grp, 2)
            group_scores = top2.sum(-1)
            _, gidx = jax.lax.top_k(group_scores, TOPK_GROUP)
            gmask = jax.nn.one_hot(gidx, N_GROUP, dtype=scores.dtype).sum(1)
            emask = jnp.repeat(gmask, gsz, axis=1)
            masked = jnp.where(emask > 0, biased, -jnp.inf)
            _, sel = jax.lax.top_k(masked, TOP_K)
            w = jnp.take_along_axis(scores, sel, axis=1)
            w = w / (w.sum(-1, keepdims=True) + 1e-20)
            return (w * SCALING, sel)

        def _moe(x, w, sel, gate_proj, up_proj, down_proj):
            cw = (jax.nn.one_hot(sel, NUM_EXPERTS, dtype=x.dtype) * w[..., None]).sum(1)

            def body(acc, inp):
                g, u, d, we = inp
                y = jax.nn.silu(x @ g.T) * (x @ u.T) @ d.T
                return (acc + we[:, None] * y, None)
            out, _ = jax.lax.scan(body, jnp.zeros_like(x), (gate_proj, up_proj, down_proj, cw.T))
            return out
        B, S, H = hidden_states.shape
        x = hidden_states.reshape(-1, H)
        w, sel = _route(x, gate_weight, expert_bias)
        out = _moe(x, w, sel, gate_proj, up_proj, down_proj)
        shared = jax.nn.silu(x @ shared_gate.T) * (x @ shared_up.T) @ shared_down.T
        return (out + shared).reshape(B, S, H)

    def _L1_xattn_ref(hidden_states, z, in_proj_w, conv_w, conv_b, x_proj_w, dt_proj_w, dt_proj_b, A_log, D):
        import jax, jax.numpy as jnp
        import numpy as np
        B_, L_, D_MODEL = (4, 512, 256)
        D_STATE, D_CONV, EXPAND = (16, 4, 2)
        D_INNER = EXPAND * D_MODEL
        DT_RANK = (D_MODEL + 15) // 16

        def silu(x):
            return x * jax.nn.sigmoid(x)
        Bsz, L, _ = hidden_states.shape
        d_inner, _, d_conv = conv_w.shape
        dt_rank = dt_proj_w.shape[1]
        d_state = A_log.shape[1]
        x = jnp.einsum('bld,ed->bel', hidden_states, in_proj_w)
        xc = jax.lax.conv_general_dilated(x, conv_w, window_strides=(1,), padding=[(d_conv - 1, 0)], feature_group_count=d_inner, dimension_numbers=('NCH', 'OIH', 'NCH'))
        x = silu(xc + conv_b[None, :, None])
        x_dbl = jnp.einsum('bdl,ed->bel', x, x_proj_w)
        dt_low, Bm, Cm = jnp.split(x_dbl, [dt_rank, dt_rank + d_state], axis=1)
        dt = jnp.einsum('brl,dr->bdl', dt_low, dt_proj_w)
        dt = jax.nn.softplus(dt + dt_proj_b[None, :, None])
        A = -jnp.exp(A_log)
        dt_t = jnp.moveaxis(dt, -1, 0)
        B_t = jnp.moveaxis(Bm, -1, 0)
        C_t = jnp.moveaxis(Cm, -1, 0)
        u_t = jnp.moveaxis(x, -1, 0)

        def step(state, inp):
            d, b, c, u = inp
            dA = jnp.exp(d[..., None] * A)
            state = state * dA + (d * u)[..., None] * b[:, None, :]
            y = jnp.einsum('bdn,bn->bd', state, c)
            return (state, y)
        state0 = jnp.zeros((Bsz, d_inner, d_state), x.dtype)
        _, ys = jax.lax.scan(step, state0, (dt_t, B_t, C_t, u_t))
        y = jnp.moveaxis(ys, 0, 2)
        y = y + D[None, :, None] * x
        y = y * silu(z)
        return jnp.swapaxes(y, 1, 2)

    def _L1_ffn_ref(x, base_w, base_b, router_w, router_b, lora_A, lora_B):
        import jax, jax.numpy as jnp
        import numpy as np
        B, S, D_IN, D_OUT, E, R = (4, 512, 512, 512, 8, 16)
        SCALING = 32.0 / 16.0
        b, s, d_in = x.shape
        n = b * s
        e = lora_A.shape[0]
        d_out = lora_B.shape[-1]
        result = jnp.einsum('bsd,od->bso', x, base_w) + base_b
        logits = jnp.einsum('bsd,ed->bse', x, router_w) + router_b
        probs = jax.nn.softmax(logits.astype(jnp.float32), axis=-1)
        top_vals, top_idx = jax.lax.top_k(probs, 2)
        top_vals = top_vals / jnp.sum(top_vals, axis=-1, keepdims=True)
        top_vals = top_vals.astype(x.dtype)
        flat_idx = top_idx.reshape(n, 2)
        flat_val = top_vals.reshape(n, 2)
        gate = jnp.zeros((n, e), x.dtype).at[jnp.arange(n)[:, None], flat_idx].set(flat_val)
        xf = x.reshape(n, d_in)
        mid = jnp.einsum('nd,edr->ner', xf, lora_A)
        mid = mid * gate[:, :, None]
        lora_out = jnp.einsum('ner,erd->nd', mid, lora_B)
        return result + SCALING * lora_out.reshape(b, s, d_out)
    x = x + jnp.tanh(g_xattn[0]) * _L0_xattn_ref(ctx_1024, _layernorm(x, axis=-1), L0_xattn_in_proj_w, L0_xattn_conv_w, L0_xattn_conv_b, L0_xattn_x_proj_w, L0_xattn_dt_proj_w, L0_xattn_dt_proj_b, L0_xattn_A_log, L0_xattn_D)
    x = x + jnp.tanh(g_ffn[0]) * _L0_ffn_ref(_layernorm(x, axis=-1), L0_ffn_gate_weight, L0_ffn_expert_bias, L0_ffn_gate_proj, L0_ffn_up_proj, L0_ffn_down_proj, L0_ffn_shared_gate, L0_ffn_shared_up, L0_ffn_shared_down)
    x = x + jnp.tanh(g_xattn[1]) * _L1_xattn_ref(ctx_1024, _layernorm(x, axis=-1), L1_xattn_in_proj_w, L1_xattn_conv_w, L1_xattn_conv_b, L1_xattn_x_proj_w, L1_xattn_dt_proj_w, L1_xattn_dt_proj_b, L1_xattn_A_log, L1_xattn_D)
    x = x + jnp.tanh(g_ffn[1]) * _L1_ffn_ref(_layernorm(x, axis=-1), L1_ffn_base_w, L1_ffn_base_b, L1_ffn_router_w, L1_ffn_router_b, L1_ffn_lora_A, L1_ffn_lora_B)
    return x

_drawn_inputs = setup_inputs


def setup_inputs(seed=0):
    import zlib

    import numpy as np

    out = dict(_drawn_inputs(seed))
    spreads = {'g_ffn': (-1.0, 0.551),
     'L0_xattn_conv_b': (0.0, 0.274),
     'L0_xattn_D': (1.0, 0.2),
     'L0_ffn_expert_bias': (0.0, 0.1),
     'L1_xattn_D': (1.0, 0.6)}
    factors = {'L0_xattn_dt_proj_w': 6.285,
     'L0_xattn_dt_proj_b': 2.874,
     'L1_xattn_in_proj_w': 3.133,
     'L1_xattn_conv_w': 3.191,
     'L1_xattn_conv_b': 8.0,
     'L1_xattn_x_proj_w': 8.0,
     'L1_xattn_dt_proj_w': 8.0,
     'L1_xattn_dt_proj_b': 8.0,
     'L1_xattn_A_log': 8.0,
     'L1_ffn_base_b': 3.838,
     'L1_ffn_router_b': 7.403}
    for name, (base, spread) in spreads.items():
        noise = np.random.default_rng([zlib.crc32(name.encode()), seed]).standard_normal(out[name].shape)
        drawn = base * np.exp(spread * noise) if base else spread * noise
        out[name] = jnp.asarray(drawn.astype(out[name].dtype))
    for name, factor in factors.items():
        out[name] = (out[name] * factor).astype(out[name].dtype)
    return out
```

```python
from contextlib import ExitStack

import concourse.bass as bass
from concourse import mybir

F32 = mybir.dt.float32
I32 = mybir.dt.int32
U32 = mybir.dt.uint32
ALU = mybir.AluOpType
ACT = mybir.ActivationFunctionType
AX = mybir.AxisListType

P = 128
NB, L, D = 4, 512, 512
DM, NS, DR, DC = 256, 16, 16, 4
ET, QT, KC = D // P, L // P, DM // P
NT = NB * QT
NE, TOPK, NGRP, GKEEP, SCALING = 16, 4, 4, 2, 2.5
GSZ = NE // NGRP
INNER = 256
IT = INNER // P
TILE = 256
RT = TILE // P
NTILE = NB * L * TOPK // TILE + NE
WGU = ET * INNER
WPK = 2 * WGU + IT * D
E1, RANK1, LSCALE = 8, 16, 2.0
EPS = 1e-5
CHC = DC + 3 + NS
C_CB, C_DB, C_D, C_A = DC, DC + 1, DC + 2, DC + 3
STAGES = 2 * NB
HS = 2 * NS
BODY = 4
FIRST_B = NB + 1
TPS = NTILE // (STAGES - FIRST_B)
BIG = 3.0e38

PRE_SCAN, PRE_MULC, PRE_W, PRE_H, PRE_Y, PRE_YEV, PRE_YS = 2, 8, 4, 2, 4, 2, 16


def build(nc, t):
    with ExitStack() as ctx:
        def sb(name, shape, dt=F32):
            return ctx.enter_context(nc.sbuf_tensor(name, shape, dt))

        def sem(name):
            return ctx.enter_context(nc.semaphore(name))

        X = sb("x_res", [P, NT, D])
        Y = sb("y_scan", [P, NB, ET, L])
        DEL = sb("delta", [P, 2, ET, L])
        DU = sb("du", [P, 2, ET, L])
        DA = sb("decay", [P, 2, 2, L])
        W = sb("state", [P, 4, 2, L])
        BC = sb("bc_rows", [P, 4, 2, L])
        SW = sb("softplus_tmp", [P, ET, L])
        ZS = sb("z_gate", [P, QT, D])
        YSB = sb("expert_out", [P, RT, D])
        HB = sb("hidden", [P, 2, 2 * TILE])
        MW = sb("expert_w", [P, 2, WPK])
        CTX = sb("ctx_t", [P, KC, L])
        INW = sb("in_w", [P, KC, D])
        XPW = sb("xproj_w", [P, 2, ET, DR + 2 * NS])
        DTW = sb("dt_w", [DR + 2 * NS, D])
        CH = sb("chan", [P, 2, ET, CHC])
        AN = sb("neg_a", [P, 2, ET, NS])
        XDBL = sb("x_dbl", [DR + 2 * NS, L])
        ID = sb("ident", [P, P])
        US = sb("upper", [P, P])
        ON = sb("ones", [P, P])
        TRI = sb("tri", [P, NE, NE])
        GW = sb("router_w", [P, ET, NE])
        EB = sb("expert_bias", [P, NE])
        TG = sb("tanh_gates", [P, 4])
        R1 = sb("router1_w", [P, ET, E1])
        RB = sb("router1_b", [P, E1])
        MV = sb("mean_var", [P, QT, 2])
        RS = sb("rstd", [P, QT])
        NBI = sb("neg_mean_rstd", [P, QT])
        SC = sb("scores", [P, QT, NE])
        RK = sb("rank", [P, NT, NE])
        CW = sb("route_w", [P, NT, NE])
        SEL = sb("selected", [P, NT, NE])
        SM = sb("small", [P, 8, QT * NE])
        SLU = sb("slots", [P, TOPK, NT], U32)
        CWK = sb("slot_w", [P, TOPK, NT])
        TE = sb("tile_expert", [P, NTILE + 2], I32)

        def flat(ap):
            return ap.rearrange("p a b -> p (a b)")

        ST = SM[:, 7, 0:QT * 6].rearrange("p (q s) -> p q s", s=6)
        XN, XNT = Y[:, 2], Y[:, 3]
        XS = ZS[:, 0:RT]
        XST = flat(ZS[:, RT:QT]).rearrange("p (k r) -> p k r", k=ET)
        HT = HB[:, :, :].rearrange("p s (i r) -> p s i r", i=IT)
        T1, T2 = flat(ZS[:, 0:2]), flat(ZS[:, 2:4])
        GK = W[:, :, :, :].rearrange("p (s a) b n -> p s (a b) n", s=2)
        BW = MW[:, 0, 0:ET * D].rearrange("p (k n) -> p k n", k=ET)
        LA = MW[:, 0, ET * D:ET * D + ET * P].rearrange("p (k n) -> p k n", k=ET)
        LB = MW[:, 0, ET * D + ET * P:ET * D + ET * P + D]
        BB = SW[0:1, 0, :]
        XN1, XNT1 = [DEL[:, 0], DEL[:, 1]], [DU[:, 0], DU[:, 1]]
        MID, MIDT = BC[:, 0, 0:1].rearrange("p a (q n) -> p (a q) n", q=QT), BC[:, 1, 0]

        PS = ctx.enter_context(nc.psum_tensor("banks", [P, 8, 512], F32))
        PRE = [PS[:, 4], PS[:, 5]]
        AUX = [PS[:, 6], PS[:, 7]]
        XT = flat(PS[:, 6:8]).rearrange("p (k r) -> p k r", k=ET)

        bc_d = nc.dram_tensor("bc_d", (STAGES, 2 * NS, L), F32, kind="Internal").ap()
        xn_d = nc.dram_tensor("xn_d", (NB * L, D), F32, kind="Internal").ap()
        xs_d = nc.dram_tensor("xs_d", ((NTILE + 1) * TILE, D), F32, kind="Internal").ap()
        ys_d = nc.dram_tensor("ys_d", (NTILE * TILE, D), F32, kind="Internal").ap()
        xs_t = xs_d.rearrange("(j r p) n -> j p r n", p=P, r=RT)
        ys_t = ys_d.rearrange("(j r p) n -> j p r n", p=P, r=RT)
        xn_t = xn_d.rearrange("(b q p) n -> b p q n", p=P, q=QT)
        x_t = t["x"].rearrange("b (q p) n -> b p q n", p=P)
        out_t = t["out"].rearrange("b (q p) n -> b p q n", p=P)

        ld_chan, ld_proj, ld_small, ld_shared = sem("ld_chan"), sem("ld_proj"), sem("ld_small"), sem("ld_shared")
        ld_x = [sem(f"ld_x{b}") for b in range(NB)]
        ld_inw, ld_dtw, ld_ffn1 = sem("ld_inw"), sem("ld_dtw"), sem("ld_ffn1")
        ctx_in, bc_stored = sem("ctx_in"), sem("bc_stored")
        bc_in = [sem(f"bc_in{u}") for u in range(BODY)]
        xn_stored, zero_filled = sem("xn_stored"), sem("zero_filled")
        staged = [sem(f"staged{i}") for i in range(2)]
        scattered = [sem(f"scattered{i}") for i in range(2)]
        tw_in = [sem(f"tw_in{i}") for i in range(2)]
        xs_in, ys_stored, gathered, out_stored = sem("xs_in"), sem("ys_stored"), sem("gathered"), sem("out_stored")
        masks, zeroed, a_ready, tg_ready, counts = sem("masks"), sem("zeroed"), sem("a_ready"), sem("tg_ready"), sem("counts")
        inproj_done, tap_first, conv_step, u_ready = sem("inproj_done"), sem("tap_first"), sem("conv_step"), sem("u_ready")
        xproj_done, xdbl_ready, dt_done, dt_read = sem("xproj_done"), sem("xdbl_ready"), sem("dt_done"), sem("dt_read")
        e_ready, w1_ready, corr_ready, ln_ready = sem("e_ready"), sem("w1_ready"), sem("corr_ready"), sem("ln_ready")
        delta_ready, seed_ready, du_ready = sem("delta_ready"), sem("seed_ready"), sem("du_ready")
        da_ready, mulb_done, scan_done = sem("da_ready"), sem("mulb_done"), sem("scan_done")
        mulc_done, w_free, seeded, y4_ready = sem("mulc_done"), sem("w_free"), sem("seeded"), sem("y4_ready")
        var_ready, std_ready, zn_ready, zs_ready = sem("var_ready"), sem("std_ready"), sem("zn_ready"), sem("zs_ready")
        yg_done, yt_done, xacc = sem("yg_done"), sem("yt_done"), sem("xacc")
        xn_ready, xnt_done, xnt_ready = sem("xn_ready"), sem("xnt_done"), sem("xnt_ready")
        router_done, sc_ready, ranked = sem("router_done"), sem("sc_ready"), sem("ranked")
        counted, slots_ready = sem("counted"), sem("slots_ready")
        shgu_done, shsil_ready, shh_ready, shdown_done, shacc = (
            sem("shgu_done"), sem("shsil_ready"), sem("shh_ready"), sem("shdown_done"), sem("shacc"))
        xt_done, xst_ready, gu_done, sil_ready, h_ready = (
            sem("xt_done"), sem("xst_ready"), sem("gu_done"), sem("sil_ready"), sem("h_ready"))
        y_done, yev, dve_step = sem("y_done"), sem("yev"), sem("dve_step")
        combined, logit_done, exp_ready, shift_ready = sem("combined"), sem("logit_done"), sem("exp_ready"), sem("shift_ready")
        mid_done, midg_ready, midt_done, midt_ready, ffn_done, x_final = (
            sem("mid_done"), sem("midg_ready"), sem("midt_done"), sem("midt_ready"), sem("ffn_done"), sem("x_final"))

        def lay(s):
            return s // NB

        def yslot(s):
            return s % 2 if s < NB else s - NB

        def bcast2(row):
            return row.unsqueeze(1).to_broadcast([P, 2, L])

        block = ctx.enter_context(nc.Block())

        @block.sync
        def _(sp):
            def load_ctx(s):
                if s > 0:
                    sp.wait_ge(inproj_done, ET * s)
                b = s % NB
                sp.dma_start(CTX[:, :, :], t["ctxT"].rearrange("(k p) n -> p k n", p=P)[:, :, b * L:(b + 1) * L]
                             ).then_inc(ctx_in, 16)

            def load_layer(layer):
                if layer:
                    sp.wait_ge(inproj_done, ET * NB)
                sp.dma_start(INW[:, :, :], t[f"in_wT{layer}"].rearrange("(k p) n -> p k n", p=P)).then_inc(ld_inw, 16)
                if layer:
                    sp.wait_ge(dt_done, ET * NB)
                sp.dma_start(DTW[2 * NS:, :], t[f"dtT{layer}"]).then_inc(ld_dtw, 16)

            def load_bc(s, i, u):
                n = i * BODY + u
                sp.wait_ge(mulc_done, i * (2 * BODY) + (HS * s + 2 * u + PRE_MULC - 2 * BODY + 2))
                src = bc_d[s].rearrange("(c n) l -> n c l", c=2)[bass.ds(n, 1), :, :]
                sp.dma_start(BC[:, u, :, :], src.rearrange("a c l -> (a c) l").partition_broadcast(P)
                             ).then_inc(bc_in[u], 16)

            def scan_loads(s):
                sp.wait_ge(bc_stored, 16 * (s + 1))
                with sp.Fori(0, NS // BODY) as i:
                    for u in range(BODY):
                        load_bc(s, i, u)

            def load_tile_w(j, slot):
                sp.wait_ge(y_done, j * 2 + (PRE_Y - 2))
                e = sp.value_load(TE[0:1, bass.ds(j, 1)] if not isinstance(j, int) else TE[0:1, j:j + 1],
                                  min_val=0, max_val=NE - 1)
                sp.dma_start(MW[:, slot, :], t["moe_w"][bass.ds(e, 1), :, :].rearrange("a p n -> p (a n)")
                             ).then_inc(tw_in[slot], 16)

            def load_tile_x(j):
                sp.wait_ge(xt_done, j)
                src = xs_t[bass.ds(j, 1)] if not isinstance(j, int) else xs_t[j:j + 1]
                sp.dma_start(XS, src.rearrange("a p r n -> p (a r) n")).then_inc(xs_in, 16)

            def store_tile(j):
                sp.wait_ge(yev, j * 2 + (2 + PRE_YEV))
                dst = ys_t[bass.ds(j, 1)]
                sp.dma_start(dst.rearrange("a p r n -> p (a r) n"), YSB[:, :, :]).then_inc(ys_stored, 16)

            load_layer(0)
            load_ctx(0)
            for layer in range(2):
                sp.dma_start(CH[:, layer], t[f"chan{layer}"].rearrange("(e p) n -> p e n", p=P)).then_inc(ld_chan, 16)
                sp.dma_start(XPW[:, layer], t[f"xprojT{layer}"].rearrange("(e p) n -> p e n", p=P)).then_inc(ld_proj, 16)
            sp.dma_start(TG[:, :], t["gates"][0, :].partition_broadcast(P)).then_inc(ld_small, 16)
            sp.dma_start(GW[:, :, :], t["gwT"].rearrange("(k p) n -> p k n", p=P)).then_inc(ld_small, 16)
            sp.dma_start(EB[:, :], t["ebias"][0, :].partition_broadcast(P)).then_inc(ld_small, 16)
            sp.dma_start(R1[:, :, :], t["r1T"].rearrange("(k p) n -> p k n", p=P)).then_inc(ld_small, 16)
            sp.dma_start(RB[:, :], t["rb"][0, :].partition_broadcast(P)).then_inc(ld_small, 16)
            for b in range(NB):
                sp.dma_start(X[:, b * QT:(b + 1) * QT, :], x_t[b]).then_inc(ld_x[b], 16)
            sp.dma_start(MW[:, 0, :], t["moe_w"][NE]).then_inc(ld_shared, 16)
            load_ctx(1)
            sp.wait_ge(zeroed, 2)
            rows = (NTILE + 1) * TILE // P
            per = rows // 7
            xs_rows = xs_d.rearrange("(c p) n -> p c n", p=P)
            for c in range(7):
                sp.dma_start(xs_rows[:, c * per:(c + 1) * per, :],
                             YSB[:, 0:1, :].to_broadcast([P, per, D])).then_inc(zero_filled, 16)
            for s in range(FIRST_B):
                load_ctx(s + 2)
                scan_loads(s)
                if s < NB:
                    sp.wait_ge(xn_ready, QT * (s + 1))
                    sp.dma_start(xn_t[s], XN).then_inc(xn_stored, 16)
                if s == 1:
                    load_layer(1)
                if s == NB - 1:
                    sp.wait_ge(xnt_done, QT * NB)
                    sp.wait_ge(shgu_done, IT * NB)
                    sp.wait_ge(xn_stored, 16 * NB)
                    for b in range(2):
                        sp.dma_start([XN, XNT][b], xn_t[b]).then_inc(staged[b], 16)
            for b in range(2, NB):
                sp.wait_ge(scattered[b % 2], 16 * QT * TOPK)
                sp.dma_start([XN, XNT][b % 2], xn_t[b]).then_inc(staged[b % 2], 16)
            sp.wait_ge(slots_ready, 2)
            sp.wait_ge(shdown_done, QT * NB)
            load_tile_w(0, 0)
            load_tile_w(1, 1)
            for i in range(2):
                sp.wait_ge(scattered[i], 16 * 2 * QT * TOPK)
            load_tile_x(0)
            for s in range(FIRST_B, STAGES):
                if s + 1 < STAGES:
                    if s + 2 < STAGES:
                        load_ctx(s + 2)
                sp.wait_ge(bc_stored, 16 * (s + 1))
                last = s == STAGES - 1
                with sp.Fori(0, NS // BODY) as i:
                    for u in range(BODY):
                        load_bc(s, i, u)
                    for u in range(BODY):
                        j = i * BODY + (TPS * (s - FIRST_B) + u)
                        load_tile_x(j + 1)
                        if u:
                            store_tile(j - 1)
                        load_tile_w(j + 2, u % 2)
                    store_tile(i * BODY + (TPS * (s - FIRST_B) + BODY - 1))
            for i in range(2):
                sp.wait_ge(tw_in[i], 16 * (NTILE // 2 + 1))
            sp.dma_start(BW, t["base_wT"].rearrange("(k p) n -> p k n", p=P)).then_inc(ld_ffn1, 16)
            sp.dma_start(LA, t["loraA"].rearrange("(k p) n -> p k n", p=P)).then_inc(ld_ffn1, 16)
            sp.dma_start(LB, t["loraB"]).then_inc(ld_ffn1, 16)
            sp.wait_ge(du_ready, STAGES)
            sp.dma_start(BB, t["base_b"]).then_inc(ld_ffn1, 16)
            for b in range(NB):
                sp.wait_ge(x_final, QT * (b + 1))
                sp.dma_start(out_t[b], X[:, b * QT:(b + 1) * QT, :]).then_inc(out_stored, 16)
            sp.wait_ge(out_stored, 16 * NB)

        @block.gpsimd
        def _(pool):
            pool.sem_inc(mulc_done, PRE_MULC)
            nc.gpsimd.memset(ID[:, :], 0.0).then_inc(masks, 1)
            nc.gpsimd.memset(ON[:, :], 1.0).then_inc(masks, 1)
            nc.gpsimd.memset(TRI[:, :, :], 1.0).then_inc(masks, 1)
            pool.wait_ge(masks, 3)
            nc.gpsimd.affine_select(out=ID[:, :], in_=ID[:, :], compare_op=ALU.not_equal, fill=1.0, base=0,
                                    pattern=[[-1, P]], channel_multiplier=1).then_inc(masks, 1)
            nc.gpsimd.affine_select(out=US[:, :], in_=ON[:, :], compare_op=ALU.is_gt, fill=0.0, base=0,
                                    pattern=[[1, P]], channel_multiplier=-1).then_inc(masks, 1)
            nc.gpsimd.affine_select(out=TRI[:, :, :], in_=TRI[:, :, :], compare_op=ALU.is_gt, fill=0.0, base=0,
                                    pattern=[[1, NE], [-1, NE]], channel_multiplier=0).then_inc(masks, 1)

            def mul_c(s):
                with pool.Fori(0, NS // BODY) as i:
                    for c in range(2 * BODY):
                        pool.wait_ge(scan_done, i * (2 * BODY) + (HS * s + c + 1 + PRE_SCAN))
                        nc.gpsimd.tensor_tensor(W[:, c % 4], W[:, c % 4], bcast2(BC[:, c // 2, 1, :]),
                                                ALU.mult).then_inc(mulc_done, 1)

            for s in range(NB):
                mul_c(s)
            pool.wait_ge(slots_ready, 2)
            pool.wait_ge(zero_filled, 16 * 7)
            for b in range(NB):
                pool.wait_ge(staged[b % 2], 16 * (b // 2 + 1))
                for q in range(QT):
                    for k in range(TOPK):
                        nc.gpsimd.indirect_dma_start(
                            out=xs_d, out_offset=bass.IndirectOffsetOnAxis(ap=SLU[:, k, b * QT + q:b * QT + q + 1], axis=0),
                            in_=[XN, XNT][b % 2][:, q, :], in_offset=None).then_inc(scattered[b % 2], 16)
            for s in range(FIRST_B, STAGES):
                mul_c(s)
            pool.wait_ge(w_free, HS * STAGES + PRE_W)
            pool.wait_ge(ys_stored, 16 * NTILE + PRE_YS)
            for g in range(NT):
                if g >= 2:
                    pool.wait_ge(combined, TOPK * (g - 1))
                for k in range(TOPK):
                    nc.gpsimd.indirect_dma_start(
                        out=GK[:, g % 2, k, :], out_offset=None, in_=ys_d,
                        in_offset=bass.IndirectOffsetOnAxis(ap=SLU[:, k, g:g + 1], axis=0)).then_inc(gathered, 16)
                pool.wait_ge(gathered, 16 * TOPK * (g + 1))

        @block.scalar
        def _(act):
            def conv_tap(s):
                sl = s % 2
                if s >= 2:
                    act.wait_ge(scan_done, HS * (s - 1) + PRE_SCAN)
                for et in range(ET):
                    act.wait_ge(inproj_done, ET * s + et + 1)
                    nc.scalar.activation(DU[:, sl, et, :], PRE[et % 2], ACT.Identity, bias=CH[:, lay(s), et, C_CB:C_CB + 1],
                                         scale=CH[:, lay(s), et, DC - 1:DC]).then_inc(tap_first, 1)

            def conv_silu(s):
                act.wait_ge(conv_step, 3 * ET * (s + 1))
                nc.scalar.activation(flat(DU[:, s % 2]), flat(DU[:, s % 2]), ACT.Silu).then_inc(u_ready, 1)

            def x_dbl(s):
                act.wait_ge(xproj_done, s + 1)
                if s:
                    act.wait_ge(bc_stored, 16 * s)
                    act.wait_ge(dt_done, ET * s)
                nc.scalar.activation(XDBL[:, :], PRE[0][0:DR + 2 * NS, :], ACT.Copy).then_inc(xdbl_ready, 1)
                act.wait_ge(xdbl_ready, s + 1)
                act.dma_start(bc_d[s], XDBL[0:2 * NS, :]).then_inc(bc_stored, 16)

            def step_size(s):
                sl = s % 2
                if 2 <= s < NB + 2:
                    act.wait_ge(yt_done, QT * (s - 1))
                elif s >= NB + 2:
                    act.wait_ge(scattered[s % 2], 16 * 2 * QT * TOPK)
                for et in range(ET):
                    act.wait_ge(dt_done, ET * s + et + 1)
                    bias = CH[:, lay(s), et, C_DB:C_DB + 1]
                    nc.scalar.activation(DEL[:, sl, et, :], PRE[et % 2], ACT.Abs, bias=bias)
                    nc.scalar.activation(Y[:, yslot(s), et, :], PRE[et % 2], ACT.Relu, bias=bias).then_inc(dt_read, 1)
                act.wait_ge(dt_read, ET * (s + 1))
                nc.scalar.activation(flat(DEL[:, sl]), flat(DEL[:, sl]), ACT.Exp, scale=-1.0).then_inc(e_ready, 1)
                act.wait_ge(corr_ready, s + 1)
                nc.scalar.activation(flat(SW[:, :, :]), flat(SW[:, :, :]), ACT.Ln).then_inc(ln_ready, 1)

            def seed(s):
                act.wait_ge(delta_ready, s + 1)
                act.wait_ge(u_ready, s + 1)
                for et in range(ET):
                    ins = nc.scalar.activation(Y[:, yslot(s), et, :], DU[:, s % 2, et, :], ACT.Identity,
                                               scale=CH[:, lay(s), et, C_D:C_D + 1])
                ins.then_inc(seed_ready, 1)

            def z_gate(f):
                act.wait_ge(zn_ready, f + 1)
                b = f % NB
                for q in range(QT):
                    ins = nc.scalar.activation(ZS[:, q, :], X[:, b * QT + q, :], ACT.Silu, bias=NBI[:, q:q + 1],
                                               scale=RS[:, q:q + 1])
                ins.then_inc(zs_ready, 1)

            def std(v):
                act.wait_ge(var_ready, v + 1)
                nc.scalar.activation(RS[:, :], RS[:, :], ACT.Sqrt).then_inc(std_ready, 1)

            def decay(s, i, c):
                act.wait_ge(scan_done, i * (2 * BODY) + (HS * s + c + PRE_SCAN - 1))
                for m in range(2):
                    et = 2 * (c % 2) + m
                    ins = nc.scalar.activation(DA[:, c % 2, m, 1:], DEL[:, s % 2, et, 1:], ACT.Exp,
                                               scale=AN[:, lay(s), et, bass.ds(i * BODY + c // 2, 1)])
                ins.then_inc(da_ready, 1)

            def decays(s):
                act.wait_ge(delta_ready, s + 1)
                with act.Fori(0, NS // BODY) as i:
                    for c in range(2 * BODY):
                        decay(s, i, c)

            def norm_t(f, xnt):
                for k in range(ET):
                    act.wait_ge(xnt_done, ET * f + k + 1)
                    nc.scalar.activation(xnt[:, k, :], AUX[k % 2], ACT.Copy).then_inc(xnt_ready, 1)

            def shared_silu(b):
                for it in range(IT):
                    act.wait_ge(shgu_done, IT * b + it + 1)
                    if b:
                        act.wait_ge(shdown_done, QT * b)
                    nc.scalar.activation(HB[:, it, :], PS[:, 2 * it], ACT.Silu).then_inc(shsil_ready, 1)

            def tile_rows(j):
                act.wait_ge(xt_done, j + 1)
                act.wait_ge(gu_done, j * 2)
                nc.scalar.activation(flat(XST), flat(XT), ACT.Copy).then_inc(xst_ready, 1)

            def tile_silu(j, u, it):
                act.wait_ge(gu_done, j * 2 + it + 1)
                act.wait_ge(y_done, j * 2 + (PRE_Y - 2))
                nc.scalar.activation(HT[:, u % 2, it, :], PS[:, it, 0:TILE], ACT.Silu).then_inc(sil_ready, 1)

            def tile_out(j):
                act.wait_ge(ys_stored, j * 16 + PRE_YS)
                for r in range(RT):
                    act.wait_ge(y_done, j * 2 + (r + 1 + PRE_Y))
                    nc.scalar.activation(YSB[:, r, :], PS[:, 2 + r], ACT.Copy).then_inc(yev, 1)

            act.wait_ge(ld_small, 16 * 5)
            nc.scalar.activation(TG[:, :], TG[:, :], ACT.Tanh).then_inc(tg_ready, 1)
            act.wait_ge(ld_chan, 32)
            for layer in range(2):
                nc.scalar.activation(AN[:, layer], CH[:, layer, :, C_A:C_A + NS], ACT.Exp).then_inc(a_ready, 1)
            act.wait_ge(a_ready, 2)
            nc.scalar.activation(AN[:, :, :, :], AN[:, :, :, :], ACT.Copy, scale=-1.0).then_inc(a_ready, 1)
            act.wait_ge(a_ready, 3)
            act.wait_ge(zeroed, 2)
            act.sem_inc(yev, PRE_YEV)
            act.sem_inc(ys_stored, PRE_YS)

            def prepare(s):
                conv_tap(s)
                conv_silu(s)
                if 2 <= s <= NB + 1:
                    shared_silu(s - 2)
                x_dbl(s)
                step_size(s)
                seed(s)

            prepare(0)
            prepare(1)
            std(0)
            z_gate(0)
            for s in range(FIRST_B):
                decays(s)
                if s < NB:
                    std(2 * s + 1)
                    norm_t(s, XNT)
                    act.wait_ge(router_done, s + 1)
                    nc.scalar.activation(SC[:, :, :], AUX[0][:, 0:QT * NE].rearrange("p (q e) -> p q e", e=NE),
                                         ACT.Sigmoid).then_inc(sc_ready, 1)
                    prepare(s + 2)
                    if s + 1 < NB:
                        std(2 * s + 2)
                        z_gate(s + 1)
            act.wait_ge(w_free, HS * FIRST_B + PRE_W)
            nc.scalar.activation(flat(Y[:, 0]), flat(PS[:, 0:4]), ACT.Copy).then_inc(y4_ready, 1)
            for s in range(FIRST_B, STAGES):
                if s + 1 < STAGES:
                    prepare(s + 1)
                if s == FIRST_B:
                    act.wait_ge(xt_done, 1)
                    nc.scalar.activation(flat(XST), flat(XT), ACT.Copy).then_inc(xst_ready, 1)
                act.wait_ge(delta_ready, s + 1)
                with act.Fori(0, NS // BODY) as i:
                    for u in range(BODY):
                        j = i * BODY + (TPS * (s - FIRST_B) + u)
                        decay(s, i, 2 * u)
                        decay(s, i, 2 * u + 1)
                        tile_silu(j, u, 0)
                        if u:
                            tile_out(j - 1)
                        tile_silu(j, u, 1)
                        tile_rows(j + 1)
                    tile_out(i * BODY + (TPS * (s - FIRST_B) + BODY - 1))
            for b in range(NB):
                std(2 * (NB + b))
                z_gate(NB + b)
                std(2 * (NB + b) + 1)
                norm_t(NB + b, XNT1[b % 2])
                act.wait_ge(shift_ready, b + 1)
                nc.scalar.activation(SM[:, 1, 0:QT * E1], SM[:, 0, 0:QT * E1], ACT.Exp).then_inc(exp_ready, 1)
                act.wait_ge(midt_done, b + 1)
                if b:
                    act.wait_ge(ffn_done, QT * b)
                nc.scalar.activation(MIDT, AUX[1], ACT.Copy).then_inc(midt_ready, 1)

        @block.tensor
        def _(pe):
            def in_proj(s):
                pe.wait_ge(ctx_in, 16 * (s + 1))
                pe.wait_ge(ld_inw, 16 * (lay(s) + 1))
                if s:
                    pe.wait_ge(dt_read, ET * s)
                for et in range(ET):
                    if et >= 2:
                        pe.wait_ge(conv_step, 3 * ET * s + 4 + et - 1)
                    for k in range(KC):
                        mm = nc.tensor.matmul(PRE[et % 2], INW[:, k, et * P:(et + 1) * P], CTX[:, k, :],
                                              start=(k == 0), stop=(k == KC - 1))
                    mm.then_inc(inproj_done, 1)

            def x_proj(s):
                pe.wait_ge(u_ready, s + 1)
                pe.wait_ge(ld_proj, 32)
                for et in range(ET):
                    mm = nc.tensor.matmul(PRE[0][0:DR + 2 * NS, :], XPW[:, lay(s), et, :], DU[:, s % 2, et, :],
                                          start=(et == 0), stop=(et == ET - 1))
                mm.then_inc(xproj_done, 1)

            def dt_proj(s):
                pe.wait_ge(xdbl_ready, s + 1)
                pe.wait_ge(ld_dtw, 16 * (lay(s) + 1))
                for et in range(ET):
                    if et >= 2:
                        pe.wait_ge(dt_read, ET * s + et - 1)
                    nc.tensor.matmul(PRE[et % 2], DTW[2 * NS:, et * P:(et + 1) * P], XDBL[2 * NS:, :],
                                     start=True, stop=True).then_inc(dt_done, 1)

            def state_sum(s):
                pe.wait_ge(seed_ready, s + 1)
                if 1 <= s:
                    pe.wait_ge(shacc, QT * min(s, NB))
                for et in range(ET):
                    nc.tensor.matmul(PS[:, et], ID[:, :], Y[:, yslot(s), et, :], start=True, stop=True)
                with pe.Fori(0, NS // BODY) as i:
                    for c in range(2 * BODY):
                        pe.wait_ge(mulc_done, i * (2 * BODY) + (HS * s + c + 1 + PRE_MULC))
                        for m in range(2):
                            mm = nc.tensor.matmul(PS[:, 2 * (c % 2) + m], ID[:, :], W[:, c % 4, m, :],
                                                  start=False, stop=True, skip_group_check=True)
                        mm.then_inc(w_free, 1)

            def y_transposes(f, y):
                pe.wait_ge(yg_done, f + 1)
                for lt in range(QT):
                    if lt >= 2:
                        pe.wait_ge(xacc, QT * f + lt - 1)
                    for et in range(ET):
                        mm = nc.tensor.transpose(AUX[lt % 2][:, et * P:(et + 1) * P], y[:, et, lt * P:(lt + 1) * P], ID[:, :])
                    mm.then_inc(yt_done, 1)

            def norm_transposes(f, xn):
                pe.wait_ge(xn_ready, QT * (f + 1))
                for k in range(ET):
                    if k >= 2:
                        pe.wait_ge(xnt_ready, ET * f + k - 1)
                    for q in range(QT):
                        mm = nc.tensor.transpose(AUX[k % 2][:, q * P:(q + 1) * P], xn[:, q, k * P:(k + 1) * P], ID[:, :])
                    mm.then_inc(xnt_done, 1)

            def route(f, xnt, w, n, done):
                pe.wait_ge(xnt_ready, ET * (f + 1))
                for q in range(QT):
                    for k in range(ET):
                        mm = nc.tensor.matmul(AUX[0][:, q * n:(q + 1) * n], xnt[:, k, q * P:(q + 1) * P], w[:, k, :],
                                              start=(k == 0), stop=(k == ET - 1))
                mm.then_inc(done, 1)

            def shared_in(b):
                pe.wait_ge(ld_shared, 16)
                for it in range(IT):
                    for g in range(2):
                        for k in range(ET):
                            at = g * WGU + k * INNER + it * P
                            mm = nc.tensor.matmul(PS[:, 2 * it + g], MW[:, 0, at:at + P], XNT[:, k, :],
                                                  start=(k == 0), stop=(k == ET - 1))
                    mm.then_inc(shgu_done, 1)

            def shared_out(b):
                pe.wait_ge(shh_ready, IT * (b + 1))
                for q in range(QT):
                    for it in range(IT):
                        at = 2 * WGU + it * D
                        mm = nc.tensor.matmul(PS[:, q], HB[:, it, q * P:(q + 1) * P], MW[:, 0, at:at + D],
                                              start=(it == 0), stop=(it == IT - 1))
                    mm.then_inc(shdown_done, 1)

            def tile_transposes(j):
                pe.wait_ge(xs_in, j * 16 + 16)
                pe.wait_ge(xst_ready, j)
                for k in range(ET):
                    for r in range(RT):
                        mm = nc.tensor.transpose(XT[:, k, r * P:(r + 1) * P], XS[:, r, k * P:(k + 1) * P], ID[:, :])
                mm.then_inc(xt_done, 1)

            def tile_in(j, u, half):
                pe.wait_ge(tw_in[u % 2], half * 16 + 16)
                pe.wait_ge(xst_ready, j + 1)
                for it in range(IT):
                    pe.wait_ge(h_ready, j * 2 + (it - 1 + PRE_H))
                    for g in range(2):
                        for k in range(ET):
                            at = g * WGU + k * INNER + it * P
                            mm = nc.tensor.matmul(PS[:, it, g * TILE:(g + 1) * TILE], MW[:, u % 2, at:at + P], XST[:, k, :],
                                                  start=(k == 0), stop=(k == ET - 1))
                    mm.then_inc(gu_done, 1)

            def tile_out(j, u):
                pe.wait_ge(h_ready, j * 2 + (2 + PRE_H))
                for r in range(RT):
                    pe.wait_ge(yev, j * 2 + (r - 1 + PRE_YEV))
                    for it in range(IT):
                        at = 2 * WGU + it * D
                        mm = nc.tensor.matmul(PS[:, 2 + r], HT[:, u % 2, it, r * P:(r + 1) * P], MW[:, u % 2, at:at + D],
                                              start=(it == 0), stop=(it == IT - 1))
                    mm.then_inc(y_done, 1)

            pe.sem_inc(w_free, PRE_W)
            pe.sem_inc(y_done, PRE_Y)
            pe.wait_ge(masks, 6)
            for s in range(2):
                in_proj(s)
                x_proj(s)
                dt_proj(s)
            for s in range(FIRST_B):
                state_sum(s)
                if s < NB:
                    y_transposes(s, Y[:, yslot(s)])
                    norm_transposes(s, XN)
                    route(s, XNT, GW, NE, router_done)
                    in_proj(s + 2)
                    shared_in(s)
                    x_proj(s + 2)
                    shared_out(s)
                    dt_proj(s + 2)
                if s == NB - 1:
                    pe.wait_ge(ranked, NB)
                    sel = SEL[:, :, :].rearrange("p t e -> p (t e)")
                    nc.tensor.matmul(AUX[0][:, 0:NT * NE], US[:, :], sel, start=True, stop=True)
                    nc.tensor.matmul(AUX[1][:, 0:NT * NE], ON[:, :], sel, start=True, stop=True).then_inc(counted, 1)
            for s in range(FIRST_B, STAGES):
                if s + 1 < STAGES:
                    in_proj(s + 1)
                    x_proj(s + 1)
                    dt_proj(s + 1)
                if s == FIRST_B:
                    pe.wait_ge(slots_ready, 2)
                    pe.wait_ge(xs_in, 16)
                    for k in range(ET):
                        for r in range(RT):
                            mm = nc.tensor.transpose(XT[:, k, r * P:(r + 1) * P], XS[:, r, k * P:(k + 1) * P], ID[:, :])
                    mm.then_inc(xt_done, 1)
                    pe.wait_ge(y4_ready, 1)
                with pe.Fori(0, NS // BODY) as i:
                    for u in range(BODY):
                        j = i * BODY + (TPS * (s - FIRST_B) + u)
                        tile_in(j, u, i * 2 + (TPS // 2 * (s - FIRST_B) + u // 2))
                        tile_transposes(j + 1)
                        tile_out(j, u)
            pe.wait_ge(ld_ffn1, 16 * 4)
            pe.wait_ge(xst_ready, NTILE + 1)
            pe.wait_ge(yev, 2 * NTILE + PRE_YEV)
            for b in range(NB):
                f = NB + b
                y_transposes(f, Y[:, b])
                norm_transposes(f, XN1[b % 2])
                xnt = XNT1[b % 2]
                route(f, xnt, R1, E1, logit_done)
                for q in range(QT):
                    for k in range(ET):
                        mm = nc.tensor.matmul(PRE[0][:, q * P:(q + 1) * P], xnt[:, k, q * P:(q + 1) * P], LA[:, k, :],
                                              start=(k == 0), stop=(k == ET - 1))
                mm.then_inc(mid_done, 1)
                if b:
                    pe.wait_ge(x_final, QT * b)
                for q in range(QT):
                    for k in range(ET):
                        nc.tensor.matmul(PS[:, q], xnt[:, k, q * P:(q + 1) * P], BW[:, k, :], start=(k == 0), stop=False)
                    nc.tensor.matmul(PS[:, q], ON[0:1, :], BB, start=False, stop=True)
                pe.wait_ge(midg_ready, b + 1)
                for q in range(QT):
                    mm = nc.tensor.transpose(AUX[1][:, q * P:(q + 1) * P], MID[:, q, :], ID[:, :])
                mm.then_inc(midt_done, 1)
                pe.wait_ge(midt_ready, b + 1)
                for q in range(QT):
                    nc.tensor.matmul(PS[:, q], MIDT[:, q * P:(q + 1) * P], LB, start=False, stop=True,
                                     skip_group_check=True).then_inc(ffn_done, 1)

        @block.vector
        def _(dve):
            steps = [0]

            def link(ins):
                steps[0] += 1
                ins.then_inc(dve_step, 1)
                dve.wait_ge(dve_step, steps[0])

            def conv(s):
                sl = s % 2
                for pair in range(ET // 2):
                    for m, j in enumerate(range(DC - 2, -1, -1)):
                        for h in range(2):
                            et, sh = 2 * pair + h, DC - 1 - j
                            if m == 0:
                                dve.wait_ge(tap_first, ET * s + et + 1)
                            else:
                                dve.wait_ge(conv_step, 3 * ET * s + 6 * pair + 2 * (m - 1) + h + 1)
                            nc.vector.scalar_tensor_tensor(
                                out=DU[:, sl, et, sh:], in0=PRE[h][:, 0:L - sh], scalar=CH[:, lay(s), et, j:j + 1],
                                in1=DU[:, sl, et, sh:], op0=ALU.mult, op1=ALU.add).then_inc(conv_step, 1)

            def step_size(s):
                dl, sw, r = flat(DEL[:, s % 2]), flat(SW[:, :, :]), flat(Y[:, yslot(s)])
                dve.wait_ge(e_ready, s + 1)
                nc.vector.tensor_scalar(sw, dl, 1.0, None, ALU.add).then_inc(w1_ready, 1)
                dve.wait_ge(w1_ready, s + 1)
                nc.vector.scalar_tensor_tensor(out=dl, in0=sw, scalar=-1.0, in1=dl, op0=ALU.add,
                                               op1=ALU.subtract).then_inc(corr_ready, 1)
                dve.wait_ge(corr_ready, s + 1)
                dve.wait_ge(ln_ready, s + 1)
                link(nc.vector.tensor_tensor(dl, sw, dl, ALU.subtract))
                nc.vector.tensor_tensor(dl, dl, r, ALU.add).then_inc(delta_ready, 1)

            def delta_u(s):
                dve.wait_ge(delta_ready, s + 1)
                dve.wait_ge(seed_ready, s + 1)
                dve.wait_ge(xproj_done, s + 1)
                nc.vector.tensor_tensor(flat(DU[:, s % 2]), flat(DU[:, s % 2]), flat(DEL[:, s % 2]),
                                        ALU.mult).then_inc(du_ready, 1)

            def stats(b, v):
                for q in range(QT):
                    ins = nc.vector.bn_stats(ST[:, q, :], X[:, b * QT + q, :])
                link(ins)
                for q in range(QT):
                    ins = nc.vector.bn_aggr(MV[:, q, :], ST[:, q, :])
                link(ins)
                nc.vector.tensor_scalar(RS[:, :], MV[:, :, 1], EPS, None, ALU.add).then_inc(var_ready, 1)
                dve.wait_ge(std_ready, v + 1)
                link(nc.vector.reciprocal(RS[:, :], RS[:, :]))

            def z_norm(f):
                stats(f % NB, 2 * f)
                nc.vector.scalar_tensor_tensor(out=NBI[:, :], in0=MV[:, :, 0], scalar=-1.0, in1=RS[:, :], op0=ALU.mult,
                                               op1=ALU.mult).then_inc(zn_ready, 1)

            def end_scan(f, y, src, gate):
                b = f % NB
                dve.wait_ge(zs_ready, f + 1)
                nc.vector.tensor_tensor(flat(y), src, flat(ZS[:, :, :]), ALU.mult).then_inc(yg_done, 1)
                for lt in range(QT):
                    dve.wait_ge(yt_done, QT * f + lt + 1)
                    xr = X[:, b * QT + lt, :]
                    nc.vector.scalar_tensor_tensor(out=xr, in0=AUX[lt % 2], scalar=TG[:, gate:gate + 1], in1=xr, op0=ALU.mult,
                                                   op1=ALU.add).then_inc(xacc, 1)
                dve.wait_ge(xacc, QT * (f + 1))

            def norm(f, xn):
                b = f % NB
                stats(b, 2 * f + 1)
                for q in range(QT):
                    nc.vector.tensor_scalar(xn[:, q, :], X[:, b * QT + q, :], MV[:, q, 0:1], RS[:, q:q + 1], ALU.subtract,
                                            ALU.mult).then_inc(xn_ready, 1)

            def rank_of(out, m, n, tri):
                a = T1[:, 0:QT * n * n].rearrange("p (q e f) -> p q e f", q=QT, e=n)
                c = T2[:, 0:QT * n * n].rearrange("p (q e f) -> p q e f", q=QT, e=n)
                other = m.unsqueeze(2).to_broadcast([P, QT, n, n])
                own = m.unsqueeze(3).to_broadcast([P, QT, n, n])
                nc.vector.tensor_tensor(a, other, own, ALU.is_gt)
                link(nc.vector.tensor_tensor(c, other, own, ALU.is_equal))
                link(nc.vector.tensor_tensor(c, c, tri.unsqueeze(1).to_broadcast([P, QT, n, n]), ALU.mult))
                link(nc.vector.tensor_tensor(a, a, c, ALU.add))
                link(nc.vector.reduce_sum(out, a, AX.X))

            def route(b):
                q16 = lambda i: SM[:, i, :].rearrange("p (q e) -> p q e", e=NE)
                dve.wait_ge(sc_ready, b + 1)
                dve.wait_ge(ld_small, 16 * 5)
                biased = q16(0)
                link(nc.vector.tensor_tensor(biased, SC[:, :, :], EB[:, :].unsqueeze(1).to_broadcast([P, QT, NE]), ALU.add))
                pairs = SM[:, 0, :].rearrange("p (n two) -> p n two", two=2)
                mx, mn = SM[:, 1, 0:32], SM[:, 2, 0:32]
                nc.vector.tensor_tensor(mx, pairs[:, :, 0], pairs[:, :, 1], ALU.max)
                link(nc.vector.tensor_tensor(mn, pairs[:, :, 0], pairs[:, :, 1], ALU.min))
                mxp, mnp = [v.rearrange("p (n two) -> p n two", two=2) for v in (mx, mn)]
                top, lo, hi2 = SM[:, 3, 0:16], SM[:, 3, 16:32], SM[:, 3, 32:48]
                nc.vector.tensor_tensor(top, mxp[:, :, 0], mxp[:, :, 1], ALU.max)
                nc.vector.tensor_tensor(lo, mxp[:, :, 0], mxp[:, :, 1], ALU.min)
                link(nc.vector.tensor_tensor(hi2, mnp[:, :, 0], mnp[:, :, 1], ALU.max))
                link(nc.vector.tensor_tensor(lo, lo, hi2, ALU.max))
                gs = SM[:, 4, 0:16]
                link(nc.vector.tensor_tensor(gs, top, lo, ALU.add))
                gr = SM[:, 4, 16:32].rearrange("p (q g) -> p q g", g=NGRP)
                rank_of(gr, gs.rearrange("p (q g) -> p q g", g=NGRP), NGRP, TRI[:, 0:NGRP, 0:NGRP])
                keep, low = SM[:, 4, 32:48], SM[:, 4, 48:64]
                link(nc.vector.tensor_scalar(keep, SM[:, 4, 16:32], float(GKEEP), None, ALU.is_lt))
                link(nc.vector.tensor_scalar(low, keep, BIG, -BIG, ALU.mult, ALU.add))
                masked = q16(5)
                by_group = lambda v: v.unsqueeze(2).to_broadcast([P, QT * NGRP, GSZ])
                g3 = lambda i: SM[:, i, :].rearrange("p (g e) -> p g e", e=GSZ)
                link(nc.vector.tensor_tensor(g3(5), g3(0), by_group(keep), ALU.mult))
                link(nc.vector.tensor_tensor(g3(5), g3(5), by_group(low), ALU.add))
                rk, sel, cw = (v[:, b * QT:(b + 1) * QT, :] for v in (RK, SEL, CW))
                rank_of(rk, masked, NE, TRI[:, :, :])
                link(nc.vector.tensor_scalar(sel, rk, float(TOPK), None, ALU.is_lt))
                link(nc.vector.tensor_tensor(cw, SC[:, :, :], sel, ALU.mult))
                tot = SM[:, 6, 0:QT]
                link(nc.vector.reduce_sum(tot, cw, AX.X))
                link(nc.vector.tensor_scalar(tot, tot, 1e-20, None, ALU.add))
                link(nc.vector.reciprocal(tot, tot))
                link(nc.vector.tensor_scalar(tot, tot, SCALING, TG[:, 2:3], ALU.mult, ALU.mult))
                nc.vector.tensor_tensor(cw, cw, tot.unsqueeze(2).to_broadcast([P, QT, NE]), ALU.mult).then_inc(ranked, 1)

            def slots():
                n2 = NT * NE
                by_e = lambda a: T1[:, a * n2:(a + 1) * n2].rearrange("p (e t) -> p e t", e=NE)
                ct, ci, ex = by_e(0), by_e(1), by_e(2)
                reset = T1[:, 3 * n2:4 * n2]
                count, rows = SM[:, 6, 0:NTILE + 2], SM[:, 5, 0:8]
                link(nc.vector.tensor_tensor_scan(count, ON[:, 0:NTILE + 2], ON[:, 0:NTILE + 2], 0.0, ALU.mult, ALU.add))
                link(nc.vector.tensor_scalar(rows, count[:, 0:8], -1.0, float(TILE), ALU.add, ALU.mult))
                link(nc.vector.memset(reset, 1.0))
                nc.vector.memset(reset.rearrange("p (e t) -> p e t", e=NE)[:, :, 0:1], 0.0)
                dve.wait_ge(counted, 1)
                link(nc.vector.tensor_copy(ct, AUX[1][:, 0:n2].rearrange("p (t e) -> p e t", e=NE)))
                link(nc.vector.tensor_tensor_scan(T1[:, n2:2 * n2], reset, T1[:, 0:n2], 0.0, ALU.mult, ALU.add))
                cnt = ci[:, :, NT - 1]
                full = T2[:, 0:NE * 8].rearrange("p (e m) -> p e m", m=8)
                link(nc.vector.tensor_tensor(full, cnt.unsqueeze(2).to_broadcast([P, NE, 8]),
                                             rows.unsqueeze(1).to_broadcast([P, NE, 8]), ALU.is_gt))
                tiles, upto, first = SM[:, 0, 0:NE], SM[:, 0, NE:2 * NE], SM[:, 0, 2 * NE:3 * NE]
                link(nc.vector.reduce_sum(tiles, full, AX.X))
                link(nc.vector.tensor_tensor_scan(upto, ON[:, 0:NE], tiles, 0.0, ALU.mult, ALU.add))
                link(nc.vector.tensor_tensor(first, upto, tiles, ALU.subtract))
                link(nc.vector.tensor_scalar(first, first, float(TILE), None, ALU.mult))
                link(nc.vector.tensor_tensor(ex, ci, ct, ALU.subtract))
                link(nc.vector.tensor_tensor(ex, ex, first.unsqueeze(2).to_broadcast([P, NE, NT]), ALU.add))
                slot = T2[:, 0:n2].rearrange("p (t e) -> p t e", e=NE)
                link(nc.vector.tensor_tensor(slot, AUX[0][:, 0:n2].rearrange("p (t e) -> p t e", e=NE),
                                             ex.rearrange("p e t -> p t e"), ALU.add))
                is_k = T2[:, n2:2 * n2].rearrange("p (t e) -> p t e", e=NE)
                part = T2[:, 2 * n2:3 * n2].rearrange("p (t e) -> p t e", e=NE)
                slk = SM[:, 1:1 + TOPK, 0:NT]
                for k in range(TOPK):
                    link(nc.vector.tensor_scalar(is_k, RK[:, :, :], float(k), None, ALU.is_equal))
                    link(nc.vector.tensor_tensor(part, is_k, slot, ALU.mult))
                    link(nc.vector.reduce_sum(slk[:, k, :], part, AX.X))
                    link(nc.vector.tensor_tensor(part, is_k, CW[:, :, :], ALU.mult))
                    link(nc.vector.reduce_sum(CWK[:, k, :], part, AX.X))
                nc.vector.tensor_copy(SLU[:, :, :], slk).then_inc(slots_ready, 1)
                ends = T1[:, 0:(NTILE + 2) * NE].rearrange("p (j e) -> p j e", e=NE)
                link(nc.vector.tensor_tensor(ends, upto.unsqueeze(1).to_broadcast([P, NTILE + 2, NE]),
                                             count.unsqueeze(2).to_broadcast([P, NTILE + 2, NE]), ALU.is_lt))
                num = SM[:, 7, 0:NTILE + 2]
                link(nc.vector.reduce_sum(num, ends, AX.X))
                nc.vector.tensor_scalar(TE[:, :], num, float(NE - 1), None, ALU.min).then_inc(slots_ready, 1)

            def mul_b(s, i, c):
                u, h = c // 2, c % 2
                if h == 0:
                    dve.wait_ge(bc_in[u], i * 16 + 16 * (NS // BODY * s + 1))
                dve.wait_ge(w_free, i * (2 * BODY) + (HS * s + c + PRE_W - 3))
                nc.vector.tensor_tensor(W[:, c % 4], DU[:, s % 2, 2 * h:2 * h + 2, :], bcast2(BC[:, u, 0, :]),
                                        ALU.mult).then_inc(mulb_done, 1)

            def scan(s, i, c):
                dve.wait_ge(mulb_done, i * (2 * BODY) + (HS * s + c + 1))
                dve.wait_ge(da_ready, i * (2 * BODY) + (HS * s + c + 1))
                nc.vector.tensor_tensor_scan(flat(W[:, c % 4]), flat(DA[:, c % 2]), flat(W[:, c % 4]), 0.0, ALU.mult,
                                             ALU.add).then_inc(scan_done, 1)

            def mul_c(s, i, c):
                dve.wait_ge(scan_done, i * (2 * BODY) + (HS * s + c + 1 + PRE_SCAN))
                nc.vector.tensor_tensor(W[:, c % 4], W[:, c % 4], bcast2(BC[:, c // 2, 1, :]), ALU.mult).then_inc(mulc_done, 1)

            def add_y(s, i, c):
                dve.wait_ge(mulc_done, i * (2 * BODY) + (HS * s + c + 1 + PRE_MULC))
                dve.wait_ge(w_free, i * (2 * BODY) + (HS * s + c - 1 + PRE_W))
                y = Y[:, yslot(s), 2 * (c % 2):2 * (c % 2) + 2, :]
                nc.vector.tensor_tensor(y, y, W[:, c % 4], ALU.add).then_inc(w_free, 1)

            def scans(s):
                dve.wait_ge(du_ready, s + 1)
                own_readout = s == NB
                with dve.Fori(0, NS // BODY) as i:
                    mul_b(s, i, 0)
                    for c in range(2 * BODY):
                        if c + 1 < 2 * BODY:
                            mul_b(s, i, c + 1)
                        scan(s, i, c)
                        if own_readout and c:
                            mul_c(s, i, c - 1)
                    if own_readout:
                        mul_c(s, i, 2 * BODY - 1)

            def tile_hidden(j, u):
                for it in range(IT):
                    dve.wait_ge(sil_ready, j * 2 + it + 1)
                    nc.vector.tensor_tensor(HT[:, u % 2, it, :], HT[:, u % 2, it, :], PS[:, it, TILE:2 * TILE],
                                            ALU.mult).then_inc(h_ready, 1)

            def shared_hidden(b):
                for it in range(IT):
                    dve.wait_ge(shsil_ready, IT * b + it + 1)
                    nc.vector.tensor_tensor(HB[:, it, :], HB[:, it, :], PS[:, 2 * it + 1], ALU.mult).then_inc(shh_ready, 1)

            def shared_add(b):
                for q in range(QT):
                    dve.wait_ge(shdown_done, QT * b + q + 1)
                    xr = X[:, b * QT + q, :]
                    nc.vector.scalar_tensor_tensor(out=xr, in0=PS[:, q], scalar=TG[:, 2:3], in1=xr, op0=ALU.mult,
                                                   op1=ALU.add).then_inc(shacc, 1)

            dve.sem_inc(scan_done, PRE_SCAN)
            dve.sem_inc(h_ready, PRE_H)
            nc.vector.memset(YSB[:, :, :], 0.0).then_inc(zeroed, 1)
            nc.vector.memset(DA[:, :, :, :], 0.0).then_inc(zeroed, 1)
            dve.wait_ge(masks, 6)
            dve.wait_ge(ld_chan, 32)
            for s in range(2):
                conv(s)
                step_size(s)
                delta_u(s)
            dve.wait_ge(tg_ready, 1)
            dve.wait_ge(ld_x[0], 16)
            z_norm(0)
            for s in range(FIRST_B):
                scans(s)
                if s < NB:
                    dve.wait_ge(w_free, HS * (s + 1) + PRE_W)
                    end_scan(s, Y[:, yslot(s)], flat(PS[:, 0:4]), 0)
                    if s:
                        dve.wait_ge(xn_stored, 16 * s)
                    norm(s, XN)
                    conv(s + 2)
                    route(s)
                    shared_hidden(s)
                    step_size(s + 2)
                    delta_u(s + 2)
                    shared_add(s)
                    if s == NB - 1:
                        slots()
                    else:
                        dve.wait_ge(ld_x[s + 1], 16)
                        z_norm(s + 1)
            for s in range(FIRST_B, STAGES):
                if s + 1 < STAGES:
                    conv(s + 1)
                    step_size(s + 1)
                    delta_u(s + 1)
                dve.wait_ge(du_ready, s + 1)
                dve.wait_ge(w_free, HS * s + PRE_W)
                with dve.Fori(0, NS // BODY) as i:
                    mul_b(s, i, 0)
                    mul_b(s, i, 1)
                    scan(s, i, 0)
                    for u in range(BODY):
                        j = i * BODY + (TPS * (s - FIRST_B) + u)
                        for c in (2 * u + 1, 2 * u + 2):
                            if c >= 2:
                                add_y(s, i, c - 2)
                            if c + 1 < 2 * BODY:
                                mul_b(s, i, c + 1)
                            if c < 2 * BODY:
                                scan(s, i, c)
                            if c == 2 * u + 1:
                                tile_hidden(j, u)
                    add_y(s, i, 2 * BODY - 1)
            for b in range(NB):
                f = NB + b
                for q in range(QT):
                    g = b * QT + q
                    dve.wait_ge(gathered, 16 * TOPK * (g + 1))
                    for k in range(TOPK):
                        if k:
                            dve.wait_ge(combined, TOPK * g + k)
                        nc.vector.scalar_tensor_tensor(out=X[:, g, :], in0=GK[:, g % 2, k, :], scalar=CWK[:, k, g:g + 1],
                                                       in1=X[:, g, :], op0=ALU.mult, op1=ALU.add).then_inc(combined, 1)
                dve.wait_ge(combined, TOPK * QT * (b + 1))
                z_norm(f)
                end_scan(f, Y[:, b], flat(Y[:, b]), 1)
                norm(f, XN1[b % 2])
                v8 = lambda i: SM[:, i, 0:QT * E1].rearrange("p (q e) -> p q e", e=E1)
                over_e = lambda v: v.unsqueeze(2).to_broadcast([P, QT, E1])
                dve.wait_ge(logit_done, b + 1)
                link(nc.vector.tensor_tensor(v8(0), AUX[0][:, 0:QT * E1].rearrange("p (q e) -> p q e", e=E1),
                                             RB[:, :].unsqueeze(1).to_broadcast([P, QT, E1]), ALU.add))
                m = SM[:, 2, 0:QT]
                link(nc.vector.reduce_max(m, v8(0), AX.X))
                nc.vector.tensor_tensor(v8(0), v8(0), over_e(m), ALU.subtract).then_inc(shift_ready, 1)
                dve.wait_ge(exp_ready, b + 1)
                link(nc.vector.reduce_sum(m, v8(1), AX.X))
                link(nc.vector.reciprocal(m, m))
                link(nc.vector.tensor_tensor(v8(1), v8(1), over_e(m), ALU.mult))
                rank_of(v8(3), v8(1), E1, TRI[:, 0:E1, 0:E1])
                link(nc.vector.tensor_scalar(v8(3), v8(3), 2.0, None, ALU.is_lt))
                link(nc.vector.tensor_tensor(v8(3), v8(3), v8(1), ALU.mult))
                link(nc.vector.reduce_sum(m, v8(3), AX.X))
                link(nc.vector.reciprocal(m, m))
                link(nc.vector.tensor_scalar(m, m, LSCALE, None, ALU.mult))
                link(nc.vector.tensor_tensor(v8(3), v8(3), over_e(m), ALU.mult))
                dve.wait_ge(mid_done, b + 1)
                if b:
                    dve.wait_ge(midt_done, b)
                nc.vector.tensor_tensor(
                    MID.rearrange("p q (e r) -> p (q e) r", r=RANK1), PRE[0].rearrange("p (n r) -> p n r", r=RANK1),
                    SM[:, 3, 0:QT * E1].unsqueeze(2).to_broadcast([P, QT * E1, RANK1]), ALU.mult).then_inc(midg_ready, 1)
                for q in range(QT):
                    dve.wait_ge(ffn_done, QT * b + q + 1)
                    xr = X[:, b * QT + q, :]
                    nc.vector.scalar_tensor_tensor(out=xr, in0=PS[:, q], scalar=TG[:, 3:4], in1=xr, op0=ALU.mult,
                                                   op1=ALU.add).then_inc(x_final, 1)


def _layouts(a):
    import numpy as np

    f = {k: np.asarray(v) for k, v in a.items()}
    c = np.ascontiguousarray
    out = {"x": c(f["x"]), "ctxT": c(f["ctx_1024"].reshape(NB * L, DM).T),
           "gates": c(np.concatenate([f["g_xattn"], f["g_ffn"]])[None, :])}
    order = list(range(DR, DR + 2 * NS)) + list(range(DR))
    for layer in range(2):
        g = lambda n: f[f"L{layer}_xattn_{n}"]
        out[f"in_wT{layer}"] = c(g("in_proj_w").T)
        out[f"chan{layer}"] = c(np.concatenate(
            [g("conv_w").reshape(D, DC), g("conv_b")[:, None], g("dt_proj_b")[:, None], g("D")[:, None], g("A_log")], axis=1))
        out[f"xprojT{layer}"] = c(g("x_proj_w")[order].T)
        out[f"dtT{layer}"] = c(g("dt_proj_w").T)

    def packed(gate, up, down):
        n = gate.shape[0]
        rows = [w.transpose(0, 2, 1).reshape(n, ET, P, INNER).transpose(0, 2, 1, 3).reshape(n, P, WGU) for w in (gate, up)]
        rows.append(down.transpose(0, 2, 1).reshape(n, IT, P, D).transpose(0, 2, 1, 3).reshape(n, P, IT * D))
        return np.concatenate(rows, axis=2)

    out["moe_w"] = c(np.concatenate([
        packed(f["L0_ffn_gate_proj"], f["L0_ffn_up_proj"], f["L0_ffn_down_proj"]),
        packed(f["L0_ffn_shared_gate"][None], f["L0_ffn_shared_up"][None], f["L0_ffn_shared_down"][None])]))
    out["gwT"] = c(f["L0_ffn_gate_weight"].T)
    out["ebias"] = c(f["L0_ffn_expert_bias"][None, :])
    out["base_wT"] = c(f["L1_ffn_base_w"].T)
    out["base_b"] = c(f["L1_ffn_base_b"][None, :])
    out["r1T"] = c(f["L1_ffn_router_w"].T)
    out["rb"] = c(f["L1_ffn_router_b"][None, :])
    out["loraA"] = c(f["L1_ffn_lora_A"].transpose(1, 0, 2).reshape(D, E1 * RANK1))
    out["loraB"] = c(f["L1_ffn_lora_B"].reshape(E1 * RANK1, D))
    return out


def kernel(**inputs):
    import concourse.bacc as _bacc
    from concourse import mybir as _mybir
    from concourse.bass_utils import run_bass_kernel_spmd as _run

    nc = _bacc.Bacc("TRN2", target_bir_lowering=False, num_devices=1)
    arrays, t = {}, {}
    for name, a in _layouts(inputs).items():
        arrays[f"in_{name}"] = a
        t[name] = nc.dram_tensor(f"in_{name}", a.shape, _mybir.dt.from_np(a.dtype), kind="ExternalInput").ap()
    t["out"] = nc.dram_tensor("out_x", (NB, L, D), F32, kind="ExternalOutput").ap()
    build(nc, t)
    return _run(nc, [arrays], core_ids=[0]).results[0]["out_x"]
```

```python
from contextlib import ExitStack

import concourse.bass as bass
from concourse import mybir

F32 = mybir.dt.float32
I32 = mybir.dt.int32
U32 = mybir.dt.uint32
ALU = mybir.AluOpType
ACT = mybir.ActivationFunctionType
AX = mybir.AxisListType

P = 128
NB, L, D = 4, 512, 512
DM, NS, DR, DC = 256, 16, 16, 4
ET, QT, KC = D // P, L // P, DM // P
NT = NB * QT
NE, TOPK, NGRP, GKEEP, SCALING = 16, 4, 4, 2, 2.5
GSZ = NE // NGRP
INNER = 256
IT = INNER // P
TILE = 256
RT = TILE // P
NTILE = NB * L * TOPK // TILE + NE
WGU = ET * INNER
WPK = 2 * WGU + IT * D
E1, RANK1, LSCALE = 8, 16, 2.0
EPS = 1e-5
CHC = DC + 3 + NS
C_CB, C_DB, C_D, C_A = DC, DC + 1, DC + 2, DC + 3
STAGES = 2 * NB
HS = 2 * NS
BODY = 4
TURNS = NS // BODY
HPT = 2 * BODY
FIRST_B = NB + 1
TPS = NTILE // (STAGES - FIRST_B)
BIG = 3.0e38

PRE_SCAN, PRE_MULC, PRE_W, PRE_H, PRE_Y, PRE_YEV, PRE_YS = 4, 8, 4, 2, 4, 2, 16


def build(nc, t):
    with ExitStack() as ctx:
        def sb(name, shape, dt=F32):
            return ctx.enter_context(nc.sbuf_tensor(name, shape, dt))

        def sem(name):
            return ctx.enter_context(nc.semaphore(name))

        X = sb("x_res", [P, NT, D])
        Y = sb("y_scan", [P, NB, ET, L])
        DEL = sb("delta", [P, 2, ET, L])
        DU = sb("du", [P, 2, ET, L])
        DA = sb("decay", [P, 2, 2, L])
        W = sb("state", [P, 4, 2, L])
        BC = sb("bc_rows", [P, 4, 2, L])
        SW = sb("softplus_tmp", [P, ET, L])
        ZS = sb("z_gate", [P, QT, D])
        YSB = sb("expert_out", [P, RT, D])
        HB = sb("hidden", [P, 2, 2 * TILE])
        MW = sb("expert_w", [P, 2, WPK])
        CTX = sb("ctx_t", [P, KC, L])
        INW = sb("in_w", [P, KC, D])
        XPW = sb("xproj_w", [P, 2, ET, DR + 2 * NS])
        DTW = sb("dt_w", [DR + 2 * NS, D])
        CH = sb("chan", [P, 2, ET, CHC])
        AN = sb("neg_a", [P, 2, ET, NS])
        XDBL = sb("x_dbl", [DR + 2 * NS, L])
        ID = sb("ident", [P, P])
        US = sb("upper", [P, P])
        ON = sb("ones", [P, P])
        TRI = sb("tri", [P, NE, NE])
        GW = sb("router_w", [P, ET, NE])
        EB = sb("expert_bias", [P, NE])
        TG = sb("tanh_gates", [P, 4])
        R1 = sb("router1_w", [P, ET, E1])
        RB = sb("router1_b", [P, E1])
        MV = sb("mean_var", [P, QT, 2])
        RS = sb("rstd", [P, QT])
        NBI = sb("neg_mean_rstd", [P, QT])
        SC = sb("scores", [P, QT, NE])
        RK = sb("rank", [P, NT, NE])
        CW = sb("route_w", [P, NT, NE])
        SEL = sb("selected", [P, NT, NE])
        SM = sb("small", [P, 8, QT * NE])
        SLU = sb("slots", [P, TOPK, NT], U32)
        CWK = sb("slot_w", [P, TOPK, NT])
        TE = sb("tile_expert", [P, NTILE + 1], I32)

        def flat(ap):
            return ap.rearrange("p a b -> p (a b)")

        ST = SM[:, 7, 0:QT * 6].rearrange("p (q s) -> p q s", s=6)
        XN, XNT = Y[:, 2], Y[:, 3]
        XS = ZS[:, 0:RT]
        XST = flat(ZS[:, RT:QT]).rearrange("p (k r) -> p k r", k=ET)
        HT = HB[:, :, :].rearrange("p s (i r) -> p s i r", i=IT)
        T1, T2 = flat(ZS[:, 0:2]), flat(ZS[:, 2:4])
        GK = [W[:, 0:2].rearrange("p a b n -> p (a b) n"), W[:, 2:4].rearrange("p a b n -> p (a b) n"),
              DA[:, :, :, :].rearrange("p a b n -> p (a b) n"),
              MW[:, 1, 0:QT * D].rearrange("p (q n) -> p q n", q=QT)]
        BW = MW[:, 0, 0:ET * D].rearrange("p (k n) -> p k n", k=ET)
        LA = MW[:, 0, ET * D:ET * D + ET * P].rearrange("p (k n) -> p k n", k=ET)
        LB = MW[:, 0, ET * D + ET * P:ET * D + ET * P + D]
        BB = SW[0:1, 0, :]
        DAS = [DA[:, 0], DA[:, 1]] + [
            MW[:, 1, a * 2 * L:(a + 1) * 2 * L].rearrange("p (m n) -> p m n", m=2) for a in range(2)]
        STAGED = [XN, MW[:, 1, 0:QT * D].rearrange("p (q n) -> p q n", q=QT)]
        XN1, XNT1 = [DEL[:, 0], DEL[:, 1]], [DU[:, 0], DU[:, 1]]
        MID, MIDT = BC[:, 0, 0:1].rearrange("p a (q n) -> p (a q) n", q=QT), BC[:, 1, 0]

        PS = ctx.enter_context(nc.psum_tensor("banks", [P, 8, 512], F32))
        PRE = [PS[:, 4], PS[:, 5]]
        AUX = [PS[:, 6], PS[:, 7]]
        XT = flat(PS[:, 6:8]).rearrange("p (k r) -> p k r", k=ET)

        bc_d = nc.dram_tensor("bc_d", (STAGES, 2 * NS, L), F32, kind="Internal").ap()
        xn_d = nc.dram_tensor("xn_d", (NB * L, D), F32, kind="Internal").ap()
        xs_d = nc.dram_tensor("xs_d", ((NTILE + 1) * TILE, D), F32, kind="Internal").ap()
        ys_d = nc.dram_tensor("ys_d", (NTILE * TILE, D), F32, kind="Internal").ap()
        xs_t = xs_d.rearrange("(j r p) n -> j p r n", p=P, r=RT)
        ys_t = ys_d.rearrange("(j r p) n -> j p r n", p=P, r=RT)
        xn_t = xn_d.rearrange("(b q p) n -> b p q n", p=P, q=QT)
        x_t = t["x"].rearrange("b (q p) n -> b p q n", p=P)
        out_t = t["out"].rearrange("b (q p) n -> b p q n", p=P)

        ld_chan, ld_proj, ld_small, ld_shared = sem("ld_chan"), sem("ld_proj"), sem("ld_small"), sem("ld_shared")
        ld_x = [sem(f"ld_x{b}") for b in range(NB)]
        ld_inw, ld_dtw, ld_ffn1 = sem("ld_inw"), sem("ld_dtw"), sem("ld_ffn1")
        ctx_in, bc_stored = sem("ctx_in"), sem("bc_stored")
        bc_in = [sem(f"bc_in{u}") for u in range(BODY)]
        xn_stored, zero_filled = sem("xn_stored"), sem("zero_filled")
        staged = [sem(f"staged{i}") for i in range(2)]
        scattered = [sem(f"scattered{i}") for i in range(2)]
        tw_in = [sem(f"tw_in{i}") for i in range(2)]
        xs_in, ys_stored, out_stored = sem("xs_in"), sem("ys_stored"), sem("out_stored")
        gathered = [sem(f"gathered{q}") for q in range(QT)]
        masks, zeroed, a_ready, tg_ready, counts = sem("masks"), sem("zeroed"), sem("a_ready"), sem("tg_ready"), sem("counts")
        inproj_done, tap_first, conv_step, u_ready = sem("inproj_done"), sem("tap_first"), sem("conv_step"), sem("u_ready")
        xproj_done, xdbl_ready, dt_done, dt_read = sem("xproj_done"), sem("xdbl_ready"), sem("dt_done"), sem("dt_read")
        e_ready, w1_ready, corr_ready, ln_ready = sem("e_ready"), sem("w1_ready"), sem("corr_ready"), sem("ln_ready")
        relu_added = sem("relu_added")
        delta_ready, seed_ready, du_ready = sem("delta_ready"), sem("seed_ready"), sem("du_ready")
        da_ready, mulb_done, scan_done = sem("da_ready"), sem("mulb_done"), sem("scan_done")
        mulc_done, w_free, seeded, y4_ready = sem("mulc_done"), sem("w_free"), sem("seeded"), sem("y4_ready")
        var_ready, std_step, std_ready, zn_ready, zs_ready = sem("var_ready"), sem("std_step"), sem("std_ready"), sem("zn_ready"), sem("zs_ready")
        yg_done, yt_done, xacc = sem("yg_done"), sem("yt_done"), sem("xacc")
        xn_ready, xnt_done, xnt_ready = sem("xn_ready"), sem("xnt_done"), sem("xnt_ready")
        router_done, sc_ready, ranked = sem("router_done"), sem("sc_ready"), sem("ranked")
        counted, counts_read, slots_ready = sem("counted"), sem("counts_read"), sem("slots_ready")
        shgu_done, shsil_ready, shh_ready, shdown_done, shacc = (
            sem("shgu_done"), sem("shsil_ready"), sem("shh_ready"), sem("shdown_done"), sem("shacc"))
        xt_done, xst_ready, gu_done, sil_ready, h_ready = (
            sem("xt_done"), sem("xst_ready"), sem("gu_done"), sem("sil_ready"), sem("h_ready"))
        hg_ready, y_done, yev, dve_step = sem("hg_ready"), sem("y_done"), sem("yev"), sem("dve_step")
        combined, logit_done, exp_ready, shift_ready = sem("combined"), sem("logit_done"), sem("exp_ready"), sem("shift_ready")
        mid_done, midg_ready, midt_done, midt_ready, ffn_done, x_final = (
            sem("mid_done"), sem("midg_ready"), sem("midt_done"), sem("midt_ready"), sem("ffn_done"), sem("x_final"))

        def lay(s):
            return s // NB

        def yslot(s):
            return s % 2 if s < NB else s - NB

        def shared_banks(b, it):
            return PRE if b == NB - 1 and it == 0 else AUX

        def shared_out_bank(b, q):
            return (PRE + AUX)[q] if b == NB - 1 else AUX[q % 2]

        def da_slots(s):
            return 4 if s < NB else 2

        def bcast2(row):
            return row.unsqueeze(1).to_broadcast([P, 2, L])

        block = ctx.enter_context(nc.Block())

        @block.sync
        def _(sp):
            def load_ctx(s):
                if s > 0:
                    sp.wait_ge(inproj_done, ET * s)
                b = s % NB
                sp.dma_start(CTX[:, :, :], t["ctxT"].rearrange("(k p) n -> p k n", p=P)[:, :, b * L:(b + 1) * L]
                             ).then_inc(ctx_in, 16)

            def load_layer_in(layer):
                if layer:
                    sp.wait_ge(inproj_done, ET * NB)
                sp.dma_start(INW[:, :, :], t[f"in_wT{layer}"].rearrange("(k p) n -> p k n", p=P)).then_inc(ld_inw, 16)

            def load_layer_dt(layer):
                if layer:
                    sp.wait_ge(dt_done, ET * NB)
                sp.dma_start(DTW[2 * NS:, :], t[f"dtT{layer}"]).then_inc(ld_dtw, 16)

            def load_bc(s, i, u):
                n = i * BODY + u
                sp.wait_ge(mulc_done, i * (2 * BODY) + (HS * s + 2 * u + PRE_MULC - 2 * BODY + 2))
                src = bc_d[s].rearrange("(c n) l -> n c l", c=2)[bass.ds(n, 1), :, :]
                sp.dma_start(BC[:, u, :, :], src.rearrange("a c l -> (a c) l").partition_broadcast(P)
                             ).then_inc(bc_in[u], 16)

            def scan_loads(s, turn):
                for u in range(BODY):
                    load_bc(s, turn, u)

            def zero_fill(c):
                sp.dma_start(xs_rows[:, bass.ds(c * per, per), :],
                             YSB[:, 0:1, :].to_broadcast([P, per, D])).then_inc(zero_filled, 16)

            def load_tile_w(j, slot):
                sp.wait_ge(y_done, j * 2 + (PRE_Y - 2))
                e = sp.value_load(TE[0:1, bass.ds(j, 1)] if not isinstance(j, int) else TE[0:1, j:j + 1],
                                  min_val=0, max_val=NE - 1)
                sp.dma_start(MW[:, slot, :], t["moe_w"][bass.ds(e, 1), :, :].rearrange("a p n -> p (a n)")
                             ).then_inc(tw_in[slot], 16)

            def load_tile_x(j):
                sp.wait_ge(xt_done, j)
                src = xs_t[bass.ds(j, 1)] if not isinstance(j, int) else xs_t[j:j + 1]
                sp.dma_start(XS, src.rearrange("a p r n -> p (a r) n")).then_inc(xs_in, 16)

            def store_tile(j):
                sp.wait_ge(yev, j * 2 + (2 + PRE_YEV))
                dst = ys_t[bass.ds(j, 1)]
                sp.dma_start(dst.rearrange("a p r n -> p (a r) n"), YSB[:, :, :]).then_inc(ys_stored, 16)

            rows = (NTILE + 1) * TILE // P
            per = rows // 14
            xs_rows = xs_d.rearrange("(c p) n -> p c n", p=P)

            load_layer_in(0)
            load_ctx(0)
            load_layer_dt(0)
            for layer in range(2):
                sp.dma_start(CH[:, layer], t[f"chan{layer}"].rearrange("(e p) n -> p e n", p=P)).then_inc(ld_chan, 16)
                sp.dma_start(XPW[:, layer], t[f"xprojT{layer}"].rearrange("(e p) n -> p e n", p=P)).then_inc(ld_proj, 16)
            sp.dma_start(TG[:, :], t["gates"][0, :].partition_broadcast(P)).then_inc(ld_small, 16)
            sp.dma_start(GW[:, :, :], t["gwT"].rearrange("(k p) n -> p k n", p=P)).then_inc(ld_small, 16)
            sp.dma_start(EB[:, :], t["ebias"][0, :].partition_broadcast(P)).then_inc(ld_small, 16)
            sp.dma_start(R1[:, :, :], t["r1T"].rearrange("(k p) n -> p k n", p=P)).then_inc(ld_small, 16)
            sp.dma_start(RB[:, :], t["rb"][0, :].partition_broadcast(P)).then_inc(ld_small, 16)
            for b in range(NB):
                sp.dma_start(X[:, b * QT:(b + 1) * QT, :], x_t[b]).then_inc(ld_x[b], 16)
            sp.dma_start(MW[:, 0, :], t["moe_w"][NE]).then_inc(ld_shared, 16)
            load_ctx(1)
            sp.wait_ge(zeroed, 5)
            for s in range(FIRST_B):
                if s == NB - 1:
                    load_layer_dt(1)
                sp.wait_ge(bc_stored, 16 * (s + 1))
                scan_loads(s, 0)
                load_ctx(s + 2)
                if s == NB - 2:
                    load_layer_in(1)
                if s < NB:
                    zero_fill(4 * s)
                with sp.Fori(1, TURNS - 1) as i:
                    scan_loads(s, i)
                    if s < NB - 1:
                        zero_fill(i + 4 * s)
                if s < NB:
                    scan_loads(s, TURNS - 1)
                    zero_fill(4 * s + (3 if s < NB - 1 else 1))
                if s:
                    sp.wait_ge(xn_ready, QT * s)
                    sp.dma_start(xn_t[s - 1], XN).then_inc(xn_stored, 16)
            sp.wait_ge(xnt_done, QT * NB)
            sp.wait_ge(xn_stored, 16 * NB)
            for b in range(NB):
                if b >= 2:
                    sp.wait_ge(scattered[b % 2], 16 * QT * TOPK)
                sp.dma_start(STAGED[b % 2], xn_t[b]).then_inc(staged[b % 2], 16)
                if b == 1:
                    scan_loads(NB, TURNS - 1)
            sp.wait_ge(slots_ready, 2)
            sp.wait_ge(shdown_done, QT * NB)
            load_tile_w(0, 0)
            for i in range(2):
                sp.wait_ge(scattered[i], 16 * 2 * QT * TOPK)
            load_tile_x(0)
            def tile_turn(s, i, last):
                for u in range(BODY):
                    j = i * BODY + (TPS * (s - FIRST_B) + u)
                    load_tile_x(j + 1)
                    load_tile_w(j + 1, (u + 1) % 2)
                    if u:
                        store_tile(j - 1)
                    if u == 0:
                        load_bc(s, i, BODY - 1)
                    elif not last:
                        load_bc(s, i + 1, u - 1)
                store_tile(i * BODY + (TPS * (s - FIRST_B) + BODY - 1))

            for s in range(FIRST_B, STAGES):
                sp.wait_ge(bc_stored, 16 * (s + 1))
                for u in range(BODY - 1):
                    load_bc(s, 0, u)
                with sp.Fori(0, TURNS - 1) as i:
                    tile_turn(s, i, False)
                if s + 2 < STAGES:
                    load_ctx(s + 2)
                tile_turn(s, TURNS - 1, True)
            for i in range(2):
                sp.wait_ge(tw_in[i], 16 * (NTILE // 2 + 1 - i))
            sp.dma_start(BW, t["base_wT"].rearrange("(k p) n -> p k n", p=P)).then_inc(ld_ffn1, 16)
            sp.dma_start(LA, t["loraA"].rearrange("(k p) n -> p k n", p=P)).then_inc(ld_ffn1, 16)
            sp.dma_start(LB, t["loraB"]).then_inc(ld_ffn1, 16)
            sp.wait_ge(du_ready, STAGES)
            sp.dma_start(BB, t["base_b"]).then_inc(ld_ffn1, 16)
            for b in range(NB):
                sp.wait_ge(x_final, QT * (b + 1))
                sp.dma_start(out_t[b], X[:, b * QT:(b + 1) * QT, :]).then_inc(out_stored, 16)
            sp.wait_ge(out_stored, 16 * NB)

        @block.gpsimd
        def _(pool):
            pool.sem_inc(mulc_done, PRE_MULC)
            nc.gpsimd.memset(ID[:, :], 0.0).then_inc(masks, 1)
            nc.gpsimd.memset(ON[:, :], 1.0).then_inc(masks, 1)
            nc.gpsimd.memset(TRI[:, :, :], 1.0).then_inc(masks, 1)
            pool.wait_ge(masks, 3)
            nc.gpsimd.affine_select(out=ID[:, :], in_=ID[:, :], compare_op=ALU.not_equal, fill=1.0, base=0,
                                    pattern=[[-1, P]], channel_multiplier=1).then_inc(masks, 1)
            nc.gpsimd.affine_select(out=US[:, :], in_=ON[:, :], compare_op=ALU.is_gt, fill=0.0, base=0,
                                    pattern=[[1, P]], channel_multiplier=-1).then_inc(masks, 1)
            nc.gpsimd.affine_select(out=TRI[:, :, :], in_=TRI[:, :, :], compare_op=ALU.is_gt, fill=0.0, base=0,
                                    pattern=[[1, NE], [-1, NE]], channel_multiplier=0).then_inc(masks, 1)

            def mul_c(s, i, c):
                pool.wait_ge(scan_done, i * HPT + (HS * s + c + 1 + PRE_SCAN))
                nc.gpsimd.tensor_tensor(W[:, c % 4], W[:, c % 4], bcast2(BC[:, c // 2, 1, :]), ALU.mult).then_inc(mulc_done, 1)

            def step_round(s):
                dl, sw = flat(DEL[:, s % 2]), flat(SW[:, :, :])
                pool.wait_ge(e_ready, s + 1)
                pool.wait_ge(delta_ready, s)
                nc.gpsimd.tensor_scalar(sw, dl, 1.0, 1.0, ALU.mult, ALU.add).then_inc(w1_ready, 1)
                pool.wait_ge(w1_ready, 2 * s)
                nc.gpsimd.tensor_scalar(sw, sw, 1.0, -1.0, ALU.mult, ALU.add).then_inc(w1_ready, 1)
                pool.wait_ge(w1_ready, 2 * s + 1)
                nc.gpsimd.tensor_tensor(sw, dl, sw, ALU.subtract).then_inc(corr_ready, 1)

            def step_relu(s):
                sw = flat(SW[:, :, :])
                pool.wait_ge(corr_ready, s + 1)
                pool.wait_ge(dt_read, ET * (s + 1))
                nc.gpsimd.tensor_tensor(sw, sw, flat(Y[:, yslot(s)]), ALU.add).then_inc(relu_added, 1)

            def step_sum(s):
                dl = flat(DEL[:, s % 2])
                pool.wait_ge(relu_added, s + 1)
                pool.wait_ge(ln_ready, s + 1)
                nc.gpsimd.tensor_tensor(dl, dl, flat(SW[:, :, :]), ALU.add).then_inc(delta_ready, 1)

            for s in range(FIRST_B):
                turn = TURNS - 1 if s < NB else 1
                with pool.Fori(0, turn) as i:
                    for c in range(HPT):
                        mul_c(s, i, c)
                for c in range(HPT):
                    mul_c(s, turn, c)
                    if c == 3:
                        step_round(s + 1)
                    if c == 5:
                        step_relu(s + 1)
                        step_sum(s + 1)
            pool.wait_ge(slots_ready, 2)
            pool.wait_ge(zero_filled, 16 * 14)
            for b in range(NB):
                pool.wait_ge(staged[b % 2], 16 * (b // 2 + 1))
                for q in range(QT):
                    for k in range(TOPK):
                        nc.gpsimd.indirect_dma_start(
                            out=xs_d, out_offset=bass.IndirectOffsetOnAxis(ap=SLU[:, k, b * QT + q:b * QT + q + 1], axis=0),
                            in_=STAGED[b % 2][:, q, :], in_offset=None).then_inc(scattered[b % 2], 16)
            for s in range(FIRST_B, STAGES):
                with pool.Fori(0, TURNS - 1) as i:
                    for c in range(HPT):
                        mul_c(s, i, c)
                for c in range(HPT):
                    mul_c(s, TURNS - 1, c)
                    if s + 1 < STAGES:
                        if c == 3:
                            step_round(s + 1)
                        if c == 4:
                            step_relu(s + 1)
                        if c == 5:
                            step_sum(s + 1)
            pool.wait_ge(w_free, HS * STAGES + PRE_W)
            pool.wait_ge(ys_stored, 16 * NTILE + PRE_YS)
            for g in range(NT):
                b, q = g // QT, g % QT
                if b:
                    pool.wait_ge(combined, TOPK * QT * (b - 1) + (TOPK - 1) * QT + q + 1)
                for k in range(TOPK):
                    nc.gpsimd.indirect_dma_start(
                        out=GK[q][:, k, :], out_offset=None, in_=ys_d,
                        in_offset=bass.IndirectOffsetOnAxis(ap=SLU[:, k, g:g + 1], axis=0)).then_inc(gathered[q], 16)

        @block.scalar
        def _(act):
            def conv_tap(s, pair):
                sl = s % 2
                if s >= 2:
                    act.wait_ge(scan_done, HS * (s - 1) + PRE_SCAN)
                for et in (2 * pair, 2 * pair + 1):
                    act.wait_ge(inproj_done, ET * s + et + 1)
                    nc.scalar.activation(DU[:, sl, et, :], PRE[et % 2], ACT.Identity, bias=CH[:, lay(s), et, C_CB:C_CB + 1],
                                         scale=CH[:, lay(s), et, DC - 1:DC]).then_inc(tap_first, 1)

            def conv_silu(s):
                act.wait_ge(conv_step, 3 * ET * (s + 1))
                nc.scalar.activation(flat(DU[:, s % 2]), flat(DU[:, s % 2]), ACT.Silu).then_inc(u_ready, 1)

            def x_dbl(s):
                act.wait_ge(xproj_done, s + 1)
                if s:
                    act.wait_ge(bc_stored, 16 * s)
                    act.wait_ge(dt_done, ET * s)
                nc.scalar.activation(XDBL[:, :], PRE[0][0:DR + 2 * NS, :], ACT.Copy).then_inc(xdbl_ready, 1)
                act.wait_ge(xdbl_ready, s + 1)
                act.dma_start(bc_d[s], XDBL[0:2 * NS, :]).then_inc(bc_stored, 16)

            def step_abs(s, pair):
                if 2 <= s < NB + 2:
                    act.wait_ge(yt_done, QT * (s - 1))
                elif s == NB + 2:
                    act.wait_ge(scattered[0], 16 * 2 * QT * TOPK)
                elif s == NB + 3:
                    act.wait_ge(shgu_done, IT * NB)
                for et in (2 * pair, 2 * pair + 1):
                    act.wait_ge(dt_done, ET * s + et + 1)
                    bias = CH[:, lay(s), et, C_DB:C_DB + 1]
                    nc.scalar.activation(DEL[:, s % 2, et, :], PRE[et % 2], ACT.Abs, bias=bias)
                    nc.scalar.activation(Y[:, yslot(s), et, :], PRE[et % 2], ACT.Relu, bias=bias).then_inc(dt_read, 1)

            def step_exp(s):
                act.wait_ge(dt_read, ET * (s + 1))
                nc.scalar.activation(flat(DEL[:, s % 2]), flat(DEL[:, s % 2]), ACT.Exp, scale=-1.0).then_inc(e_ready, 1)

            def step_log(s):
                act.wait_ge(corr_ready, s + 1)
                nc.scalar.activation(flat(DEL[:, s % 2]), flat(DEL[:, s % 2]), ACT.Ln, bias=1.0).then_inc(ln_ready, 1)

            def seed(s):
                act.wait_ge(relu_added, s + 1)
                act.wait_ge(u_ready, s + 1)
                for et in range(ET):
                    ins = nc.scalar.activation(Y[:, yslot(s), et, :], DU[:, s % 2, et, :], ACT.Identity,
                                               scale=CH[:, lay(s), et, C_D:C_D + 1])
                ins.then_inc(seed_ready, 1)

            def z_gate(f):
                act.wait_ge(zn_ready, 2 * f + 1)
                b = f % NB
                for q in range(QT):
                    ins = nc.scalar.activation(ZS[:, q, :], X[:, b * QT + q, :], ACT.Silu, bias=NBI[:, q:q + 1],
                                               scale=RS[:, q:q + 1])
                ins.then_inc(zs_ready, 1)

            def norm(f, xn):
                act.wait_ge(zn_ready, 2 * f + 2)
                if 0 < f < NB:
                    act.wait_ge(xn_stored, 16 * f)
                for q in range(QT):
                    nc.scalar.activation(xn[:, q, :], X[:, (f % NB) * QT + q, :], ACT.Identity, bias=NBI[:, q:q + 1],
                                         scale=RS[:, q:q + 1]).then_inc(xn_ready, 1)

            def rstd(v):
                rstd_log(v)
                rstd_exp(v)

            def rstd_log(v):
                act.wait_ge(var_ready, v + 1)
                nc.scalar.activation(RS[:, :], RS[:, :], ACT.Ln).then_inc(std_step, 1)

            def rstd_exp(v):
                act.wait_ge(std_step, v + 1)
                nc.scalar.activation(RS[:, :], RS[:, :], ACT.Exp, scale=-0.5).then_inc(std_ready, 1)

            def decay(s, i, c):
                n = da_slots(s)
                act.wait_ge(scan_done, i * HPT + (HS * s + c + 1 + PRE_SCAN - n))
                for m in range(2):
                    et = 2 * (c % 2) + m
                    ins = nc.scalar.activation(DAS[c % n][:, m, 1:], DEL[:, s % 2, et, 1:], ACT.Exp,
                                               scale=AN[:, lay(s), et, bass.ds(i * BODY + c // 2, 1)])
                ins.then_inc(da_ready, 1)

            def norm_t(f, xnt, ks):
                for k in ks:
                    act.wait_ge(xnt_done, ET * f + k + 1)
                    if 0 < f < NB:
                        act.wait_ge(shgu_done, IT * f)
                    nc.scalar.activation(xnt[:, k, :], AUX[k % 2], ACT.Copy).then_inc(xnt_ready, 1)

            def route_exp(f):
                act.wait_ge(router_done, f + 1)
                nc.scalar.activation(SC[:, :, :], AUX[0][:, 0:QT * NE].rearrange("p (q e) -> p q e", e=NE), ACT.Exp,
                                     scale=-1.0).then_inc(sc_ready, 1)

            def shared_tanh(b, it):
                act.wait_ge(shgu_done, IT * b + it + 1)
                if b:
                    act.wait_ge(shdown_done, QT * b)
                nc.scalar.activation(HB[:, it, :], shared_banks(b, it)[0], ACT.Tanh, scale=0.5).then_inc(shsil_ready, 1)

            def tile_rows(j):
                act.wait_ge(xt_done, j + 1)
                if not isinstance(j, int) or j:
                    act.wait_ge(gu_done, j * 2)
                nc.scalar.activation(flat(XST), flat(XT), ACT.Copy).then_inc(xst_ready, 1)

            def tile_tanh(j, u, it):
                act.wait_ge(gu_done, j * 2 + it + 1)
                act.wait_ge(y_done, j * 2 + (PRE_Y - 2))
                nc.scalar.activation(HT[:, u % 2, it, :], PS[:, it, 0:TILE], ACT.Tanh, scale=0.5).then_inc(sil_ready, 1)

            def tile_out(j):
                act.wait_ge(ys_stored, j * 16 + PRE_YS)
                for r in range(RT):
                    act.wait_ge(y_done, j * 2 + (r + 1 + PRE_Y))
                    nc.scalar.activation(YSB[:, r, :], PS[:, 2 + r], ACT.Copy).then_inc(yev, 1)

            act.wait_ge(ld_small, 16 * 5)
            nc.scalar.activation(TG[:, :], TG[:, :], ACT.Tanh).then_inc(tg_ready, 1)
            act.wait_ge(tg_ready, 1)
            nc.scalar.activation(TG[:, 2:3], TG[:, 2:3], ACT.Copy, scale=0.5).then_inc(tg_ready, 1)
            act.wait_ge(ld_chan, 32)
            for layer in range(2):
                nc.scalar.activation(AN[:, layer], CH[:, layer, :, C_A:C_A + NS], ACT.Exp).then_inc(a_ready, 1)
            act.wait_ge(a_ready, 2)
            nc.scalar.activation(AN[:, :, :, :], AN[:, :, :, :], ACT.Copy, scale=-1.0).then_inc(a_ready, 1)
            act.wait_ge(a_ready, 3)
            act.wait_ge(zeroed, 5)
            act.sem_inc(yev, PRE_YEV)
            act.sem_inc(ys_stored, PRE_YS)

            for pair in range(2):
                conv_tap(0, pair)
            conv_silu(0)
            x_dbl(0)
            for pair in range(2):
                step_abs(0, pair)
            step_exp(0)
            step_log(0)
            seed(0)
            for s in range(FIRST_B):
                f, p, g = s - 1, s + 1, s - 2
                act.wait_ge(delta_ready, s + 1)
                for c in range(HPT):
                    decay(s, 0, c)
                    if c == 1:
                        conv_tap(p, 0)
                        if g >= 0:
                            shared_tanh(g, 1)
                    if c == 6:
                        conv_tap(p, 1)
                conv_silu(p)
                if s < NB:
                    with act.Fori(1, TURNS - 1) as i:
                        for c in range(HPT):
                            decay(s, i, c)
                turn = TURNS - 1 if s < NB else 1
                x_dbl(p)
                if f >= 0:
                    rstd(2 * f + 1)
                    norm(f, XN)
                for c in range(HPT):
                    decay(s, turn, c)
                    if c == 2:
                        step_abs(p, 0)
                        if f >= 0:
                            norm_t(f, XNT, (0, 1))
                    if c == 3:
                        step_abs(p, 1)
                        step_exp(p)
                        if f >= 0:
                            norm_t(f, XNT, (2, 3))
                    if c == 5:
                        if f >= 0:
                            route_exp(f)
                        if s < NB:
                            rstd_log(2 * s)
                        step_log(p)
                        if s < NB:
                            rstd_exp(2 * s)
                    if c == 6 and 0 <= f < NB - 1:
                        shared_tanh(f, 0)
                seed(p)
                if s < NB:
                    z_gate(s)
            for it in range(IT):
                shared_tanh(NB - 1, it)
            with act.Fori(2, TURNS) as i:
                for c in range(HPT):
                    decay(NB, i, c)
            act.wait_ge(w_free, HS * FIRST_B + PRE_W)
            nc.scalar.activation(flat(Y[:, 0]), flat(PS[:, 0:4]), ACT.Copy).then_inc(y4_ready, 1)
            tile_rows(0)

            def tile_turn(s, i, prep):
                for u in range(BODY):
                    j = i * BODY + (TPS * (s - FIRST_B) + u)
                    if prep == 2 and u == 0:
                        x_dbl(s + 1)
                    decay(s, i, 2 * u)
                    tile_tanh(j, u, 0)
                    decay(s, i, 2 * u + 1)
                    tile_tanh(j, u, 1)
                    tile_rows(j + 1)
                    tile_out(j)
                    if prep == 1 and u < 2:
                        conv_tap(s + 1, u)
                    if prep == 1 and u == 3:
                        conv_silu(s + 1)
                    if prep == 2 and u < 2:
                        step_abs(s + 1, u)
                    if prep == 2 and u == 1:
                        step_exp(s + 1)
                    if prep == 2 and u == 2:
                        step_log(s + 1)
                    if prep == 2 and u == 3:
                        seed(s + 1)

            for s in range(FIRST_B, STAGES):
                act.wait_ge(delta_ready, s + 1)
                prep = s + 1 < STAGES
                with act.Fori(0, TURNS - 2 if prep else TURNS) as i:
                    tile_turn(s, i, 0)
                if prep:
                    tile_turn(s, TURNS - 2, 1)
                    tile_turn(s, TURNS - 1, 2)
            for b in range(NB + 1):
                f, l = NB + b, b - 1
                if b < NB:
                    rstd(2 * f)
                if l >= 0:
                    act.wait_ge(shift_ready, l + 1)
                    nc.scalar.activation(SM[:, 1, 0:QT * E1], SM[:, 0, 0:QT * E1], ACT.Exp).then_inc(exp_ready, 1)
                if b < NB:
                    z_gate(f)
                if l >= 0:
                    act.wait_ge(midt_done, l + 1)
                    if l:
                        act.wait_ge(ffn_done, QT * l)
                    nc.scalar.activation(MIDT, PRE[1], ACT.Copy).then_inc(midt_ready, 1)
                if b < NB:
                    rstd(2 * f + 1)
                    norm(f, XN1[b % 2])
                    norm_t(f, XNT1[b % 2], range(ET))

        @block.tensor
        def _(pe):
            def in_proj(s, pair):
                pe.wait_ge(ctx_in, 16 * (s + 1))
                pe.wait_ge(ld_inw, 16 * (lay(s) + 1))
                if s:
                    pe.wait_ge(dt_read, ET * s)
                for et in (2 * pair, 2 * pair + 1):
                    if pair:
                        pe.wait_ge(conv_step, 3 * ET * s + 4 + et - 1)
                    for k in range(KC):
                        mm = nc.tensor.matmul(PRE[et % 2], INW[:, k, et * P:(et + 1) * P], CTX[:, k, :],
                                              start=(k == 0), stop=(k == KC - 1))
                    mm.then_inc(inproj_done, 1)

            def x_proj(s):
                pe.wait_ge(u_ready, s + 1)
                pe.wait_ge(ld_proj, 32)
                for et in range(ET):
                    mm = nc.tensor.matmul(PRE[0][0:DR + 2 * NS, :], XPW[:, lay(s), et, :], DU[:, s % 2, et, :],
                                          start=(et == 0), stop=(et == ET - 1))
                mm.then_inc(xproj_done, 1)

            def dt_proj(s, pair):
                pe.wait_ge(xdbl_ready, s + 1)
                pe.wait_ge(ld_dtw, 16 * (lay(s) + 1))
                for et in (2 * pair, 2 * pair + 1):
                    if pair:
                        pe.wait_ge(dt_read, ET * s + et - 1)
                    nc.tensor.matmul(PRE[et % 2], DTW[2 * NS:, et * P:(et + 1) * P], XDBL[2 * NS:, :],
                                     start=True, stop=True).then_inc(dt_done, 1)

            def sum_skip(s):
                pe.wait_ge(seed_ready, s + 1)
                for et in range(ET):
                    nc.tensor.matmul(PS[:, et], ID[:, :], Y[:, yslot(s), et, :], start=True, stop=True)

            def sum_state(s, i, c):
                pe.wait_ge(mulc_done, i * HPT + (HS * s + c + 1 + PRE_MULC))
                for m in range(2):
                    mm = nc.tensor.matmul(PS[:, 2 * (c % 2) + m], ID[:, :], W[:, c % 4, m, :],
                                          start=False, stop=True, skip_group_check=True)
                mm.then_inc(w_free, 1)

            def y_transposes(f, y, lts):
                pe.wait_ge(yg_done, f + 1)
                for lt in lts:
                    if lt >= 2:
                        pe.wait_ge(xacc, QT * f + lt - 1)
                    for et in range(ET):
                        mm = nc.tensor.transpose(AUX[lt % 2][:, et * P:(et + 1) * P], y[:, et, lt * P:(lt + 1) * P], ID[:, :])
                    mm.then_inc(yt_done, 1)

            def norm_transposes(f, xn, ks):
                pe.wait_ge(xn_ready, QT * (f + 1))
                for k in ks:
                    if k >= 2:
                        pe.wait_ge(xnt_ready, ET * f + k - 1)
                    for q in range(QT):
                        mm = nc.tensor.transpose(AUX[k % 2][:, q * P:(q + 1) * P], xn[:, q, k * P:(k + 1) * P], ID[:, :])
                    mm.then_inc(xnt_done, 1)

            def route(f, xnt, w, n, done):
                pe.wait_ge(xnt_ready, ET * (f + 1))
                for q in range(QT):
                    for k in range(ET):
                        mm = nc.tensor.matmul(AUX[0][:, q * n:(q + 1) * n], xnt[:, k, q * P:(q + 1) * P], w[:, k, :],
                                              start=(k == 0), stop=(k == ET - 1))
                mm.then_inc(done, 1)

            def shared_in(b, it):
                pe.wait_ge(ld_shared, 16)
                if b == NB - 1 and it == 0:
                    pe.wait_ge(dt_read, ET * (NB + 2))
                elif b == NB - 1:
                    pe.wait_ge(counts_read, 1)
                elif it:
                    pe.wait_ge(shh_ready, IT * b + it)
                else:
                    pe.wait_ge(sc_ready, b + 1)
                for g in range(2):
                    for k in range(ET):
                        at = g * WGU + k * INNER + it * P
                        mm = nc.tensor.matmul(shared_banks(b, it)[g], MW[:, 0, at:at + P], XNT[:, k, :], start=(k == 0), stop=(k == ET - 1))
                mm.then_inc(shgu_done, 1)

            def shared_out(b, qs):
                pe.wait_ge(shh_ready, IT * (b + 1))
                for q in qs:
                    for it in range(IT):
                        at = 2 * WGU + it * D
                        mm = nc.tensor.matmul(shared_out_bank(b, q), HB[:, it, q * P:(q + 1) * P], MW[:, 0, at:at + D],
                                              start=(it == 0), stop=(it == IT - 1))
                    mm.then_inc(shdown_done, 1)

            def tile_transposes(j):
                pe.wait_ge(xs_in, j * 16 + 16)
                if not isinstance(j, int) or j:
                    pe.wait_ge(xst_ready, j)
                for k in range(ET):
                    for r in range(RT):
                        mm = nc.tensor.transpose(XT[:, k, r * P:(r + 1) * P], XS[:, r, k * P:(k + 1) * P], ID[:, :])
                mm.then_inc(xt_done, 1)

            def tile_in(j, u, half):
                pe.wait_ge(tw_in[u % 2], half * 16 + 16)
                pe.wait_ge(xst_ready, j + 1)
                for it in range(IT):
                    pe.wait_ge(h_ready, j * 2 + (it - 1 + PRE_H))
                    for g in range(2):
                        for k in range(ET):
                            at = g * WGU + k * INNER + it * P
                            mm = nc.tensor.matmul(PS[:, it, g * TILE:(g + 1) * TILE], MW[:, u % 2, at:at + P], XST[:, k, :],
                                                  start=(k == 0), stop=(k == ET - 1))
                    mm.then_inc(gu_done, 1)

            def tile_out(j, u):
                pe.wait_ge(h_ready, j * 2 + (2 + PRE_H))
                for r in range(RT):
                    pe.wait_ge(yev, j * 2 + (r - 1 + PRE_YEV))
                    for it in range(IT):
                        at = 2 * WGU + it * D
                        mm = nc.tensor.matmul(PS[:, 2 + r], HT[:, u % 2, it, r * P:(r + 1) * P], MW[:, u % 2, at:at + D],
                                              start=(it == 0), stop=(it == IT - 1))
                    mm.then_inc(y_done, 1)

            pe.sem_inc(w_free, PRE_W)
            pe.sem_inc(y_done, PRE_Y)
            pe.wait_ge(masks, 6)
            for pair in range(2):
                in_proj(0, pair)
            x_proj(0)
            for pair in range(2):
                dt_proj(0, pair)
            in_proj(1, 0)
            for s in range(FIRST_B):
                f, p, g = s - 1, s + 1, s - 2
                if g >= 0:
                    shared_out(g, (0, 1))
                if f >= 0:
                    if g >= 0:
                        pe.wait_ge(shacc, QT * g + 2)
                    y_transposes(f, Y[:, yslot(f)], (0, 1))
                sum_skip(s)
                for c in range(HPT):
                    sum_state(s, 0, c)
                    if c == 1:
                        if f >= 0:
                            y_transposes(f, Y[:, yslot(f)], (2, 3))
                    if c == 3:
                        in_proj(p, 1)
                    if c == 5 and g >= 0:
                        pe.wait_ge(xacc, QT * (f + 1))
                        shared_out(g, (2, 3))
                x_proj(p)
                if s < NB:
                    with pe.Fori(1, TURNS - 1) as i:
                        for c in range(HPT):
                            sum_state(s, i, c)
                turn = TURNS - 1 if s < NB else 1
                dt_proj(p, 0)
                for c in range(HPT):
                    sum_state(s, turn, c)
                    if c == 0 and f >= 0:
                        if g >= 0:
                            pe.wait_ge(shacc, QT * (g + 1))
                        norm_transposes(f, XN, (0, 1))
                    if c == 1:
                        dt_proj(p, 1)
                        if f >= 0:
                            norm_transposes(f, XN, (2, 3))
                    if c == 3 and f >= 0:
                        route(f, XNT, GW, NE, router_done)
                    if c == 4 and 0 <= f < NB - 1:
                        shared_in(f, 0)
                    if c == 5 and 0 <= f < NB - 1:
                        shared_in(f, 1)
                    if c == 6 and s < NB:
                        in_proj(p + 1, 0)
            pe.wait_ge(ranked, NB)
            sel = SEL[:, :, :].rearrange("p t e -> p (t e)")
            nc.tensor.matmul(AUX[0][:, 0:NT * NE], US[:, :], sel, start=True, stop=True)
            nc.tensor.matmul(AUX[1][:, 0:NT * NE], ON[:, :], sel, start=True, stop=True).then_inc(counted, 1)
            for it in range(IT):
                shared_in(NB - 1, it)
            shared_out(NB - 1, range(QT))
            with pe.Fori(2, TURNS) as i:
                for c in range(HPT):
                    sum_state(NB, i, c)
            pe.wait_ge(shacc, QT * NB)
            tile_transposes(0)
            pe.wait_ge(y4_ready, 1)

            def tile_turn(s, i, prep):
                for u in range(BODY):
                    j = i * BODY + (TPS * (s - FIRST_B) + u)
                    tile_in(j, u, i * 2 + (TPS // 2 * (s - FIRST_B) + u // 2))
                    tile_transposes(j + 1)
                    tile_out(j, u)
                    if prep == 1 and u < 2:
                        in_proj(s + 1, u)
                    if prep == 1 and u == 3:
                        x_proj(s + 1)
                    if prep == 2 and u < 2:
                        dt_proj(s + 1, u)

            for s in range(FIRST_B, STAGES):
                prep = s + 1 < STAGES
                with pe.Fori(0, TURNS - 2 if prep else TURNS) as i:
                    tile_turn(s, i, 0)
                if prep:
                    tile_turn(s, TURNS - 2, 1)
                    tile_turn(s, TURNS - 1, 2)
            pe.wait_ge(ld_ffn1, 16 * 4)
            pe.wait_ge(xst_ready, NTILE + 1)
            pe.wait_ge(yev, 2 * NTILE + PRE_YEV)
            for b in range(NB + 1):
                f, l = NB + b, b - 1
                if l >= 0:
                    pe.wait_ge(midg_ready, l + 1)
                    for q in range(QT):
                        mm = nc.tensor.transpose(PRE[1][:, q * P:(q + 1) * P], MID[:, q, :], ID[:, :])
                    mm.then_inc(midt_done, 1)
                    pe.wait_ge(midt_ready, l + 1)
                    for q in range(QT):
                        nc.tensor.matmul(PS[:, q], MIDT[:, q * P:(q + 1) * P], LB, start=False, stop=True,
                                         skip_group_check=True).then_inc(ffn_done, 1)
                if b < NB:
                    xnt = XNT1[b % 2]
                    y_transposes(f, Y[:, b], range(QT))
                    norm_transposes(f, XN1[b % 2], range(ET))
                    route(f, xnt, R1, E1, logit_done)
                    for q in range(QT):
                        for k in range(ET):
                            mm = nc.tensor.matmul(PRE[0][:, q * P:(q + 1) * P], xnt[:, k, q * P:(q + 1) * P], LA[:, k, :],
                                                  start=(k == 0), stop=(k == ET - 1))
                    mm.then_inc(mid_done, 1)
                    if b:
                        pe.wait_ge(x_final, QT * b)
                    for q in range(QT):
                        for k in range(ET):
                            nc.tensor.matmul(PS[:, q], xnt[:, k, q * P:(q + 1) * P], BW[:, k, :], start=(k == 0), stop=False)
                        nc.tensor.matmul(PS[:, q], ON[0:1, :], BB, start=False, stop=True)

        @block.vector
        def _(dve):
            steps = [0]

            def link(ins):
                steps[0] += 1
                ins.then_inc(dve_step, 1)
                dve.wait_ge(dve_step, steps[0])

            def conv(s, pair):
                sl = s % 2
                for m, j in enumerate(range(DC - 2, -1, -1)):
                    for h in range(2):
                        et, sh = 2 * pair + h, DC - 1 - j
                        if m == 0:
                            dve.wait_ge(tap_first, ET * s + et + 1)
                        else:
                            dve.wait_ge(conv_step, 3 * ET * s + 6 * pair + 2 * (m - 1) + h + 1)
                        nc.vector.scalar_tensor_tensor(
                            out=DU[:, sl, et, sh:], in0=PRE[h][:, 0:L - sh], scalar=CH[:, lay(s), et, j:j + 1],
                            in1=DU[:, sl, et, sh:], op0=ALU.mult, op1=ALU.add).then_inc(conv_step, 1)

            def step_first():
                dl, sw, relu = flat(DEL[:, 0]), flat(SW[:, :, :]), flat(Y[:, yslot(0)])
                dve.wait_ge(e_ready, 1)
                nc.vector.tensor_scalar(sw, dl, 1.0, -1.0, ALU.add, ALU.add).then_inc(w1_ready, 1)
                dve.wait_ge(w1_ready, 1)
                nc.vector.tensor_tensor(sw, dl, sw, ALU.subtract).then_inc(corr_ready, 1)
                dve.wait_ge(corr_ready, 1)
                nc.vector.tensor_tensor(sw, sw, relu, ALU.add).then_inc(relu_added, 1)
                dve.wait_ge(relu_added, 1)
                dve.wait_ge(ln_ready, 1)
                nc.vector.tensor_tensor(dl, dl, sw, ALU.add).then_inc(delta_ready, 1)

            def delta_u(s):
                dve.wait_ge(delta_ready, s + 1)
                dve.wait_ge(seed_ready, s + 1)
                dve.wait_ge(xproj_done, s + 1)
                nc.vector.tensor_tensor(flat(DU[:, s % 2]), flat(DU[:, s % 2]), flat(DEL[:, s % 2]),
                                        ALU.mult).then_inc(du_ready, 1)

            def stats(b):
                for q in range(QT):
                    ins = nc.vector.bn_stats(ST[:, q, :], X[:, b * QT + q, :])
                link(ins)
                for q in range(QT):
                    ins = nc.vector.bn_aggr(MV[:, q, :], ST[:, q, :])
                link(ins)
                nc.vector.tensor_scalar(RS[:, :], MV[:, :, 1], EPS, None, ALU.add).then_inc(var_ready, 1)

            def scan_gate(f, y, src):
                dve.wait_ge(zs_ready, f + 1)
                nc.vector.tensor_tensor(flat(y), src, flat(ZS[:, :, :]), ALU.mult).then_inc(yg_done, 1)

            def scan_add(f, lts, gate):
                for lt in lts:
                    dve.wait_ge(yt_done, QT * f + lt + 1)
                    xr = X[:, (f % NB) * QT + lt, :]
                    nc.vector.scalar_tensor_tensor(out=xr, in0=AUX[lt % 2], scalar=TG[:, gate:gate + 1], in1=xr, op0=ALU.mult,
                                                   op1=ALU.add).then_inc(xacc, 1)

            def norm_bias(v):
                dve.wait_ge(std_ready, v + 1)
                nc.vector.scalar_tensor_tensor(out=NBI[:, :], in0=MV[:, :, 0], scalar=-1.0, in1=RS[:, :], op0=ALU.mult,
                                               op1=ALU.mult).then_inc(zn_ready, 1)

            def rank_of(out, m, n, tri, s1=T1, s2=T2):
                a = s1[:, 0:QT * n * n].rearrange("p (q e f) -> p q e f", q=QT, e=n)
                c = s2[:, 0:QT * n * n].rearrange("p (q e f) -> p q e f", q=QT, e=n)
                other = m.unsqueeze(2).to_broadcast([P, QT, n, n])
                own = m.unsqueeze(3).to_broadcast([P, QT, n, n])
                nc.vector.tensor_tensor(a, other, own, ALU.is_gt)
                link(nc.vector.tensor_tensor(c, other, own, ALU.is_equal))
                link(nc.vector.tensor_tensor(c, c, tri.unsqueeze(1).to_broadcast([P, QT, n, n]), ALU.mult))
                link(nc.vector.tensor_tensor(a, a, c, ALU.add))
                link(nc.vector.reduce_sum(out, a, AX.X))

            def route(b):
                q16 = lambda i: SM[:, i, :].rearrange("p (q e) -> p q e", e=NE)
                dve.wait_ge(sc_ready, b + 1)
                dve.wait_ge(ld_small, 16 * 5)
                link(nc.vector.tensor_scalar(SC[:, :, :], SC[:, :, :], 1.0, None, ALU.add))
                link(nc.vector.reciprocal(SC[:, :, :], SC[:, :, :]))
                biased = q16(0)
                link(nc.vector.tensor_tensor(biased, SC[:, :, :], EB[:, :].unsqueeze(1).to_broadcast([P, QT, NE]), ALU.add))
                pairs = SM[:, 0, :].rearrange("p (n two) -> p n two", two=2)
                mx, mn = SM[:, 1, 0:32], SM[:, 2, 0:32]
                nc.vector.tensor_tensor(mx, pairs[:, :, 0], pairs[:, :, 1], ALU.max)
                link(nc.vector.tensor_tensor(mn, pairs[:, :, 0], pairs[:, :, 1], ALU.min))
                mxp, mnp = [v.rearrange("p (n two) -> p n two", two=2) for v in (mx, mn)]
                top, lo, hi2 = SM[:, 3, 0:16], SM[:, 3, 16:32], SM[:, 3, 32:48]
                nc.vector.tensor_tensor(top, mxp[:, :, 0], mxp[:, :, 1], ALU.max)
                nc.vector.tensor_tensor(lo, mxp[:, :, 0], mxp[:, :, 1], ALU.min)
                link(nc.vector.tensor_tensor(hi2, mnp[:, :, 0], mnp[:, :, 1], ALU.max))
                link(nc.vector.tensor_tensor(lo, lo, hi2, ALU.max))
                gs = SM[:, 4, 0:16]
                link(nc.vector.tensor_tensor(gs, top, lo, ALU.add))
                gr = SM[:, 4, 16:32].rearrange("p (q g) -> p q g", g=NGRP)
                rank_of(gr, gs.rearrange("p (q g) -> p q g", g=NGRP), NGRP, TRI[:, 0:NGRP, 0:NGRP])
                keep, low = SM[:, 4, 32:48], SM[:, 4, 48:64]
                link(nc.vector.tensor_scalar(keep, SM[:, 4, 16:32], float(GKEEP), None, ALU.is_lt))
                link(nc.vector.tensor_scalar(low, keep, BIG, -BIG, ALU.mult, ALU.add))
                masked = q16(5)
                by_group = lambda v: v.unsqueeze(2).to_broadcast([P, QT * NGRP, GSZ])
                g3 = lambda i: SM[:, i, :].rearrange("p (g e) -> p g e", e=GSZ)
                link(nc.vector.tensor_tensor(g3(5), g3(0), by_group(keep), ALU.mult))
                link(nc.vector.tensor_tensor(g3(5), g3(5), by_group(low), ALU.add))
                rk, sel, cw = (v[:, b * QT:(b + 1) * QT, :] for v in (RK, SEL, CW))
                rank_of(rk, masked, NE, TRI[:, :, :])
                link(nc.vector.tensor_scalar(sel, rk, float(TOPK), None, ALU.is_lt))
                link(nc.vector.tensor_tensor(cw, SC[:, :, :], sel, ALU.mult))
                tot = SM[:, 6, 0:QT]
                link(nc.vector.reduce_sum(tot, cw, AX.X))
                link(nc.vector.tensor_scalar(tot, tot, 1e-20, None, ALU.add))
                link(nc.vector.reciprocal(tot, tot))
                link(nc.vector.tensor_scalar(tot, tot, SCALING, TG[:, 2:3], ALU.mult, ALU.mult))
                nc.vector.tensor_tensor(cw, cw, tot.unsqueeze(2).to_broadcast([P, QT, NE]), ALU.mult).then_inc(ranked, 1)

            def slots():
                n2 = NT * NE
                by_e = lambda a: T1[:, a * n2:(a + 1) * n2].rearrange("p (e t) -> p e t", e=NE)
                ct, ci, ex = by_e(0), by_e(1), by_e(2)
                reset = T1[:, 3 * n2:4 * n2]
                count, rows = SM[:, 6, 0:NTILE + 1], SM[:, 5, 0:8]
                link(nc.vector.tensor_tensor_scan(count, ON[:, 0:NTILE + 1], ON[:, 0:NTILE + 1], 0.0, ALU.mult, ALU.add))
                link(nc.vector.tensor_scalar(rows, count[:, 0:8], -1.0, float(TILE), ALU.add, ALU.mult))
                link(nc.vector.memset(reset, 1.0))
                nc.vector.memset(reset.rearrange("p (e t) -> p e t", e=NE)[:, :, 0:1], 0.0)
                dve.wait_ge(counted, 1)
                before = T2[:, 3 * n2:4 * n2]
                nc.vector.tensor_copy(before, AUX[0][:, 0:n2])
                nc.vector.tensor_copy(ct, AUX[1][:, 0:n2].rearrange("p (t e) -> p e t", e=NE)).then_inc(counts_read, 1)
                dve.wait_ge(counts_read, 1)
                link(nc.vector.tensor_tensor_scan(T1[:, n2:2 * n2], reset, T1[:, 0:n2], 0.0, ALU.mult, ALU.add))
                cnt = ci[:, :, NT - 1]
                full = T2[:, 0:NE * 8].rearrange("p (e m) -> p e m", m=8)
                link(nc.vector.tensor_tensor(full, cnt.unsqueeze(2).to_broadcast([P, NE, 8]),
                                             rows.unsqueeze(1).to_broadcast([P, NE, 8]), ALU.is_gt))
                tiles, upto, first = SM[:, 0, 0:NE], SM[:, 0, NE:2 * NE], SM[:, 0, 2 * NE:3 * NE]
                link(nc.vector.reduce_sum(tiles, full, AX.X))
                link(nc.vector.tensor_tensor_scan(upto, ON[:, 0:NE], tiles, 0.0, ALU.mult, ALU.add))
                link(nc.vector.tensor_tensor(first, upto, tiles, ALU.subtract))
                link(nc.vector.tensor_scalar(first, first, float(TILE), None, ALU.mult))
                link(nc.vector.tensor_tensor(ex, ci, ct, ALU.subtract))
                link(nc.vector.tensor_tensor(ex, ex, first.unsqueeze(2).to_broadcast([P, NE, NT]), ALU.add))
                slot = T2[:, 0:n2].rearrange("p (t e) -> p t e", e=NE)
                link(nc.vector.tensor_tensor(slot, before.rearrange("p (t e) -> p t e", e=NE),
                                             ex.rearrange("p e t -> p t e"), ALU.add))
                is_k = T2[:, n2:2 * n2].rearrange("p (t e) -> p t e", e=NE)
                part = T2[:, 2 * n2:3 * n2].rearrange("p (t e) -> p t e", e=NE)
                slk = SM[:, 1:1 + TOPK, 0:NT]
                for k in range(TOPK):
                    link(nc.vector.tensor_scalar(is_k, RK[:, :, :], float(k), None, ALU.is_equal))
                    link(nc.vector.tensor_tensor(part, is_k, slot, ALU.mult))
                    link(nc.vector.reduce_sum(slk[:, k, :], part, AX.X))
                    link(nc.vector.tensor_tensor(part, is_k, CW[:, :, :], ALU.mult))
                    link(nc.vector.reduce_sum(CWK[:, k, :], part, AX.X))
                nc.vector.tensor_copy(SLU[:, :, :], slk).then_inc(slots_ready, 1)
                ends = T1[:, 0:(NTILE + 1) * NE].rearrange("p (j e) -> p j e", e=NE)
                link(nc.vector.tensor_tensor(ends, upto.unsqueeze(1).to_broadcast([P, NTILE + 1, NE]),
                                             count.unsqueeze(2).to_broadcast([P, NTILE + 1, NE]), ALU.is_lt))
                num = SM[:, 7, 0:NTILE + 1]
                link(nc.vector.reduce_sum(num, ends, AX.X))
                nc.vector.tensor_scalar(TE[:, :], num, float(NE - 1), None, ALU.min).then_inc(slots_ready, 1)

            def mul_b(s, i, c):
                u, h = c // 2, c % 2
                if h == 0:
                    dve.wait_ge(bc_in[u], i * 16 + 16 * (NS // BODY * s + 1))
                dve.wait_ge(w_free, i * (2 * BODY) + (HS * s + c + PRE_W - 3))
                nc.vector.tensor_tensor(W[:, c % 4], DU[:, s % 2, 2 * h:2 * h + 2, :], bcast2(BC[:, u, 0, :]),
                                        ALU.mult).then_inc(mulb_done, 1)

            def scan(s, i, c):
                dve.wait_ge(mulb_done, i * (2 * BODY) + (HS * s + c + 1))
                dve.wait_ge(da_ready, i * (2 * BODY) + (HS * s + c + 1))
                nc.vector.tensor_tensor_scan(flat(W[:, c % 4]), flat(DAS[c % da_slots(s)]), flat(W[:, c % 4]), 0.0, ALU.mult,
                                             ALU.add).then_inc(scan_done, 1)

            def mul_c(s, i, c):
                dve.wait_ge(scan_done, i * HPT + (HS * s + c + 1 + PRE_SCAN))
                dve.wait_ge(mulc_done, i * HPT + (HS * s + c + PRE_MULC))
                nc.vector.tensor_tensor(W[:, c % 4], W[:, c % 4], bcast2(BC[:, c // 2, 1, :]), ALU.mult).then_inc(mulc_done, 1)

            def add_y(s, i, c):
                dve.wait_ge(mulc_done, i * (2 * BODY) + (HS * s + c + 1 + PRE_MULC))
                dve.wait_ge(w_free, i * (2 * BODY) + (HS * s + c - 1 + PRE_W))
                y = Y[:, yslot(s), 2 * (c % 2):2 * (c % 2) + 2, :]
                nc.vector.tensor_tensor(y, y, W[:, c % 4], ALU.add).then_inc(w_free, 1)

            def half(s, i, c):
                if c + 1 < HPT:
                    mul_b(s, i, c + 1)
                scan(s, i, c)

            def tile_hidden(j, u, it):
                h = HT[:, u % 2, it, :]
                dve.wait_ge(sil_ready, j * 2 + it + 1)
                nc.vector.scalar_tensor_tensor(out=h, in0=h, scalar=1.0, in1=PS[:, it, 0:TILE], op0=ALU.add,
                                               op1=ALU.mult).then_inc(hg_ready, 1)
                dve.wait_ge(hg_ready, j * 2 + it + 1)
                nc.vector.tensor_tensor(h, h, PS[:, it, TILE:2 * TILE], ALU.mult).then_inc(h_ready, 1)

            def shared_hidden(b, it):
                h = HB[:, it, :]
                dve.wait_ge(shsil_ready, IT * b + it + 1)
                link(nc.vector.scalar_tensor_tensor(out=h, in0=h, scalar=1.0, in1=shared_banks(b, it)[0], op0=ALU.add,
                                                    op1=ALU.mult))
                nc.vector.tensor_tensor(h, h, shared_banks(b, it)[1], ALU.mult).then_inc(shh_ready, 1)

            def shared_add(b, qs):
                for q in qs:
                    dve.wait_ge(shdown_done, QT * b + q + 1)
                    xr = X[:, b * QT + q, :]
                    nc.vector.scalar_tensor_tensor(out=xr, in0=shared_out_bank(b, q), scalar=TG[:, 2:3], in1=xr, op0=ALU.mult,
                                                   op1=ALU.add).then_inc(shacc, 1)

            dve.sem_inc(scan_done, PRE_SCAN)
            dve.sem_inc(h_ready, PRE_H)
            nc.vector.memset(YSB[:, :, :], 0.0).then_inc(zeroed, 1)
            for da in DAS:
                nc.vector.memset(da, 0.0).then_inc(zeroed, 1)
            dve.wait_ge(masks, 6)
            dve.wait_ge(ld_chan, 32)
            for pair in range(2):
                conv(0, pair)
            step_first()
            delta_u(0)
            dve.wait_ge(tg_ready, 2)
            for s in range(FIRST_B):
                f, p, g = s - 1, s + 1, s - 2
                dve.wait_ge(du_ready, s + 1)
                mul_b(s, 0, 0)
                for c in range(HPT):
                    if c == 3:
                        scan(s, 0, c)
                        if 0 <= g:
                            shared_add(g, (0, 1))
                        if f >= 0:
                            dve.wait_ge(w_free, HS * s + PRE_W)
                            scan_gate(f, Y[:, yslot(f)], flat(PS[:, 0:4]))
                        conv(p, 0)
                        if f >= 0:
                            scan_add(f, (0, 1), 0)
                        mul_b(s, 0, c + 1)
                    else:
                        half(s, 0, c)
                    if c == 1 and g >= 0:
                        shared_hidden(g, 1)
                    if c == 4 and f >= 0:
                        scan_add(f, (2, 3), 0)
                    if c == 5 and f >= 0:
                        dve.wait_ge(xacc, QT * (f + 1))
                        stats(f)
                    if c == 6:
                        conv(p, 1)
                if g >= 0:
                    shared_add(g, (2, 3))
                if s < NB:
                    with dve.Fori(1, TURNS - 1) as i:
                        mul_b(s, i, 0)
                        for c in range(HPT):
                            half(s, i, c)
                turn = TURNS - 1 if s < NB else 1
                mul_b(s, turn, 0)
                if f >= 0:
                    norm_bias(2 * f + 1)
                for c in range(HPT):
                    half(s, turn, c)
                    if c == 3 and s < NB:
                        dve.wait_ge(ld_x[s], 16)
                        if s:
                            dve.wait_ge(xn_ready, QT * s)
                        stats(s)
                    if c == 5:
                        if f >= 0:
                            route(f)
                        if s < NB:
                            norm_bias(2 * s)
                    if c == 6 and 0 <= f < NB - 1:
                        shared_hidden(f, 0)
                delta_u(p)
            slots()
            for it in range(IT):
                shared_hidden(NB - 1, it)
            with dve.Fori(2, TURNS) as i:
                mul_b(NB, i, 0)
                for c in range(HPT):
                    half(NB, i, c)
                    if c:
                        mul_c(NB, i, c - 1)
                mul_c(NB, i, HPT - 1)
            shared_add(NB - 1, range(QT))

            def tile_turn(s, i, prep):
                mul_b(s, i, 0)
                for u in range(BODY):
                    j = i * BODY + (TPS * (s - FIRST_B) + u)
                    for h in range(2):
                        c = 2 * u + h
                        tile_hidden(j, u, h)
                        if h and c >= 3:
                            add_y(s, i, c - 3)
                        half(s, i, c)
                        if h and c >= 2:
                            add_y(s, i, c - 2)
                    if prep == 1 and 1 <= u <= 2:
                        conv(s + 1, u - 1)
                    if prep == 2 and u == 3:
                        delta_u(s + 1)
                add_y(s, i, HPT - 2)
                add_y(s, i, HPT - 1)

            for s in range(FIRST_B, STAGES):
                dve.wait_ge(du_ready, s + 1)
                dve.wait_ge(w_free, HS * s + PRE_W)
                prep = s + 1 < STAGES
                with dve.Fori(0, TURNS - 2 if prep else TURNS) as i:
                    tile_turn(s, i, 0)
                if prep:
                    tile_turn(s, TURNS - 2, 1)
                    tile_turn(s, TURNS - 1, 2)

            def combine(b):
                for k in range(TOPK):
                    for q in range(QT):
                        if k:
                            dve.wait_ge(combined, TOPK * QT * b + QT * (k - 1) + q + 1)
                        else:
                            dve.wait_ge(gathered[q], 16 * TOPK * (b + 1))
                        xr, g = X[:, b * QT + q, :], b * QT + q
                        nc.vector.scalar_tensor_tensor(out=xr, in0=GK[q][:, k, :], scalar=CWK[:, k, g:g + 1], in1=xr,
                                                       op0=ALU.mult, op1=ALU.add).then_inc(combined, 1)
                dve.wait_ge(combined, TOPK * QT * (b + 1))

            v8 = lambda i: SM[:, i, 0:QT * E1].rearrange("p (q e) -> p q e", e=E1)
            over_e = lambda v: v.unsqueeze(2).to_broadcast([P, QT, E1])

            def lora_logits(b):
                dve.wait_ge(logit_done, b + 1)
                link(nc.vector.tensor_tensor(v8(0), AUX[0][:, 0:QT * E1].rearrange("p (q e) -> p q e", e=E1),
                                             RB[:, :].unsqueeze(1).to_broadcast([P, QT, E1]), ALU.add))
                m = SM[:, 2, 0:QT]
                link(nc.vector.reduce_max(m, v8(0), AX.X))
                nc.vector.tensor_tensor(v8(0), v8(0), over_e(m), ALU.subtract).then_inc(shift_ready, 1)

            def lora_gates(b):
                m = SM[:, 2, 0:QT]
                dve.wait_ge(exp_ready, b + 1)
                link(nc.vector.reduce_sum(m, v8(1), AX.X))
                link(nc.vector.reciprocal(m, m))
                link(nc.vector.tensor_tensor(v8(1), v8(1), over_e(m), ALU.mult))
                rank_of(v8(3), v8(1), E1, TRI[:, 0:E1, 0:E1], flat(SW[:, 1:2]), flat(SW[:, 2:3]))
                link(nc.vector.tensor_scalar(v8(3), v8(3), 2.0, None, ALU.is_lt))
                link(nc.vector.tensor_tensor(v8(3), v8(3), v8(1), ALU.mult))
                link(nc.vector.reduce_sum(m, v8(3), AX.X))
                link(nc.vector.reciprocal(m, m))
                link(nc.vector.tensor_scalar(m, m, LSCALE, None, ALU.mult))
                link(nc.vector.tensor_tensor(v8(3), v8(3), over_e(m), ALU.mult))
                dve.wait_ge(mid_done, b + 1)
                if b:
                    dve.wait_ge(midt_done, b)
                nc.vector.tensor_tensor(
                    MID.rearrange("p q (e r) -> p (q e) r", r=RANK1), PRE[0].rearrange("p (n r) -> p n r", r=RANK1),
                    SM[:, 3, 0:QT * E1].unsqueeze(2).to_broadcast([P, QT * E1, RANK1]), ALU.mult).then_inc(midg_ready, 1)

            def lora_add(b):
                for q in range(QT):
                    dve.wait_ge(ffn_done, QT * b + q + 1)
                    xr = X[:, b * QT + q, :]
                    nc.vector.scalar_tensor_tensor(out=xr, in0=PS[:, q], scalar=TG[:, 3:4], in1=xr, op0=ALU.mult,
                                                   op1=ALU.add).then_inc(x_final, 1)

            for b in range(NB + 1):
                f, l = NB + b, b - 1
                if b < NB:
                    combine(b)
                    dve.wait_ge(xn_ready, QT * f)
                    stats(b)
                if l >= 0:
                    lora_logits(l)
                if b < NB:
                    norm_bias(2 * f)
                if l >= 0:
                    lora_gates(l)
                if b < NB:
                    scan_gate(f, Y[:, b], flat(Y[:, b]))
                if l >= 0:
                    lora_add(l)
                if b < NB:
                    scan_add(f, range(QT), 1)
                    dve.wait_ge(xacc, QT * (f + 1))
                    stats(b)
                    norm_bias(2 * f + 1)


def _layouts(a):
    import numpy as np

    f = {k: np.asarray(v) for k, v in a.items()}
    c = np.ascontiguousarray
    out = {"x": c(f["x"]), "ctxT": c(f["ctx_1024"].reshape(NB * L, DM).T),
           "gates": c(np.concatenate([f["g_xattn"], f["g_ffn"]])[None, :])}
    order = list(range(DR, DR + 2 * NS)) + list(range(DR))
    for layer in range(2):
        g = lambda n: f[f"L{layer}_xattn_{n}"]
        out[f"in_wT{layer}"] = c(g("in_proj_w").T)
        out[f"chan{layer}"] = c(np.concatenate(
            [g("conv_w").reshape(D, DC), g("conv_b")[:, None], g("dt_proj_b")[:, None], g("D")[:, None], g("A_log")], axis=1))
        out[f"xprojT{layer}"] = c(g("x_proj_w")[order].T)
        out[f"dtT{layer}"] = c(g("dt_proj_w").T)

    def packed(gate, up, down):
        n = gate.shape[0]
        rows = [w.transpose(0, 2, 1).reshape(n, ET, P, INNER).transpose(0, 2, 1, 3).reshape(n, P, WGU) for w in (gate, up)]
        rows.append(down.transpose(0, 2, 1).reshape(n, IT, P, D).transpose(0, 2, 1, 3).reshape(n, P, IT * D))
        return np.concatenate(rows, axis=2)

    out["moe_w"] = c(np.concatenate([
        packed(f["L0_ffn_gate_proj"], f["L0_ffn_up_proj"], f["L0_ffn_down_proj"]),
        packed(f["L0_ffn_shared_gate"][None], f["L0_ffn_shared_up"][None], f["L0_ffn_shared_down"][None])]))
    out["gwT"] = c(f["L0_ffn_gate_weight"].T)
    out["ebias"] = c(f["L0_ffn_expert_bias"][None, :])
    out["base_wT"] = c(f["L1_ffn_base_w"].T)
    out["base_b"] = c(f["L1_ffn_base_b"][None, :])
    out["r1T"] = c(f["L1_ffn_router_w"].T)
    out["rb"] = c(f["L1_ffn_router_b"][None, :])
    out["loraA"] = c(f["L1_ffn_lora_A"].transpose(1, 0, 2).reshape(D, E1 * RANK1))
    out["loraB"] = c(f["L1_ffn_lora_B"].reshape(E1 * RANK1, D))
    return out


def kernel(**inputs):
    import concourse.bacc as _bacc
    from concourse import mybir as _mybir
    from concourse.bass_utils import run_bass_kernel_spmd as _run

    nc = _bacc.Bacc("TRN2", target_bir_lowering=False, num_devices=1)
    arrays, t = {}, {}
    for name, a in _layouts(inputs).items():
        arrays[f"in_{name}"] = a
        t[name] = nc.dram_tensor(f"in_{name}", a.shape, _mybir.dt.from_np(a.dtype), kind="ExternalInput").ap()
    t["out"] = nc.dram_tensor("out_x", (NB, L, D), F32, kind="ExternalOutput").ap()
    build(nc, t)
    return _run(nc, [arrays], core_ids=[0]).results[0]["out_x"]
```

```python
from contextlib import ExitStack

import concourse.bass as bass
from concourse import mybir

F32 = mybir.dt.float32
I32 = mybir.dt.int32
U32 = mybir.dt.uint32
ALU = mybir.AluOpType
ACT = mybir.ActivationFunctionType
AX = mybir.AxisListType

P = 128
NB, L, D = 4, 512, 512
DM, NS, DR, DC = 256, 16, 16, 4
ET, QT, KC = D // P, L // P, DM // P
NT = NB * QT
NE, TOPK, NGRP, GKEEP, SCALING = 16, 4, 4, 2, 2.5
GSZ = NE // NGRP
INNER = 256
IT = INNER // P
TILE = 256
RT = TILE // P
NTILE = (NB * L * TOPK + NE * (TILE - 1)) // TILE
WGU = ET * INNER
WPK = 2 * WGU + IT * D
E1, RANK1, LSCALE = 8, 16, 2.0
MR = E1 * RANK1 + E1
EPS = 1e-5
CHC = DC + 3 + NS
C_CB, C_DB, C_D, C_A = DC, DC + 1, DC + 2, DC + 3
STAGES = 2 * NB
HS = 2 * NS
BODY = 4
TURNS = NS // BODY
HPT = 2 * BODY
FIRST_B = NB + 1
TPS = -(-NTILE // (STAGES - FIRST_B))
ZCH = TURNS * NB
ZROWS = -(-NTILE * TILE // (P * ZCH))
BIG = 3.0e38

PRE_SCAN, PRE_MULC, PRE_W, PRE_H, PRE_Y, PRE_YEV, PRE_YS = 4, 8, 4, 2, 4, 2, 16


def build(nc, t):
    with ExitStack() as ctx:
        def sb(name, shape, dt=F32):
            return ctx.enter_context(nc.sbuf_tensor(name, shape, dt))

        def sem(name):
            return ctx.enter_context(nc.semaphore(name))

        X = sb("x_res", [P, NT, D])
        Y = sb("y_scan", [P, NB, ET, L])
        DEL = sb("delta", [P, 2, ET, L])
        DU = sb("du", [P, 2, ET, L])
        DA = sb("decay", [P, 2, 2, L])
        W = sb("state", [P, 4, 2, L])
        BC = sb("bc_rows", [P, 4, 2, L])
        SW = sb("softplus_tmp", [P, ET, L])
        ZS = sb("z_gate", [P, QT, D])
        YSB = sb("expert_out", [P, RT, D])
        HB = sb("hidden", [P, 2, 2 * TILE])
        MW = sb("expert_w", [P, 2, WPK])
        CTX = sb("ctx_t", [P, KC, L])
        INW = sb("in_w", [P, KC, D])
        XPW = sb("xproj_w", [P, 2, ET, DR + 2 * NS])
        DTW = sb("dt_w", [DR + 2 * NS, D])
        CH = sb("chan", [P, 2, ET, CHC])
        AN = sb("neg_a", [P, 2, ET, NS])
        XDBL = sb("x_dbl", [DR + 2 * NS, L])
        ID = sb("ident", [P, P])
        US = sb("upper", [P, P])
        ON = sb("ones", [P, P])
        TRI = sb("tri", [P, NE, NE])
        GW = sb("router_w", [P, ET, NE])
        EB = sb("expert_bias", [P, NE])
        TG = sb("tanh_gates", [P, 4])
        RB = sb("router1_b", [P, E1])
        MV = sb("mean_var", [P, QT, 2])
        RS = sb("rstd", [P, QT])
        NBI = sb("neg_mean_rstd", [P, QT])
        SC = sb("scores", [P, QT, NE])
        RK = sb("rank", [P, NT, NE])
        CW = sb("route_w", [P, NT, NE])
        SEL = sb("selected", [P, NT, NE])
        SM = sb("small", [P, 8, QT * NE])
        SLU = sb("slots", [P, TOPK, NT], U32)
        CWK = sb("slot_w", [P, TOPK, NT])
        TE = sb("tile_expert", [P, NTILE], I32)

        def flat(ap):
            return ap.rearrange("p a b -> p (a b)")

        ST = SM[:, 7, 0:QT * 6].rearrange("p (q s) -> p q s", s=6)
        XN, XNT = Y[:, 2], Y[:, 3]
        XS = ZS[:, 0:RT]
        XST = flat(ZS[:, RT:QT]).rearrange("p (k r) -> p k r", k=ET)
        HT = HB[:, :, :].rearrange("p s (i r) -> p s i r", i=IT)
        T1, T2 = flat(ZS[:, 0:2]), flat(ZS[:, 2:4])
        GK = [W[:, 0:2].rearrange("p a b n -> p (a b) n"), W[:, 2:4].rearrange("p a b n -> p (a b) n"),
              DA[:, :, :, :].rearrange("p a b n -> p (a b) n"),
              MW[:, 1, 0:QT * D].rearrange("p (q n) -> p q n", q=QT)]
        BW = MW[:, 0, 0:ET * D].rearrange("p (k n) -> p k n", k=ET)
        LA = MW[:, 0, ET * D:ET * D + ET * MR].rearrange("p (k n) -> p k n", k=ET)
        LB = MW[:, 1, QT * D:QT * D + D]
        BB = SW[:, 0, :]
        DAS = [DA[:, 0], DA[:, 1]] + [
            MW[:, 1, a * 2 * L:(a + 1) * 2 * L].rearrange("p (m n) -> p m n", m=2) for a in range(2)]
        STAGED = [XN, MW[:, 1, 0:QT * D].rearrange("p (q n) -> p q n", q=QT)]
        XN1, XNT1 = [DEL[:, 0], DEL[:, 1]], [DU[:, 0], DU[:, 1]]
        MID, MIDT = BC[:, 0, 0:1].rearrange("p a (q n) -> p (a q) n", q=QT), BC[:, 1, 0]

        PS = ctx.enter_context(nc.psum_tensor("banks", [P, 8, 512], F32))
        PRE = [PS[:, 4], PS[:, 5]]
        AUX = [PS[:, 6], PS[:, 7]]
        MIDL = [bank[:, 0:2 * MR].rearrange("p (q m) -> p q m", m=MR) for bank in (PRE[0], AUX[0])]
        XT = flat(PS[:, 6:8]).rearrange("p (k r) -> p k r", k=ET)

        bc_d = nc.dram_tensor("bc_d", (STAGES, 2 * NS, L), F32, kind="Internal").ap()
        xn_d = nc.dram_tensor("xn_d", (NB * L, D), F32, kind="Internal").ap()
        xs_d = nc.dram_tensor("xs_d", (ZCH * ZROWS * P, D), F32, kind="Internal").ap()
        ys_d = nc.dram_tensor("ys_d", (NTILE * TILE, D), F32, kind="Internal").ap()
        xs_t = xs_d.rearrange("(j r p) n -> j p r n", p=P, r=RT)
        ys_t = ys_d.rearrange("(j r p) n -> j p r n", p=P, r=RT)
        xn_t = xn_d.rearrange("(b q p) n -> b p q n", p=P, q=QT)
        x_t = t["x"].rearrange("b (q p) n -> b p q n", p=P)
        out_t = t["out"].rearrange("b (q p) n -> b p q n", p=P)

        ld_chan, ld_proj, ld_small, ld_shared = sem("ld_chan"), sem("ld_proj"), sem("ld_small"), sem("ld_shared")
        ld_x = [sem(f"ld_x{b}") for b in range(NB)]
        ld_inw, ld_dtw, ld_ffn1 = sem("ld_inw"), sem("ld_dtw"), sem("ld_ffn1")
        ctx_in, bc_stored = sem("ctx_in"), sem("bc_stored")
        bc_in = [sem(f"bc_in{u}") for u in range(BODY)]
        xn_stored, zero_filled = sem("xn_stored"), sem("zero_filled")
        staged = [sem(f"staged{i}") for i in range(2)]
        scattered = [sem(f"scattered{i}") for i in range(2)]
        tw_in = [sem(f"tw_in{i}") for i in range(2)]
        xs_in, ys_stored, out_stored = sem("xs_in"), sem("ys_stored"), sem("out_stored")
        gathered = [sem(f"gathered{q}") for q in range(QT)]
        masks, zeroed, a_ready, tg_ready, counts = sem("masks"), sem("zeroed"), sem("a_ready"), sem("tg_ready"), sem("counts")
        inproj_done, tap_first, conv_step, u_ready = sem("inproj_done"), sem("tap_first"), sem("conv_step"), sem("u_ready")
        xproj_done, xdbl_ready, dt_done, dt_read = sem("xproj_done"), sem("xdbl_ready"), sem("dt_done"), sem("dt_read")
        e_ready, w1_ready, corr_ready, ln_ready = sem("e_ready"), sem("w1_ready"), sem("corr_ready"), sem("ln_ready")
        relu_added, bias_ready, bias_added = sem("relu_added"), sem("bias_ready"), sem("bias_added")
        delta_ready, seed_ready, du_ready = sem("delta_ready"), sem("seed_ready"), sem("du_ready")
        da_ready, mulb_done, scan_done = sem("da_ready"), sem("mulb_done"), sem("scan_done")
        mulc_done, w_free, seeded, y4_ready = sem("mulc_done"), sem("w_free"), sem("seeded"), sem("y4_ready")
        var_ready, std_step, std_ready, zn_ready, zs_ready = sem("var_ready"), sem("std_step"), sem("std_ready"), sem("zn_ready"), sem("zs_ready")
        yg_done, yt_done, xacc = sem("yg_done"), sem("yt_done"), sem("xacc")
        xn_ready, xnt_done, xnt_ready = sem("xn_ready"), sem("xnt_done"), sem("xnt_ready")
        router_done, sc_ready, ranked = sem("router_done"), sem("sc_ready"), sem("ranked")
        counted, counts_read, slots_ready = sem("counted"), sem("counts_read"), sem("slots_ready")
        shgu_done, shsil_ready, shh_ready, shdown_done, shacc = (
            sem("shgu_done"), sem("shsil_ready"), sem("shh_ready"), sem("shdown_done"), sem("shacc"))
        xt_done, xst_ready, gu_done, sil_ready, h_ready = (
            sem("xt_done"), sem("xst_ready"), sem("gu_done"), sem("sil_ready"), sem("h_ready"))
        hg_ready, y_done, yev, dve_step = sem("hg_ready"), sem("y_done"), sem("yev"), sem("dve_step")
        combined, exp_ready, shift_ready = sem("combined"), sem("exp_ready"), sem("shift_ready")
        mid_done, midg_ready, midt_done, midt_ready, ffn_done, x_final = (
            sem("mid_done"), sem("midg_ready"), sem("midt_done"), sem("midt_ready"), sem("ffn_done"), sem("x_final"))

        def pre_bank(s, et):
            return PS[:, et] if s == 0 else PRE[et % 2]

        def lay(s):
            return s // NB

        def yslot(s):
            return s % 2 if s < NB else s - NB

        def da_slots(s, turn):
            return 4 if s < NB or s == NB and turn < 2 else 2

        def bcast2(row):
            return row.unsqueeze(1).to_broadcast([P, 2, L])

        block = ctx.enter_context(nc.Block())

        @block.sync
        def _(sp):
            def load_ctx(s):
                if s > 0:
                    sp.wait_ge(inproj_done, ET * s)
                b = s % NB
                sp.dma_start(CTX[:, :, :], t["ctxT"].rearrange("(k p) n -> p k n", p=P)[:, :, b * L:(b + 1) * L]
                             ).then_inc(ctx_in, 16)

            def load_layer_in(layer):
                if layer:
                    sp.wait_ge(inproj_done, ET * NB)
                sp.dma_start(INW[:, :, :], t[f"in_wT{layer}"].rearrange("(k p) n -> p k n", p=P)).then_inc(ld_inw, 16)

            def load_layer_dt(layer):
                if layer:
                    sp.wait_ge(dt_done, ET * NB)
                sp.dma_start(DTW[2 * NS:, :], t[f"dtT{layer}"]).then_inc(ld_dtw, 16)

            def load_bc(s, i, u):
                n = i * BODY + u
                sp.wait_ge(mulc_done, i * (2 * BODY) + (HS * s + 2 * u + PRE_MULC - 2 * BODY + 2))
                src = bc_d[s].rearrange("(c n) l -> n c l", c=2)[bass.ds(n, 1), :, :]
                sp.dma_start(BC[:, u, :, :], src.rearrange("a c l -> (a c) l").partition_broadcast(P)
                             ).then_inc(bc_in[u], 16)

            def scan_loads(s, turn):
                for u in range(BODY):
                    load_bc(s, turn, u)

            def zero_fill(c):
                sp.dma_start(xs_rows[:, bass.ds(c * ZROWS, ZROWS), :],
                             YSB[:, 0:1, :].to_broadcast([P, ZROWS, D])).then_inc(zero_filled, 16)

            def load_tile_w(j, slot):
                sp.wait_ge(y_done, j * 2 + (PRE_Y - 2))
                e = sp.value_load(TE[0:1, bass.ds(j, 1)] if not isinstance(j, int) else TE[0:1, j:j + 1],
                                  min_val=0, max_val=NE - 1)
                sp.dma_start(MW[:, slot, :], t["moe_w"][bass.ds(e, 1), :, :].rearrange("a p n -> p (a n)")
                             ).then_inc(tw_in[slot], 16)

            def load_tile_x(j):
                sp.wait_ge(xt_done, j)
                src = xs_t[bass.ds(j, 1)] if not isinstance(j, int) else xs_t[j:j + 1]
                sp.dma_start(XS, src.rearrange("a p r n -> p (a r) n")).then_inc(xs_in, 16)

            def store_tile(j):
                sp.wait_ge(yev, j * 2 + (2 + PRE_YEV))
                dst = ys_t[bass.ds(j, 1)] if not isinstance(j, int) else ys_t[j:j + 1]
                sp.dma_start(dst.rearrange("a p r n -> p (a r) n"), YSB[:, :, :]).then_inc(ys_stored, 16)

            xs_rows = xs_d.rearrange("(c p) n -> p c n", p=P)

            load_layer_in(0)
            load_ctx(0)
            load_layer_dt(0)
            for layer in range(2):
                sp.dma_start(CH[:, layer], t[f"chan{layer}"].rearrange("(e p) n -> p e n", p=P)).then_inc(ld_chan, 16)
                sp.dma_start(XPW[:, layer], t[f"xprojT{layer}"].rearrange("(e p) n -> p e n", p=P)).then_inc(ld_proj, 16)
            sp.dma_start(TG[:, :], t["gates"][0, :].partition_broadcast(P)).then_inc(ld_small, 16)
            sp.dma_start(GW[:, :, :], t["gwT"].rearrange("(k p) n -> p k n", p=P)).then_inc(ld_small, 16)
            sp.dma_start(EB[:, :], t["ebias"][0, :].partition_broadcast(P)).then_inc(ld_small, 16)
            sp.dma_start(RB[:, :], t["rb"][0, :].partition_broadcast(P)).then_inc(ld_small, 16)
            for b in range(NB):
                sp.dma_start(X[:, b * QT:(b + 1) * QT, :], x_t[b]).then_inc(ld_x[b], 16)
            sp.dma_start(MW[:, 0, :], t["moe_w"][NE]).then_inc(ld_shared, 16)
            load_ctx(1)
            sp.wait_ge(zeroed, 5)
            for s in range(FIRST_B):
                if s == NB - 1:
                    load_layer_dt(1)
                sp.wait_ge(bc_stored, 16 * (s + 1))
                scan_loads(s, 0)
                load_ctx(s + 2)
                if s == NB - 2:
                    load_layer_in(1)
                if s < NB:
                    zero_fill(4 * s)
                with sp.Fori(1, TURNS - 1) as i:
                    scan_loads(s, i)
                    if s < NB:
                        zero_fill(i + 4 * s)
                if s < NB:
                    scan_loads(s, TURNS - 1)
                    zero_fill(4 * s + 3)
                if s:
                    sp.wait_ge(xn_ready, QT * s)
                    sp.dma_start(xn_t[s - 1], XN).then_inc(xn_stored, 16)
            sp.wait_ge(xnt_done, QT * NB)
            sp.wait_ge(xn_stored, 16 * NB)
            for b in range(NB):
                if b == 1:
                    sp.wait_ge(scan_done, HS * NB + 2 * HPT + PRE_SCAN)
                if b >= 2:
                    sp.wait_ge(scattered[b % 2], 16 * QT * TOPK)
                sp.dma_start(STAGED[b % 2], xn_t[b]).then_inc(staged[b % 2], 16)
                if b == 1:
                    load_bc(NB, TURNS - 1, 0)
                    load_bc(NB, TURNS - 1, 1)
                if b == 2:
                    load_bc(NB, TURNS - 1, 2)
                    load_bc(NB, TURNS - 1, 3)
            sp.wait_ge(slots_ready, 2)
            sp.wait_ge(shdown_done, QT * NB)
            load_tile_w(0, 0)
            for i in range(2):
                sp.wait_ge(scattered[i], 16 * 2 * QT * TOPK)
            load_tile_x(0)
            def tile_turn(s, i, last):
                for u in range(BODY):
                    j = i * BODY + (TPS * (s - FIRST_B) + u)
                    if not isinstance(j, int) or j < NTILE - 1:
                        load_tile_x(j + 1)
                        load_tile_w(j + 1, (u + 1) % 2)
                    if u:
                        store_tile(j - 1)
                    if u == 0:
                        load_bc(s, i, BODY - 1)
                    elif not last:
                        load_bc(s, i + 1, u - 1)
                if not isinstance(j, int) or j < NTILE:
                    store_tile(j)

            for s in range(FIRST_B, STAGES):
                sp.wait_ge(bc_stored, 16 * (s + 1))
                for u in range(BODY - 1):
                    load_bc(s, 0, u)
                with sp.Fori(0, TURNS - 1) as i:
                    tile_turn(s, i, False)
                if s + 2 < STAGES:
                    load_ctx(s + 2)
                tile_turn(s, TURNS - 1, True)
            sp.wait_ge(y_done, 2 * NTILE + PRE_Y)
            for i in range(2):
                sp.wait_ge(tw_in[i], 16 * ((NTILE - i) // 2))
            sp.dma_start(BW, t["base_wT"].rearrange("(k p) n -> p k n", p=P)).then_inc(ld_ffn1, 16)
            sp.dma_start(LA, t["loraA"].rearrange("(k p) n -> p k n", p=P)).then_inc(ld_ffn1, 16)
            sp.dma_start(LB, t["loraB"]).then_inc(ld_ffn1, 16)
            sp.wait_ge(du_ready, STAGES)
            sp.dma_start(BB, t["base_b"][0, :].partition_broadcast(P)).then_inc(ld_ffn1, 16)
            for b in range(NB - 1):
                sp.wait_ge(x_final, QT * (b + 1))
                sp.dma_start(out_t[b], X[:, b * QT:(b + 1) * QT, :]).then_inc(out_stored, 16)
            for q in range(QT):
                sp.wait_ge(x_final, QT * (NB - 1) + q + 1)
                sp.dma_start(out_t[NB - 1][:, q, :], X[:, (NB - 1) * QT + q, :]).then_inc(out_stored, 16)
            sp.wait_ge(out_stored, 16 * (NB - 1 + QT))

        @block.gpsimd
        def _(pool):
            pool.sem_inc(mulc_done, PRE_MULC)
            nc.gpsimd.memset(ID[:, :], 0.0).then_inc(masks, 1)
            nc.gpsimd.memset(ON[:, :], 1.0).then_inc(masks, 1)
            nc.gpsimd.memset(TRI[:, :, :], 1.0).then_inc(masks, 1)
            pool.wait_ge(masks, 3)
            nc.gpsimd.affine_select(out=ID[:, :], in_=ID[:, :], compare_op=ALU.not_equal, fill=1.0, base=0,
                                    pattern=[[-1, P]], channel_multiplier=1).then_inc(masks, 1)
            nc.gpsimd.affine_select(out=US[:, :], in_=ON[:, :], compare_op=ALU.is_gt, fill=0.0, base=0,
                                    pattern=[[1, P]], channel_multiplier=-1).then_inc(masks, 1)
            nc.gpsimd.affine_select(out=TRI[:, :, :], in_=TRI[:, :, :], compare_op=ALU.is_gt, fill=0.0, base=0,
                                    pattern=[[1, NE], [-1, NE]], channel_multiplier=0).then_inc(masks, 1)

            def mul_c(s, i, c):
                pool.wait_ge(scan_done, i * HPT + (HS * s + c + 1 + PRE_SCAN))
                nc.gpsimd.tensor_tensor(W[:, c % 4], W[:, c % 4], bcast2(BC[:, c // 2, 1, :]), ALU.mult).then_inc(mulc_done, 1)

            def step_round(s):
                dl, sw = flat(DEL[:, s % 2]), flat(SW[:, :, :])
                pool.wait_ge(e_ready, s + 1)
                pool.wait_ge(delta_ready, s)
                nc.gpsimd.tensor_scalar(sw, dl, 1.0, 1.0, ALU.mult, ALU.add).then_inc(w1_ready, 1)
                n = s - 2 if s < FIRST_B else s - 3
                pool.wait_ge(w1_ready, 2 * n + 1)
                nc.gpsimd.tensor_scalar(sw, sw, 1.0, -1.0, ALU.mult, ALU.add).then_inc(w1_ready, 1)
                pool.wait_ge(w1_ready, 2 * n + 2)
                nc.gpsimd.tensor_tensor(sw, dl, sw, ALU.subtract).then_inc(corr_ready, 1)

            def step_relu(s):
                sw = flat(SW[:, :, :])
                pool.wait_ge(corr_ready, s + 1)
                pool.wait_ge(dt_read, ET * (s + 1))
                nc.gpsimd.tensor_tensor(sw, sw, flat(Y[:, yslot(s)]), ALU.add).then_inc(relu_added, 1)

            def step_sum(s):
                dl = flat(DEL[:, s % 2])
                pool.wait_ge(relu_added, s + 1)
                pool.wait_ge(ln_ready, s + 1)
                nc.gpsimd.tensor_tensor(dl, dl, flat(SW[:, :, :]), ALU.add).then_inc(delta_ready, 1)

            for s in range(NB):
                with pool.Fori(0, TURNS - 1) as i:
                    for c in range(HPT):
                        mul_c(s, i, c)
                for c in range(HPT):
                    mul_c(s, TURNS - 1, c)
                    if c == 3 and s:
                        step_round(s + 1)
                    if c == 5 and s:
                        step_relu(s + 1)
                        step_sum(s + 1)
            with pool.Fori(0, 2) as i:
                for c in range(HPT):
                    mul_c(NB, i, c)
            pool.wait_ge(slots_ready, 2)
            pool.wait_ge(zero_filled, 16 * ZCH)
            for b in range(NB):
                pool.wait_ge(staged[b % 2], 16 * (b // 2 + 1))
                for q in range(QT):
                    for k in range(TOPK):
                        nc.gpsimd.indirect_dma_start(
                            out=xs_d, out_offset=bass.IndirectOffsetOnAxis(ap=SLU[:, k, b * QT + q:b * QT + q + 1], axis=0),
                            in_=STAGED[b % 2][:, q, :], in_offset=None).then_inc(scattered[b % 2], 16)
            for s in range(FIRST_B, STAGES):
                with pool.Fori(0, TURNS - 1) as i:
                    for c in range(HPT):
                        mul_c(s, i, c)
                for c in range(HPT):
                    mul_c(s, TURNS - 1, c)
                    if s + 1 < STAGES:
                        if c == 2:
                            step_round(s + 1)
                        if c == 3:
                            step_relu(s + 1)
                        if c == 4:
                            step_sum(s + 1)

            def add_bias(b):
                pool.wait_ge(bias_ready, 1)
                pool.wait_ge(xn_ready, QT * (NB + b + 1))
                xr = X[:, b * QT:(b + 1) * QT, :]
                nc.gpsimd.tensor_tensor(xr, xr, BB.unsqueeze(1).to_broadcast([P, QT, D]), ALU.add).then_inc(bias_added, 1)

            pool.wait_ge(w_free, HS * STAGES + PRE_W)
            pool.wait_ge(ys_stored, 16 * NTILE + PRE_YS)
            for g in range(NT):
                b, q = g // QT, g % QT
                if b:
                    pool.wait_ge(combined, TOPK * QT * (b - 1) + (TOPK - 1) * QT + q + 1)
                for k in range(TOPK):
                    nc.gpsimd.indirect_dma_start(
                        out=GK[q][:, k, :], out_offset=None, in_=ys_d,
                        in_offset=bass.IndirectOffsetOnAxis(ap=SLU[:, k, g:g + 1], axis=0)).then_inc(gathered[q], 16)
                if q == QT - 1 and b:
                    add_bias(b - 1)
            add_bias(NB - 1)

        @block.scalar
        def _(act):
            def conv_tap(s, pair):
                sl = s % 2
                if s >= 2:
                    act.wait_ge(scan_done, HS * (s - 1) + PRE_SCAN)
                for et in (2 * pair, 2 * pair + 1):
                    act.wait_ge(inproj_done, ET * s + et + 1)
                    nc.scalar.activation(DU[:, sl, et, :], pre_bank(s, et), ACT.Identity, bias=CH[:, lay(s), et, C_CB:C_CB + 1],
                                         scale=CH[:, lay(s), et, DC - 1:DC]).then_inc(tap_first, 1)

            def conv_silu(s):
                act.wait_ge(conv_step, 3 * ET * (s + 1))
                nc.scalar.activation(flat(DU[:, s % 2]), flat(DU[:, s % 2]), ACT.Silu).then_inc(u_ready, 1)

            def x_dbl(s):
                act.wait_ge(xproj_done, s + 1)
                if s:
                    act.wait_ge(bc_stored, 16 * s)
                    act.wait_ge(dt_done, ET * s)
                nc.scalar.activation(XDBL[:, :], PRE[0][0:DR + 2 * NS, :], ACT.Copy).then_inc(xdbl_ready, 1)
                act.wait_ge(xdbl_ready, s + 1)
                act.dma_start(bc_d[s], XDBL[0:2 * NS, :]).then_inc(bc_stored, 16)

            def step_abs(s, pair):
                if 2 <= s < NB + 2:
                    act.wait_ge(yt_done, QT * (s - 1))
                elif s == NB + 2:
                    act.wait_ge(scattered[0], 16 * 2 * QT * TOPK)
                elif s == NB + 3:
                    act.wait_ge(shgu_done, IT * NB)
                for et in (2 * pair, 2 * pair + 1):
                    act.wait_ge(dt_done, ET * s + et + 1)
                    bias = CH[:, lay(s), et, C_DB:C_DB + 1]
                    nc.scalar.activation(DEL[:, s % 2, et, :], pre_bank(s, et), ACT.Abs, bias=bias)
                    nc.scalar.activation(Y[:, yslot(s), et, :], pre_bank(s, et), ACT.Relu, bias=bias).then_inc(dt_read, 1)

            def step_exp(s):
                act.wait_ge(dt_read, ET * (s + 1))
                nc.scalar.activation(flat(DEL[:, s % 2]), flat(DEL[:, s % 2]), ACT.Exp, scale=-1.0).then_inc(e_ready, 1)

            def step_log(s):
                act.wait_ge(corr_ready, s + 1)
                nc.scalar.activation(flat(DEL[:, s % 2]), flat(DEL[:, s % 2]), ACT.Ln, bias=1.0).then_inc(ln_ready, 1)

            def seed(s):
                act.wait_ge(relu_added, s + 1)
                act.wait_ge(u_ready, s + 1)
                for et in range(ET):
                    ins = nc.scalar.activation(Y[:, yslot(s), et, :], DU[:, s % 2, et, :], ACT.Identity,
                                               scale=CH[:, lay(s), et, C_D:C_D + 1])
                ins.then_inc(seed_ready, 1)

            def z_gate(f):
                act.wait_ge(zn_ready, 2 * f + 1)
                b = f % NB
                for q in range(QT):
                    ins = nc.scalar.activation(ZS[:, q, :], X[:, b * QT + q, :], ACT.Silu, bias=NBI[:, q:q + 1],
                                               scale=RS[:, q:q + 1])
                ins.then_inc(zs_ready, 1)

            def norm(f, xn):
                act.wait_ge(zn_ready, 2 * f + 2)
                if 0 < f < NB:
                    act.wait_ge(xn_stored, 16 * f)
                for q in range(QT):
                    nc.scalar.activation(xn[:, q, :], X[:, (f % NB) * QT + q, :], ACT.Identity, bias=NBI[:, q:q + 1],
                                         scale=RS[:, q:q + 1]).then_inc(xn_ready, 1)

            def rstd(v):
                rstd_log(v)
                rstd_exp(v)

            def rstd_log(v):
                act.wait_ge(var_ready, v + 1)
                nc.scalar.activation(RS[:, :], RS[:, :], ACT.Ln).then_inc(std_step, 1)

            def rstd_exp(v):
                act.wait_ge(std_step, v + 1)
                nc.scalar.activation(RS[:, :], RS[:, :], ACT.Exp, scale=-0.5).then_inc(std_ready, 1)

            def decay(s, i, c):
                n = da_slots(s, i)
                act.wait_ge(scan_done, i * HPT + (HS * s + c + 1 + PRE_SCAN - n))
                for m in range(2):
                    et = 2 * (c % 2) + m
                    ins = nc.scalar.activation(DAS[c % n][:, m, 1:], DEL[:, s % 2, et, 1:], ACT.Exp,
                                               scale=AN[:, lay(s), et, bass.ds(i * BODY + c // 2, 1)])
                ins.then_inc(da_ready, 1)

            def norm_t(f, xnt, ks):
                for k in ks:
                    act.wait_ge(xnt_done, ET * f + k + 1)
                    if 0 < f < NB:
                        act.wait_ge(shgu_done, IT * f)
                    nc.scalar.activation(xnt[:, k, :], AUX[k % 2], ACT.Copy).then_inc(xnt_ready, 1)

            def route_exp(f):
                act.wait_ge(router_done, f + 1)
                nc.scalar.activation(SC[:, :, :], AUX[0][:, 0:QT * NE].rearrange("p (q e) -> p q e", e=NE), ACT.Exp,
                                     scale=-1.0).then_inc(sc_ready, 1)

            def shared_tanh(b, it):
                act.wait_ge(shgu_done, IT * b + it + 1)
                if b:
                    act.wait_ge(shdown_done, QT * b)
                nc.scalar.activation(HB[:, it, :], AUX[0], ACT.Tanh, scale=0.5).then_inc(shsil_ready, 1)

            def tile_rows(j):
                act.wait_ge(xt_done, j + 1)
                if not isinstance(j, int) or j:
                    act.wait_ge(gu_done, j * 2)
                nc.scalar.activation(flat(XST), flat(XT), ACT.Copy).then_inc(xst_ready, 1)

            def tile_tanh(j, u, it):
                act.wait_ge(gu_done, j * 2 + it + 1)
                act.wait_ge(y_done, j * 2 + (PRE_Y - 2))
                nc.scalar.activation(HT[:, u % 2, it, :], PS[:, it, 0:TILE], ACT.Tanh, scale=0.5).then_inc(sil_ready, 1)

            def tile_out(j):
                act.wait_ge(ys_stored, j * 16 + PRE_YS)
                for r in range(RT):
                    act.wait_ge(y_done, j * 2 + (r + 1 + PRE_Y))
                    nc.scalar.activation(YSB[:, r, :], PS[:, 2 + r], ACT.Copy).then_inc(yev, 1)

            act.wait_ge(ld_small, 16 * 4)
            nc.scalar.activation(TG[:, :], TG[:, :], ACT.Tanh).then_inc(tg_ready, 1)
            act.wait_ge(tg_ready, 1)
            nc.scalar.activation(TG[:, 2:3], TG[:, 2:3], ACT.Copy, scale=0.5).then_inc(tg_ready, 1)
            act.wait_ge(ld_chan, 32)
            for layer in range(2):
                nc.scalar.activation(AN[:, layer], CH[:, layer, :, C_A:C_A + NS], ACT.Exp).then_inc(a_ready, 1)
            act.wait_ge(a_ready, 2)
            nc.scalar.activation(AN[:, :, :, :], AN[:, :, :, :], ACT.Copy, scale=-1.0).then_inc(a_ready, 1)
            act.wait_ge(a_ready, 3)
            act.wait_ge(zeroed, 5)
            act.sem_inc(yev, PRE_YEV)
            act.sem_inc(ys_stored, PRE_YS)

            for pair in range(2):
                conv_tap(0, pair)
            conv_silu(0)
            x_dbl(0)
            for pair in range(2):
                step_abs(0, pair)
            step_exp(0)
            step_log(0)
            seed(0)
            for s in range(FIRST_B):
                f, p, g = s - 1, s + 1, s - 2
                act.wait_ge(delta_ready, s + 1)
                for c in range(HPT):
                    decay(s, 0, c)
                    if c == 1:
                        conv_tap(p, 0)
                        if g >= 0:
                            shared_tanh(g, 1)
                    if c == 3 and f >= 0:
                        z_gate(f)
                    if c == 6:
                        conv_tap(p, 1)
                if s == NB:
                    break
                conv_silu(p)
                with act.Fori(1, TURNS - 1) as i:
                    for c in range(HPT):
                        decay(s, i, c)
                x_dbl(p)
                if f >= 0:
                    rstd(2 * f + 1)
                for c in range(HPT):
                    decay(s, TURNS - 1, c)
                    if c == 1 and f >= 0:
                        norm(f, XN)
                    if c == 2:
                        step_abs(p, 0)
                    if c == 3:
                        step_abs(p, 1)
                        if f >= 0:
                            norm_t(f, XNT, (0, 1))
                    if c == 4:
                        if f >= 0:
                            norm_t(f, XNT, (2, 3))
                        step_exp(p)
                    if c == 5:
                        if f >= 0:
                            route_exp(f)
                        rstd_log(2 * s)
                        step_log(p)
                        rstd_exp(2 * s)
                    if c == 6 and f >= 0:
                        shared_tanh(f, 0)
                seed(p)
            s, f, p = NB, NB - 1, NB + 1
            rstd(2 * f + 1)
            for c in range(HPT):
                decay(s, 1, c)
                if c == 1:
                    norm(f, XN)
                if c == 3:
                    norm_t(f, XNT, (0, 1))
                if c == 4:
                    norm_t(f, XNT, (2, 3))
            route_exp(f)
            conv_silu(p)
            x_dbl(p)
            for c in range(HPT):
                decay(s, 2, c)
                if c == 1:
                    shared_tanh(f, 0)
                if c == 3:
                    step_abs(p, 0)
                if c == 5:
                    shared_tanh(f, 1)
            step_abs(p, 1)
            step_exp(p)
            for c in range(HPT):
                decay(s, 3, c)
                if c == 2:
                    step_log(p)
                if c == 5:
                    seed(p)
            act.wait_ge(w_free, HS * FIRST_B + PRE_W)
            nc.scalar.activation(flat(Y[:, 0]), flat(PS[:, 0:4]), ACT.Copy).then_inc(y4_ready, 1)
            tile_rows(0)

            def tile_turn(s, i, prep):
                for u in range(BODY):
                    j = i * BODY + (TPS * (s - FIRST_B) + u)
                    if prep == 2 and u == 0:
                        x_dbl(s + 1)
                    more = not isinstance(j, int) or j < NTILE - 1
                    here = more or j < NTILE
                    decay(s, i, 2 * u)
                    if prep == 1 and u in (0, 2):
                        conv_tap(s + 1, u // 2)
                    if here:
                        tile_tanh(j, u, 0)
                    decay(s, i, 2 * u + 1)
                    if here:
                        tile_tanh(j, u, 1)
                    if prep == 2 and u == 0:
                        step_abs(s + 1, 0)
                    if more:
                        tile_rows(j + 1)
                    if prep == 1 and u == 3:
                        conv_silu(s + 1)
                    if prep == 2 and u == 3:
                        seed(s + 1)
                    if here:
                        tile_out(j)
                    if prep == 2 and u == 0:
                        step_abs(s + 1, 1)
                        step_exp(s + 1)
                    if prep == 2 and u == 2:
                        step_log(s + 1)

            for s in range(FIRST_B, STAGES):
                act.wait_ge(delta_ready, s + 1)
                prep = s + 1 < STAGES
                with act.Fori(0, TURNS - 2 if prep else TURNS - 1) as i:
                    tile_turn(s, i, 0)
                if prep:
                    tile_turn(s, TURNS - 2, 1)
                tile_turn(s, TURNS - 1, 2 if prep else 0)
            act.wait_ge(ld_ffn1, 16 * 4)
            nc.scalar.activation(BB, BB, ACT.Copy, scale=TG[:, 3:4]).then_inc(bias_ready, 1)
            for b in range(NB + 1):
                f, l = NB + b, b - 1
                if b < NB:
                    rstd(2 * f)
                if l >= 0:
                    act.wait_ge(shift_ready, l + 1)
                    nc.scalar.activation(SM[:, 1, 0:QT * E1], SM[:, 0, 0:QT * E1], ACT.Exp).then_inc(exp_ready, 1)
                if b < NB:
                    z_gate(f)
                if l >= 0:
                    act.wait_ge(midt_done, l + 1)
                    if l:
                        act.wait_ge(ffn_done, QT * l)
                    nc.scalar.activation(MIDT, PRE[1], ACT.Copy).then_inc(midt_ready, 1)
                if b < NB:
                    rstd(2 * f + 1)
                    norm(f, XN1[b % 2])
                    norm_t(f, XNT1[b % 2], range(ET))

        @block.tensor
        def _(pe):
            def in_proj(s, pair):
                pe.wait_ge(ctx_in, 16 * (s + 1))
                pe.wait_ge(ld_inw, 16 * (lay(s) + 1))
                if s:
                    pe.wait_ge(dt_read, ET * s)
                for et in (2 * pair, 2 * pair + 1):
                    if pair and s:
                        pe.wait_ge(conv_step, 3 * ET * s + 4 + et - 1)
                    for k in range(KC):
                        mm = nc.tensor.matmul(pre_bank(s, et), INW[:, k, et * P:(et + 1) * P], CTX[:, k, :],
                                              start=(k == 0), stop=(k == KC - 1))
                    mm.then_inc(inproj_done, 1)

            def x_proj(s):
                pe.wait_ge(u_ready, s + 1)
                pe.wait_ge(ld_proj, 32)
                for et in range(ET):
                    mm = nc.tensor.matmul(PRE[0][0:DR + 2 * NS, :], XPW[:, lay(s), et, :], DU[:, s % 2, et, :],
                                          start=(et == 0), stop=(et == ET - 1))
                mm.then_inc(xproj_done, 1)

            def dt_proj(s, pair):
                pe.wait_ge(xdbl_ready, s + 1)
                pe.wait_ge(ld_dtw, 16 * (lay(s) + 1))
                for et in (2 * pair, 2 * pair + 1):
                    if pair and s:
                        pe.wait_ge(dt_read, ET * s + et - 1)
                    nc.tensor.matmul(pre_bank(s, et), DTW[2 * NS:, et * P:(et + 1) * P], XDBL[2 * NS:, :],
                                     start=True, stop=True).then_inc(dt_done, 1)

            def sum_skip(s):
                pe.wait_ge(seed_ready, s + 1)
                for et in range(ET):
                    nc.tensor.matmul(PS[:, et], ID[:, :], Y[:, yslot(s), et, :], start=True, stop=True)

            def sum_state(s, i, c):
                pe.wait_ge(mulc_done, i * HPT + (HS * s + c + 1 + PRE_MULC))
                for m in range(2):
                    mm = nc.tensor.matmul(PS[:, 2 * (c % 2) + m], ID[:, :], W[:, c % 4, m, :],
                                          start=False, stop=True, skip_group_check=True)
                mm.then_inc(w_free, 1)

            def y_transposes(f, y, lts):
                pe.wait_ge(yg_done, f + 1)
                for lt in lts:
                    if lt >= 2:
                        pe.wait_ge(xacc, QT * f + lt - 1)
                    for et in range(ET):
                        mm = nc.tensor.transpose(AUX[lt % 2][:, et * P:(et + 1) * P], y[:, et, lt * P:(lt + 1) * P], ID[:, :])
                    mm.then_inc(yt_done, 1)

            def norm_transposes(f, xn, ks):
                pe.wait_ge(xn_ready, QT * (f + 1))
                for k in ks:
                    if k >= 2:
                        pe.wait_ge(xnt_ready, ET * f + k - 1)
                    for q in range(QT):
                        mm = nc.tensor.transpose(AUX[k % 2][:, q * P:(q + 1) * P], xn[:, q, k * P:(k + 1) * P], ID[:, :])
                    mm.then_inc(xnt_done, 1)

            def route(f):
                pe.wait_ge(xnt_ready, ET * (f + 1))
                for q in range(QT):
                    for k in range(ET):
                        mm = nc.tensor.matmul(AUX[0][:, q * NE:(q + 1) * NE], XNT[:, k, q * P:(q + 1) * P], GW[:, k, :],
                                              start=(k == 0), stop=(k == ET - 1))
                mm.then_inc(router_done, 1)

            def shared_in(b, it):
                pe.wait_ge(ld_shared, 16)
                if b == NB - 1 and it == 0:
                    pe.wait_ge(counts_read, 1)
                elif it:
                    pe.wait_ge(shh_ready, IT * b + it)
                else:
                    pe.wait_ge(sc_ready, b + 1)
                for g in range(2):
                    for k in range(ET):
                        at = g * WGU + k * INNER + it * P
                        mm = nc.tensor.matmul(AUX[g], MW[:, 0, at:at + P], XNT[:, k, :], start=(k == 0), stop=(k == ET - 1))
                mm.then_inc(shgu_done, 1)

            def shared_out(b, qs):
                pe.wait_ge(shh_ready, IT * (b + 1))
                for q in qs:
                    for it in range(IT):
                        at = 2 * WGU + it * D
                        mm = nc.tensor.matmul(AUX[q % 2], HB[:, it, q * P:(q + 1) * P], MW[:, 0, at:at + D],
                                              start=(it == 0), stop=(it == IT - 1))
                    mm.then_inc(shdown_done, 1)

            def tile_transposes(j):
                pe.wait_ge(xs_in, j * 16 + 16)
                if not isinstance(j, int) or j:
                    pe.wait_ge(xst_ready, j)
                for k in range(ET):
                    for r in range(RT):
                        mm = nc.tensor.transpose(XT[:, k, r * P:(r + 1) * P], XS[:, r, k * P:(k + 1) * P], ID[:, :])
                mm.then_inc(xt_done, 1)

            def tile_in(j, u, half):
                pe.wait_ge(tw_in[u % 2], half * 16 + 16)
                pe.wait_ge(xst_ready, j + 1)
                for it in range(IT):
                    pe.wait_ge(h_ready, j * 2 + (it - 1 + PRE_H))
                    for g in range(2):
                        for k in range(ET):
                            at = g * WGU + k * INNER + it * P
                            mm = nc.tensor.matmul(PS[:, it, g * TILE:(g + 1) * TILE], MW[:, u % 2, at:at + P], XST[:, k, :],
                                                  start=(k == 0), stop=(k == ET - 1))
                    mm.then_inc(gu_done, 1)

            def tile_out(j, u):
                for it in range(IT):
                    pe.wait_ge(h_ready, j * 2 + (it + 1 + PRE_H))
                    for r in range(RT):
                        if it == 0:
                            pe.wait_ge(yev, j * 2 + (r - 1 + PRE_YEV))
                        at = 2 * WGU + it * D
                        mm = nc.tensor.matmul(PS[:, 2 + r], HT[:, u % 2, it, r * P:(r + 1) * P], MW[:, u % 2, at:at + D],
                                              start=(it == 0), stop=(it == IT - 1))
                        if it == IT - 1:
                            mm.then_inc(y_done, 1)

            pe.sem_inc(w_free, PRE_W)
            pe.sem_inc(y_done, PRE_Y)
            pe.wait_ge(masks, 6)
            for pair in range(2):
                in_proj(0, pair)
            x_proj(0)
            for pair in range(2):
                dt_proj(0, pair)
            in_proj(1, 0)
            for s in range(FIRST_B):
                f, p, g = s - 1, s + 1, s - 2
                if g >= 0:
                    shared_out(g, (0, 1))
                if f >= 0:
                    pe.wait_ge(yg_done, f + 1)
                sum_skip(s)
                for c in range(HPT):
                    sum_state(s, 0, c)
                    if c == 1 and f >= 0:
                        if g >= 0:
                            pe.wait_ge(shacc, QT * g + 2)
                        y_transposes(f, Y[:, yslot(f)], (0, 1))
                    if c == 2 and f >= 0:
                        y_transposes(f, Y[:, yslot(f)], (2, 3))
                    if c == 3:
                        in_proj(p, 1)
                    if c == 5 and g >= 0:
                        pe.wait_ge(xacc, QT * (f + 1))
                        shared_out(g, (2, 3))
                if s == NB:
                    break
                x_proj(p)
                with pe.Fori(1, TURNS - 1) as i:
                    for c in range(HPT):
                        sum_state(s, i, c)
                dt_proj(p, 0)
                for c in range(HPT):
                    sum_state(s, TURNS - 1, c)
                    if c == 1:
                        dt_proj(p, 1)
                    if c == 1 and f >= 0:
                        if g >= 0:
                            pe.wait_ge(shacc, QT * (g + 1))
                        norm_transposes(f, XN, (0, 1))
                    if c == 2 and f >= 0:
                        norm_transposes(f, XN, (2, 3))
                    if c == 3 and f >= 0:
                        route(f)
                    if c == 3 and f >= 0:
                        shared_in(f, 0)
                    if c == 4:
                        in_proj(p + 1, 0)
                    if c == 5 and f >= 0:
                        shared_in(f, 1)
            s, f, p = NB, NB - 1, NB + 1
            for c in range(HPT):
                sum_state(s, 1, c)
                if c == 1:
                    pe.wait_ge(shacc, QT * f)
                    norm_transposes(f, XN, (0, 1))
                if c == 2:
                    norm_transposes(f, XN, (2, 3))
                if c == 3:
                    route(f)
            pe.wait_ge(ranked, NB)
            sel = SEL[:, :, :].rearrange("p t e -> p (t e)")
            nc.tensor.matmul(AUX[0][:, 0:NT * NE], US[:, :], sel, start=True, stop=True)
            nc.tensor.matmul(AUX[1][:, 0:NT * NE], ON[:, :], sel, start=True, stop=True).then_inc(counted, 1)
            x_proj(p)
            shared_in(f, 0)
            dt_proj(p, 0)
            for c in range(HPT):
                sum_state(s, 2, c)
                if c == 2:
                    shared_in(f, 1)
                if c == 4:
                    dt_proj(p, 1)
                if c == 6:
                    shared_out(f, (0, 1))
            for c in range(HPT):
                sum_state(s, 3, c)
                if c == 3:
                    pe.wait_ge(shacc, QT * f + 2)
                    shared_out(f, (2, 3))
            pe.wait_ge(shacc, QT * NB)
            tile_transposes(0)
            pe.wait_ge(y4_ready, 1)

            def tile_turn(s, i, prep):
                for u in range(BODY):
                    j = i * BODY + (TPS * (s - FIRST_B) + u)
                    if isinstance(j, int) and j >= NTILE:
                        break
                    if prep == 1 and u == 0:
                        in_proj(s + 1, 0)
                    tile_in(j, u, i * 2 + (TPS // 2 * (s - FIRST_B) + u // 2))
                    if prep == 2 and u == 0:
                        dt_proj(s + 1, 0)
                    if not isinstance(j, int) or j < NTILE - 1:
                        tile_transposes(j + 1)
                    tile_out(j, u)
                    if prep == 1 and u == 1:
                        in_proj(s + 1, 1)
                    if prep == 1 and u == 3:
                        x_proj(s + 1)
                    if prep == 2 and u == 0:
                        dt_proj(s + 1, 1)

            for s in range(FIRST_B, STAGES):
                prep = s + 1 < STAGES
                with pe.Fori(0, TURNS - 2 if prep else TURNS - 1) as i:
                    tile_turn(s, i, 0)
                if prep:
                    tile_turn(s, TURNS - 2, 1)
                tile_turn(s, TURNS - 1, 2 if prep else 0)
            pe.wait_ge(ld_ffn1, 16 * 4)
            pe.wait_ge(xst_ready, NTILE)
            pe.wait_ge(yev, 2 * NTILE + PRE_YEV)

            def base(b, q):
                xnt = XNT1[b % 2]
                for k in range(ET):
                    nc.tensor.matmul(PS[:, q], xnt[:, k, q * P:(q + 1) * P], BW[:, k, :], start=(k == 0),
                                     stop=(k == ET - 1))

            for b in range(NB + 1):
                f, l = NB + b, b - 1
                if l >= 0:
                    if l:
                        pe.wait_ge(x_final, QT * l)
                    base(l, 0)
                    base(l, 1)
                    base(l, 2)
                    pe.wait_ge(midg_ready, l + 1)
                    for q in range(QT):
                        mm = nc.tensor.transpose(PRE[1][:, q * P:(q + 1) * P], MID[:, q, :], ID[:, :])
                    mm.then_inc(midt_done, 1)
                if b < NB:
                    y_transposes(f, Y[:, b], (0, 1))
                    y_transposes(f, Y[:, b], (2, 3))
                if l >= 0:
                    base(l, 3)
                    pe.wait_ge(midt_ready, l + 1)
                    for q in range(QT):
                        nc.tensor.matmul(PS[:, q], MIDT[:, q * P:(q + 1) * P], LB, start=False, stop=True,
                                         skip_group_check=True).then_inc(ffn_done, 1)
                if b < NB:
                    xnt = XNT1[b % 2]
                    norm_transposes(f, XN1[b % 2], range(ET))
                    pe.wait_ge(xnt_ready, ET * (f + 1))
                    for q in range(QT):
                        for k in range(ET):
                            mm = nc.tensor.matmul(MIDL[q // 2][:, q % 2, :], xnt[:, k, q * P:(q + 1) * P], LA[:, k, :],
                                                  start=(k == 0), stop=(k == ET - 1))
                    mm.then_inc(mid_done, 1)

        @block.vector
        def _(dve):
            steps = [0]

            def link(ins):
                steps[0] += 1
                ins.then_inc(dve_step, 1)
                dve.wait_ge(dve_step, steps[0])

            def conv(s, pair, taps=range(DC - 1)):
                sl = s % 2
                for m in taps:
                    j = DC - 2 - m
                    for h in range(2):
                        et, sh = 2 * pair + h, DC - 1 - j
                        if m == 0:
                            dve.wait_ge(tap_first, ET * s + et + 1)
                        else:
                            dve.wait_ge(conv_step, 3 * ET * s + 6 * pair + 2 * (m - 1) + h + 1)
                        nc.vector.scalar_tensor_tensor(
                            out=DU[:, sl, et, sh:], in0=pre_bank(s, et)[:, 0:L - sh], scalar=CH[:, lay(s), et, j:j + 1],
                            in1=DU[:, sl, et, sh:], op0=ALU.mult, op1=ALU.add).then_inc(conv_step, 1)

            def step_round(s):
                dl, sw = flat(DEL[:, s % 2]), flat(SW[:, :, :])
                dve.wait_ge(e_ready, s + 1)
                if s:
                    dve.wait_ge(delta_ready, s)
                link(nc.vector.tensor_scalar(sw, dl, 1.0, -1.0, ALU.add, ALU.add))
                nc.vector.tensor_tensor(sw, dl, sw, ALU.subtract).then_inc(corr_ready, 1)

            def step_relu(s):
                sw = flat(SW[:, :, :])
                dve.wait_ge(corr_ready, s + 1)
                nc.vector.tensor_tensor(sw, sw, flat(Y[:, yslot(s)]), ALU.add).then_inc(relu_added, 1)

            def step_sum(s):
                dl = flat(DEL[:, s % 2])
                dve.wait_ge(relu_added, s + 1)
                dve.wait_ge(ln_ready, s + 1)
                nc.vector.tensor_tensor(dl, dl, flat(SW[:, :, :]), ALU.add).then_inc(delta_ready, 1)

            def delta_u(s):
                dve.wait_ge(delta_ready, s + 1)
                dve.wait_ge(seed_ready, s + 1)
                dve.wait_ge(xproj_done, s + 1)
                nc.vector.tensor_tensor(flat(DU[:, s % 2]), flat(DU[:, s % 2]), flat(DEL[:, s % 2]),
                                        ALU.mult).then_inc(du_ready, 1)

            def stats(b):
                for q in range(QT):
                    ins = nc.vector.bn_stats(ST[:, q, :], X[:, b * QT + q, :])
                link(ins)
                for q in range(QT):
                    ins = nc.vector.bn_aggr(MV[:, q, :], ST[:, q, :])
                link(ins)
                nc.vector.tensor_scalar(RS[:, :], MV[:, :, 1], EPS, None, ALU.add).then_inc(var_ready, 1)

            def scan_gate(f, y, src):
                dve.wait_ge(zs_ready, f + 1)
                nc.vector.tensor_tensor(flat(y), src, flat(ZS[:, :, :]), ALU.mult).then_inc(yg_done, 1)

            def scan_add(f, lts, gate):
                for lt in lts:
                    dve.wait_ge(yt_done, QT * f + lt + 1)
                    xr = X[:, (f % NB) * QT + lt, :]
                    nc.vector.scalar_tensor_tensor(out=xr, in0=AUX[lt % 2], scalar=TG[:, gate:gate + 1], in1=xr, op0=ALU.mult,
                                                   op1=ALU.add).then_inc(xacc, 1)

            def norm_bias(v):
                dve.wait_ge(std_ready, v + 1)
                nc.vector.scalar_tensor_tensor(out=NBI[:, :], in0=MV[:, :, 0], scalar=-1.0, in1=RS[:, :], op0=ALU.mult,
                                               op1=ALU.mult).then_inc(zn_ready, 1)

            def rank_of(out, m, n, tri, s1=T1, s2=T2):
                a = s1[:, 0:QT * n * n].rearrange("p (q e f) -> p q e f", q=QT, e=n)
                c = s2[:, 0:QT * n * n].rearrange("p (q e f) -> p q e f", q=QT, e=n)
                other = m.unsqueeze(2).to_broadcast([P, QT, n, n])
                own = m.unsqueeze(3).to_broadcast([P, QT, n, n])
                nc.vector.tensor_tensor(a, other, own, ALU.is_gt)
                link(nc.vector.tensor_tensor(c, other, own, ALU.is_equal))
                link(nc.vector.tensor_tensor(c, c, tri.unsqueeze(1).to_broadcast([P, QT, n, n]), ALU.mult))
                link(nc.vector.tensor_tensor(a, a, c, ALU.add))
                link(nc.vector.reduce_sum(out, a, AX.X))

            def route(b):
                q16 = lambda i: SM[:, i, :].rearrange("p (q e) -> p q e", e=NE)
                dve.wait_ge(sc_ready, b + 1)
                dve.wait_ge(ld_small, 16 * 4)
                link(nc.vector.tensor_scalar(SC[:, :, :], SC[:, :, :], 1.0, None, ALU.add))
                link(nc.vector.reciprocal(SC[:, :, :], SC[:, :, :]))
                biased = q16(0)
                link(nc.vector.tensor_tensor(biased, SC[:, :, :], EB[:, :].unsqueeze(1).to_broadcast([P, QT, NE]), ALU.add))
                pairs = SM[:, 0, :].rearrange("p (n two) -> p n two", two=2)
                mx, mn = SM[:, 1, 0:32], SM[:, 2, 0:32]
                nc.vector.tensor_tensor(mx, pairs[:, :, 0], pairs[:, :, 1], ALU.max)
                link(nc.vector.tensor_tensor(mn, pairs[:, :, 0], pairs[:, :, 1], ALU.min))
                mxp, mnp = [v.rearrange("p (n two) -> p n two", two=2) for v in (mx, mn)]
                top, lo, hi2 = SM[:, 3, 0:16], SM[:, 3, 16:32], SM[:, 3, 32:48]
                nc.vector.tensor_tensor(top, mxp[:, :, 0], mxp[:, :, 1], ALU.max)
                nc.vector.tensor_tensor(lo, mxp[:, :, 0], mxp[:, :, 1], ALU.min)
                link(nc.vector.tensor_tensor(hi2, mnp[:, :, 0], mnp[:, :, 1], ALU.max))
                link(nc.vector.tensor_tensor(lo, lo, hi2, ALU.max))
                gs = SM[:, 4, 0:16]
                link(nc.vector.tensor_tensor(gs, top, lo, ALU.add))
                gr = SM[:, 4, 16:32].rearrange("p (q g) -> p q g", g=NGRP)
                rank_of(gr, gs.rearrange("p (q g) -> p q g", g=NGRP), NGRP, TRI[:, 0:NGRP, 0:NGRP])
                keep, low = SM[:, 4, 32:48], SM[:, 4, 48:64]
                link(nc.vector.tensor_scalar(keep, SM[:, 4, 16:32], float(GKEEP), None, ALU.is_lt))
                link(nc.vector.tensor_scalar(low, keep, BIG, -BIG, ALU.mult, ALU.add))
                masked = q16(5)
                by_group = lambda v: v.unsqueeze(2).to_broadcast([P, QT * NGRP, GSZ])
                g3 = lambda i: SM[:, i, :].rearrange("p (g e) -> p g e", e=GSZ)
                link(nc.vector.tensor_tensor(g3(5), g3(0), by_group(keep), ALU.mult))
                link(nc.vector.tensor_tensor(g3(5), g3(5), by_group(low), ALU.add))
                rk, sel, cw = (v[:, b * QT:(b + 1) * QT, :] for v in (RK, SEL, CW))
                rank_of(rk, masked, NE, TRI[:, :, :])
                link(nc.vector.tensor_scalar(sel, rk, float(TOPK), None, ALU.is_lt))
                link(nc.vector.tensor_tensor(cw, SC[:, :, :], sel, ALU.mult))
                tot = SM[:, 6, 0:QT]
                link(nc.vector.reduce_sum(tot, cw, AX.X))
                link(nc.vector.tensor_scalar(tot, tot, 1e-20, None, ALU.add))
                link(nc.vector.reciprocal(tot, tot))
                link(nc.vector.tensor_scalar(tot, tot, SCALING, TG[:, 2:3], ALU.mult, ALU.mult))
                nc.vector.tensor_tensor(cw, cw, tot.unsqueeze(2).to_broadcast([P, QT, NE]), ALU.mult).then_inc(ranked, 1)

            def slots():
                n2 = NT * NE
                by_e = lambda a: T1[:, a * n2:(a + 1) * n2].rearrange("p (e t) -> p e t", e=NE)
                ct, ci, ex = by_e(0), by_e(1), by_e(2)
                reset = T1[:, 3 * n2:4 * n2]
                count, rows = SM[:, 6, 0:NTILE], SM[:, 5, 0:8]
                dve.wait_ge(ranked, NB)
                link(nc.vector.tensor_tensor_scan(count, ON[:, 0:NTILE], ON[:, 0:NTILE], 0.0, ALU.mult, ALU.add))
                link(nc.vector.tensor_scalar(rows, count[:, 0:8], -1.0, float(TILE), ALU.add, ALU.mult))
                link(nc.vector.memset(reset, 1.0))
                nc.vector.memset(reset.rearrange("p (e t) -> p e t", e=NE)[:, :, 0:1], 0.0)
                dve.wait_ge(counted, 1)
                before = T2[:, 3 * n2:4 * n2]
                nc.vector.tensor_copy(before, AUX[0][:, 0:n2])
                nc.vector.tensor_copy(ct, AUX[1][:, 0:n2].rearrange("p (t e) -> p e t", e=NE)).then_inc(counts_read, 1)
                dve.wait_ge(counts_read, 1)
                link(nc.vector.tensor_tensor_scan(T1[:, n2:2 * n2], reset, T1[:, 0:n2], 0.0, ALU.mult, ALU.add))
                cnt = ci[:, :, NT - 1]
                full = T2[:, 0:NE * 8].rearrange("p (e m) -> p e m", m=8)
                link(nc.vector.tensor_tensor(full, cnt.unsqueeze(2).to_broadcast([P, NE, 8]),
                                             rows.unsqueeze(1).to_broadcast([P, NE, 8]), ALU.is_gt))
                tiles, upto, first = SM[:, 0, 0:NE], SM[:, 0, NE:2 * NE], SM[:, 0, 2 * NE:3 * NE]
                link(nc.vector.reduce_sum(tiles, full, AX.X))
                link(nc.vector.tensor_tensor_scan(upto, ON[:, 0:NE], tiles, 0.0, ALU.mult, ALU.add))
                link(nc.vector.tensor_tensor(first, upto, tiles, ALU.subtract))
                link(nc.vector.tensor_scalar(first, first, float(TILE), None, ALU.mult))
                link(nc.vector.tensor_tensor(ex, ci, ct, ALU.subtract))
                link(nc.vector.tensor_tensor(ex, ex, first.unsqueeze(2).to_broadcast([P, NE, NT]), ALU.add))
                slot = T2[:, 0:n2].rearrange("p (t e) -> p t e", e=NE)
                link(nc.vector.tensor_tensor(slot, before.rearrange("p (t e) -> p t e", e=NE),
                                             ex.rearrange("p e t -> p t e"), ALU.add))
                slk = SM[:, 1:1 + TOPK, 0:NT]
                parts = [T1[:, k * n2:(k + 1) * n2].rearrange("p (t e) -> p t e", e=NE) for k in range(TOPK)]

                def of_rank(out, v):
                    for k in range(TOPK):
                        ins = nc.vector.scalar_tensor_tensor(out=parts[k], in0=RK[:, :, :], scalar=float(k), in1=v,
                                                             op0=ALU.is_equal, op1=ALU.mult)
                    link(ins)
                    for k in range(TOPK):
                        ins = nc.vector.reduce_sum(out[:, k, :], parts[k], AX.X)
                    link(ins)

                of_rank(slk, slot)
                nc.vector.tensor_copy(SLU[:, :, :], slk).then_inc(slots_ready, 1)
                ends = T1[:, 0:(NTILE) * NE].rearrange("p (j e) -> p j e", e=NE)
                link(nc.vector.tensor_tensor(ends, upto.unsqueeze(1).to_broadcast([P, NTILE, NE]),
                                             count.unsqueeze(2).to_broadcast([P, NTILE, NE]), ALU.is_lt))
                num = SM[:, 7, 0:NTILE]
                link(nc.vector.reduce_sum(num, ends, AX.X))
                nc.vector.tensor_scalar(TE[:, :], num, float(NE - 1), None, ALU.min).then_inc(slots_ready, 1)
                dve.wait_ge(slots_ready, 2)
                of_rank(CWK, CW[:, :, :])

            def mul_b(s, i, c):
                u, h = c // 2, c % 2
                if h == 0:
                    dve.wait_ge(bc_in[u], i * 16 + 16 * (NS // BODY * s + 1))
                dve.wait_ge(w_free, i * (2 * BODY) + (HS * s + c + PRE_W - 3))
                nc.vector.tensor_tensor(W[:, c % 4], DU[:, s % 2, 2 * h:2 * h + 2, :], bcast2(BC[:, u, 0, :]),
                                        ALU.mult).then_inc(mulb_done, 1)

            def scan(s, i, c):
                dve.wait_ge(mulb_done, i * (2 * BODY) + (HS * s + c + 1))
                dve.wait_ge(da_ready, i * (2 * BODY) + (HS * s + c + 1))
                nc.vector.tensor_tensor_scan(flat(W[:, c % 4]), flat(DAS[c % da_slots(s, i)]), flat(W[:, c % 4]), 0.0, ALU.mult,
                                             ALU.add).then_inc(scan_done, 1)

            def mul_c(s, i, c):
                dve.wait_ge(scan_done, i * HPT + (HS * s + c + 1 + PRE_SCAN))
                dve.wait_ge(mulc_done, i * HPT + (HS * s + c + PRE_MULC))
                nc.vector.tensor_tensor(W[:, c % 4], W[:, c % 4], bcast2(BC[:, c // 2, 1, :]), ALU.mult).then_inc(mulc_done, 1)

            def add_y(s, i, c):
                dve.wait_ge(mulc_done, i * (2 * BODY) + (HS * s + c + 1 + PRE_MULC))
                dve.wait_ge(w_free, i * (2 * BODY) + (HS * s + c - 1 + PRE_W))
                y = Y[:, yslot(s), 2 * (c % 2):2 * (c % 2) + 2, :]
                nc.vector.tensor_tensor(y, y, W[:, c % 4], ALU.add).then_inc(w_free, 1)

            def half(s, i, c):
                if c + 1 < HPT:
                    mul_b(s, i, c + 1)
                scan(s, i, c)

            def tile_hidden(j, u, it):
                h = HT[:, u % 2, it, :]
                dve.wait_ge(sil_ready, j * 2 + it + 1)
                nc.vector.scalar_tensor_tensor(out=h, in0=h, scalar=1.0, in1=PS[:, it, 0:TILE], op0=ALU.add,
                                               op1=ALU.mult).then_inc(hg_ready, 1)
                dve.wait_ge(hg_ready, j * 2 + it + 1)
                nc.vector.tensor_tensor(h, h, PS[:, it, TILE:2 * TILE], ALU.mult).then_inc(h_ready, 1)

            def shared_hidden(b, it):
                h = HB[:, it, :]
                dve.wait_ge(shsil_ready, IT * b + it + 1)
                link(nc.vector.scalar_tensor_tensor(out=h, in0=h, scalar=1.0, in1=AUX[0], op0=ALU.add,
                                                    op1=ALU.mult))
                nc.vector.tensor_tensor(h, h, AUX[1], ALU.mult).then_inc(shh_ready, 1)

            def shared_add(b, qs):
                for q in qs:
                    dve.wait_ge(shdown_done, QT * b + q + 1)
                    xr = X[:, b * QT + q, :]
                    nc.vector.scalar_tensor_tensor(out=xr, in0=AUX[q % 2], scalar=TG[:, 2:3], in1=xr, op0=ALU.mult,
                                                   op1=ALU.add).then_inc(shacc, 1)

            dve.sem_inc(scan_done, PRE_SCAN)
            dve.sem_inc(h_ready, PRE_H)
            nc.vector.memset(YSB[:, :, :], 0.0).then_inc(zeroed, 1)
            for da in DAS:
                nc.vector.memset(da, 0.0).then_inc(zeroed, 1)
            dve.wait_ge(masks, 6)
            dve.wait_ge(ld_chan, 32)
            for pair in range(2):
                conv(0, pair)
            step_round(0)
            step_relu(0)
            step_sum(0)
            delta_u(0)
            dve.wait_ge(tg_ready, 2)
            for s in range(FIRST_B):
                f, p, g = s - 1, s + 1, s - 2
                dve.wait_ge(du_ready, s + 1)
                mul_b(s, 0, 0)
                for c in range(HPT):
                    if c == 3:
                        scan(s, 0, c)
                        if f >= 0:
                            dve.wait_ge(w_free, HS * s + PRE_W)
                            scan_gate(f, Y[:, yslot(f)], flat(PS[:, 0:4]))
                        if 0 <= g:
                            shared_add(g, (0, 1))
                        conv(p, 0)
                        mul_b(s, 0, c + 1)
                    else:
                        half(s, 0, c)
                    if c == 2 and g >= 0:
                        shared_hidden(g, 1)
                    if c == 4 and f >= 0:
                        scan_add(f, (0, 1), 0)
                    if c == 5 and f >= 0:
                        scan_add(f, (2, 3), 0)
                        dve.wait_ge(xacc, QT * (f + 1))
                        stats(f)
                    if c == 6:
                        conv(p, 1)
                if g >= 0:
                    shared_add(g, (2, 3))
                if s == NB:
                    break
                with dve.Fori(1, TURNS - 1) as i:
                    mul_b(s, i, 0)
                    for c in range(HPT):
                        half(s, i, c)
                if f >= 0:
                    norm_bias(2 * f + 1)
                mul_b(s, TURNS - 1, 0)
                for c in range(HPT):
                    half(s, TURNS - 1, c)
                    if c == 3:
                        dve.wait_ge(ld_x[s], 16)
                        if s:
                            dve.wait_ge(xn_ready, QT * s)
                        stats(s)
                    if s == 0:
                        if c == 4:
                            step_round(p)
                        if c == 5:
                            step_relu(p)
                        if c == 6:
                            step_sum(p)
                    if c == 5:
                        if f >= 0:
                            route(f)
                        norm_bias(2 * s)
                    if c == 6 and f >= 0:
                        shared_hidden(f, 0)
                delta_u(p)
            s, f, p = NB, NB - 1, NB + 1
            norm_bias(2 * f + 1)
            mul_b(s, 1, 0)
            for c in range(HPT):
                half(s, 1, c)
            route(f)
            slots()
            for turn in (2, 3):
                mul_b(s, turn, 0)
                for c in range(HPT):
                    half(s, turn, c)
                    if c:
                        mul_c(s, turn, c - 1)
                    if turn == 2 and c in (1, 5):
                        shared_hidden(f, c // 5)
                    if turn == 3:
                        if c == 1:
                            shared_add(f, (0, 1))
                            step_round(p)
                        if c == 3:
                            step_relu(p)
                        if c == 5:
                            step_sum(p)
                            shared_add(f, (2, 3))
                mul_c(s, turn, HPT - 1)
            delta_u(p)

            def tile_turn(s, i, prep):
                mul_b(s, i, 0)
                for u in range(BODY):
                    j = i * BODY + (TPS * (s - FIRST_B) + u)
                    for h in range(2):
                        c = 2 * u + h
                        if not isinstance(j, int) or j < NTILE:
                            tile_hidden(j, u, h)
                        if h and c >= 3:
                            add_y(s, i, c - 3)
                        half(s, i, c)
                        if h and c >= 2:
                            add_y(s, i, c - 2)
                        if prep == 1 and c % (HPT // 2) < DC - 1:
                            conv(s + 1, c // (HPT // 2), [c % (HPT // 2)])
                    if prep == 2 and u == 3:
                        delta_u(s + 1)
                add_y(s, i, HPT - 2)
                add_y(s, i, HPT - 1)

            for s in range(FIRST_B, STAGES):
                dve.wait_ge(du_ready, s + 1)
                dve.wait_ge(w_free, HS * s + PRE_W)
                prep = s + 1 < STAGES
                with dve.Fori(0, TURNS - 2 if prep else TURNS - 1) as i:
                    tile_turn(s, i, 0)
                if prep:
                    tile_turn(s, TURNS - 2, 1)
                tile_turn(s, TURNS - 1, 2 if prep else 0)

            def combine(b):
                steps_kq = [(k, q) for q in range(QT) for k in range(TOPK)] if b == 0 else [
                    (k, q) for k in range(TOPK) for q in range(QT)]
                for n, (k, q) in enumerate(steps_kq):
                    if k:
                        dve.wait_ge(combined, TOPK * QT * b + n - (QT if b else 1) + 1)
                    else:
                        dve.wait_ge(gathered[q], 16 * TOPK * (b + 1))
                    xr, g = X[:, b * QT + q, :], b * QT + q
                    nc.vector.scalar_tensor_tensor(out=xr, in0=GK[q][:, k, :], scalar=CWK[:, k, g:g + 1], in1=xr,
                                                   op0=ALU.mult, op1=ALU.add).then_inc(combined, 1)
                dve.wait_ge(combined, TOPK * QT * (b + 1))

            v8 = lambda i: SM[:, i, 0:QT * E1].rearrange("p (q e) -> p q e", e=E1)
            over_e = lambda v: v.unsqueeze(2).to_broadcast([P, QT, E1])

            def lora_logits(b):
                dve.wait_ge(mid_done, b + 1)
                for h in range(2):
                    ins = nc.vector.tensor_tensor(v8(0)[:, 2 * h:2 * h + 2, :], MIDL[h][:, :, E1 * RANK1:],
                                                  RB[:, :].unsqueeze(1).to_broadcast([P, 2, E1]), ALU.add)
                link(ins)
                m = SM[:, 2, 0:QT]
                link(nc.vector.reduce_max(m, v8(0), AX.X))
                nc.vector.tensor_tensor(v8(0), v8(0), over_e(m), ALU.subtract).then_inc(shift_ready, 1)

            def lora_gates(b):
                m = SM[:, 2, 0:QT]
                dve.wait_ge(exp_ready, b + 1)
                link(nc.vector.reduce_sum(m, v8(1), AX.X))
                link(nc.vector.reciprocal(m, m))
                link(nc.vector.tensor_tensor(v8(1), v8(1), over_e(m), ALU.mult))
                rank_of(v8(3), v8(1), E1, TRI[:, 0:E1, 0:E1], flat(SW[:, 1:2]), flat(SW[:, 2:3]))
                link(nc.vector.tensor_scalar(v8(3), v8(3), 2.0, None, ALU.is_lt))
                link(nc.vector.tensor_tensor(v8(3), v8(3), v8(1), ALU.mult))
                link(nc.vector.reduce_sum(m, v8(3), AX.X))
                link(nc.vector.reciprocal(m, m))
                link(nc.vector.tensor_scalar(m, m, LSCALE, None, ALU.mult))
                link(nc.vector.tensor_tensor(v8(3), v8(3), over_e(m), ALU.mult))
                if b:
                    dve.wait_ge(midt_done, b)
                by_expert = lambda v: v.rearrange("p q (e r) -> p q e r", r=RANK1)
                for h in range(2):
                    gates = v8(3)[:, 2 * h:2 * h + 2, :].unsqueeze(3).to_broadcast([P, 2, E1, RANK1])
                    ins = nc.vector.tensor_tensor(by_expert(MID[:, 2 * h:2 * h + 2, :]),
                                                  by_expert(MIDL[h][:, :, 0:E1 * RANK1]), gates, ALU.mult)
                ins.then_inc(midg_ready, 1)

            def lora_add(b):
                dve.wait_ge(bias_added, b + 1)
                for q in range(QT):
                    dve.wait_ge(ffn_done, QT * b + q + 1)
                    xr = X[:, b * QT + q, :]
                    nc.vector.scalar_tensor_tensor(out=xr, in0=PS[:, q], scalar=TG[:, 3:4], in1=xr, op0=ALU.mult,
                                                   op1=ALU.add).then_inc(x_final, 1)

            for b in range(NB + 1):
                f, l = NB + b, b - 1
                if b < NB:
                    combine(b)
                    dve.wait_ge(xn_ready, QT * f)
                    stats(b)
                if l >= 0:
                    lora_logits(l)
                if b < NB:
                    norm_bias(2 * f)
                if l >= 0:
                    lora_gates(l)
                if b < NB:
                    scan_gate(f, Y[:, b], flat(Y[:, b]))
                    scan_add(f, range(QT), 1)
                    dve.wait_ge(xacc, QT * (f + 1))
                    stats(b)
                    norm_bias(2 * f + 1)
                if l >= 0:
                    lora_add(l)


def _layouts(a):
    import numpy as np

    f = {k: np.asarray(v) for k, v in a.items()}
    c = np.ascontiguousarray
    out = {"x": c(f["x"]), "ctxT": c(f["ctx_1024"].reshape(NB * L, DM).T),
           "gates": c(np.concatenate([f["g_xattn"], f["g_ffn"]])[None, :])}
    order = list(range(DR, DR + 2 * NS)) + list(range(DR))
    for layer in range(2):
        g = lambda n: f[f"L{layer}_xattn_{n}"]
        out[f"in_wT{layer}"] = c(g("in_proj_w").T)
        out[f"chan{layer}"] = c(np.concatenate(
            [g("conv_w").reshape(D, DC), g("conv_b")[:, None], g("dt_proj_b")[:, None], g("D")[:, None], g("A_log")], axis=1))
        out[f"xprojT{layer}"] = c(g("x_proj_w")[order].T)
        out[f"dtT{layer}"] = c(g("dt_proj_w").T)

    def packed(gate, up, down):
        n = gate.shape[0]
        rows = [w.transpose(0, 2, 1).reshape(n, ET, P, INNER).transpose(0, 2, 1, 3).reshape(n, P, WGU) for w in (gate, up)]
        rows.append(down.transpose(0, 2, 1).reshape(n, IT, P, D).transpose(0, 2, 1, 3).reshape(n, P, IT * D))
        return np.concatenate(rows, axis=2)

    out["moe_w"] = c(np.concatenate([
        packed(f["L0_ffn_gate_proj"], f["L0_ffn_up_proj"], f["L0_ffn_down_proj"]),
        packed(f["L0_ffn_shared_gate"][None], f["L0_ffn_shared_up"][None], f["L0_ffn_shared_down"][None])]))
    out["gwT"] = c(f["L0_ffn_gate_weight"].T)
    out["ebias"] = c(f["L0_ffn_expert_bias"][None, :])
    out["base_wT"] = c(f["L1_ffn_base_w"].T)
    out["base_b"] = c(f["L1_ffn_base_b"][None, :])
    out["rb"] = c(f["L1_ffn_router_b"][None, :])
    out["loraA"] = c(np.concatenate(
        [f["L1_ffn_lora_A"].transpose(1, 0, 2).reshape(D, E1 * RANK1), f["L1_ffn_router_w"].T], axis=1))
    out["loraB"] = c(f["L1_ffn_lora_B"].reshape(E1 * RANK1, D))
    return out


def kernel(**inputs):
    import concourse.bacc as _bacc
    from concourse import mybir as _mybir
    from concourse.bass_utils import run_bass_kernel_spmd as _run

    nc = _bacc.Bacc("TRN2", target_bir_lowering=False, num_devices=1)
    arrays, t = {}, {}
    for name, a in _layouts(inputs).items():
        arrays[f"in_{name}"] = a
        t[name] = nc.dram_tensor(f"in_{name}", a.shape, _mybir.dt.from_np(a.dtype), kind="ExternalInput").ap()
    t["out"] = nc.dram_tensor("out_x", (NB, L, D), F32, kind="ExternalOutput").ap()
    build(nc, t)
    return _run(nc, [arrays], core_ids=[0]).results[0]["out_x"]
```
